# Optimizing a Trainium2 kernel written in Bass

```python
import numpy as np
import jax
import jax.numpy as jnp

def _softmax(x, axis=-1):
    return jax.nn.softmax(x, axis=axis)

def _gelu(x):
    return jax.nn.gelu(x, approximate=True)

def _silu(x):
    return jax.nn.silu(x)

def _sigmoid(x):
    return jax.nn.sigmoid(x)

def _layernorm(x, axis=-1, eps=1e-05):
    m = jnp.mean(x, axis=axis, keepdims=True)
    v = jnp.var(x, axis=axis, keepdims=True)
    return (x - m) / jnp.sqrt(v + eps)

def _scatter_add(tgt, idx, src, axis=0):
    return tgt.at[idx].add(src)

def _segment_sum(src, seg, n):
    return jax.ops.segment_sum(src, seg, n)
kernel_name = 'mk_decoder_postln_d2_seqx_r8_7b88fd'

def setup_inputs(seed: int=0):
    np.random.seed(seed)
    _w = jnp.asarray

    def _rec_inputs():
        import jax
        import jax.numpy as jnp
        _rk = jax.random.key(seed)
        x = 0.0002417 + 0.9998 * jax.random.normal(jax.random.fold_in(_rk, 1), (64, 128, 128), jnp.float32)
        _lenS = 128 - jax.random.randint(jax.random.fold_in(_rk, 7), (64,), 0, max(1, 128 // 4) + 1, jnp.int32)
        _lenS2 = 77 - jax.random.randint(jax.random.fold_in(_rk, 8), (64,), 0, max(1, 77 // 4) + 1, jnp.int32)
        _ctx_1024P = jax.random.normal(jax.random.fold_in(_rk, 11), (64, 16, 128), jnp.float32)
        _ctx_1024c = jax.random.dirichlet(jax.random.fold_in(_rk, 511), 0.3 * jnp.ones((16,), jnp.float32), (64, 77))
        _ctx_1024t = jnp.einsum('bsk,bkd->bsd', _ctx_1024c, _ctx_1024P)
        _ctx_1024t = _ctx_1024t * jax.lax.rsqrt(jnp.mean(jnp.square(_ctx_1024t)) + 1e-12) * 0.953939
        ctx_1024 = 7.22013e-05 + 1.00017 * (_ctx_1024t + 0.3 * jax.random.normal(jax.random.fold_in(_rk, 611), (64, 77, 128), jnp.float32))
        _validS = jnp.arange(128)[None, :] < _lenS[:, None]
        _validS2 = jnp.arange(77)[None, :] < _lenS2[:, None]
        _causal = jnp.tril(jnp.ones((128, 128), dtype=bool))
        mask_Bx1x1xS2_ik0 = jnp.where(jnp.broadcast_to(_validS2[:, None, None, :], (64, 1, 1, 77)), 0, 1).astype(jnp.int32)
        return (x, ctx_1024, mask_Bx1x1xS2_ik0)
    x, ctx_1024, mask_Bx1x1xS2_ik0 = _rec_inputs()

    def _L0_attn_setup():
        import jax, jax.numpy as jnp
        import numpy as np
        B, L, DM = (4, 256, 128)
        NL = 4
        DI = 2 * DM
        DS = 16
        DR = DM // 16
        DC = 4
        EPS = 1e-05

        def _layernorm(x, w, b):
            m = jnp.mean(x, -1, keepdims=True)
            xc = x - m
            v = jnp.mean(xc * xc, -1, keepdims=True)
            return xc * jax.lax.rsqrt(v + EPS) * w + b

        def _causal_conv(x, w, b):
            xt = jnp.transpose(x, (0, 2, 1))
            out = jax.lax.conv_general_dilated(xt, w[:, None, :], (1,), [(DC - 1, 0)], feature_group_count=DI)
            return jnp.transpose(out + b[None, :, None], (0, 2, 1))

        def _selective_scan(u, dt, Bm, Cm, A, D):

            def step(h, inp):
                ut, dtt, bt, ct = inp
                dA = jnp.exp(dtt[..., None] * A)
                h = dA * h + (dtt * ut)[..., None] * bt[:, None, :]
                y = jnp.einsum('bdn,bn->bd', h, ct)
                return (h, y)
            h0 = jnp.zeros((u.shape[0], A.shape[0], A.shape[1]), u.dtype)
            xs = (u.swapaxes(0, 1), dt.swapaxes(0, 1), Bm.swapaxes(0, 1), Cm.swapaxes(0, 1))
            _, ys = jax.lax.scan(step, h0, xs)
            return ys.swapaxes(0, 1) + u * D

        def _mamba(h, in_w, cw, cb, xp_w, dtp_w, dtp_b, A_log, D, out_w):
            xz = jnp.einsum('bld,ed->ble', h, in_w)
            xin, z = jnp.split(xz, 2, axis=-1)
            xc = jax.nn.silu(_causal_conv(xin, cw, cb))
            dbc = jnp.einsum('bld,ed->ble', xc, xp_w)
            dtr, Bm, Cm = (dbc[..., :DR], dbc[..., DR:DR + DS], dbc[..., DR + DS:])
            dt = jax.nn.softplus(jnp.einsum('blr,dr->bld', dtr, dtp_w) + dtp_b)
            A = -jnp.exp(A_log)
            y = _selective_scan(xc, dt, Bm, Cm, A, D)
            y = y * jax.nn.silu(z)
            return jnp.einsum('bld,ed->ble', y, out_w)

        def _forward(input_ids, norm_w, norm_b, in_proj_w, conv_w, conv_b, x_proj_w, dt_proj_w, dt_proj_b, A_log, D, out_proj_w, normf_w, normf_b):
            hidden = input_ids
            residual = None
            for i in range(NL):
                residual = hidden + residual if residual is not None else hidden
                hidden = _layernorm(residual, norm_w[i], norm_b[i])
                hidden = _mamba(hidden, in_proj_w[i], conv_w[i], conv_b[i], x_proj_w[i], dt_proj_w[i], dt_proj_b[i], A_log[i], D[i], out_proj_w[i])
            residual = hidden + residual
            return _layernorm(residual, normf_w, normf_b)
        key = jax.random.key(seed)
        ks = jax.random.split(key, 8)
        s = 0.02
        A = jnp.broadcast_to(jnp.arange(1, DS + 1, dtype=jnp.float32), (NL, DI, DS))
        return {'input_ids': jax.random.normal(ks[0], (B, L, DM), jnp.float32), 'norm_w': jnp.ones((NL, DM), jnp.float32), 'norm_b': jnp.zeros((NL, DM), jnp.float32), 'in_proj_w': jax.random.normal(ks[1], (NL, 2 * DI, DM), jnp.float32) * s, 'conv_w': jax.random.normal(ks[2], (NL, DI, DC), jnp.float32) * 0.5, 'conv_b': jnp.zeros((NL, DI), jnp.float32), 'x_proj_w': jax.random.normal(ks[3], (NL, DR + 2 * DS, DI), jnp.float32) * s, 'dt_proj_w': jax.random.normal(ks[4], (NL, DI, DR), jnp.float32) * DR ** (-0.5), 'dt_proj_b': jax.random.uniform(ks[5], (NL, DI), jnp.float32, -5.0, -3.0), 'A_log': jnp.log(A), 'D': jnp.ones((NL, DI), jnp.float32), 'out_proj_w': jax.random.normal(ks[6], (NL, DM, DI), jnp.float32) * s, 'normf_w': jnp.ones((DM,), jnp.float32), 'normf_b': jnp.zeros((DM,), jnp.float32)}
    _L0_attn_all = _L0_attn_setup()
    _L0_attn_in = {k: v for k, v in _L0_attn_all.items() if k in ('norm_w', 'norm_b', 'in_proj_w', 'conv_w', 'conv_b', 'x_proj_w', 'dt_proj_w', 'dt_proj_b', 'A_log', 'D', 'out_proj_w', 'normf_w', 'normf_b')}
    del _L0_attn_all

    def _L0_xattn_setup():
        import jax, jax.numpy as jnp
        import numpy as np
        import math
        D_MODEL = 128
        HEADS = 16
        D_K = D_MODEL // HEADS
        N, L = (4, 256)
        key0 = jax.random.key(seed)
        ks = jax.random.split(key0, 12)
        s = 1.0 / math.sqrt(D_MODEL)
        return {'value': jax.random.normal(ks[0], (N, L, D_MODEL), jnp.float32), 'key': jax.random.normal(ks[1], (N, L, D_MODEL), jnp.float32), 'query': jax.random.normal(ks[2], (N, L, D_MODEL), jnp.float32), 'mask': jax.random.randint(ks[3], (N, 1, 1, L), 0, 2, jnp.int32), 'wq': jax.random.normal(ks[4], (D_MODEL, D_MODEL), jnp.float32) * s, 'bq': jax.random.normal(ks[5], (D_MODEL,), jnp.float32) * s, 'wk': jax.random.normal(ks[6], (D_MODEL, D_MODEL), jnp.float32) * s, 'bk': jax.random.normal(ks[7], (D_MODEL,), jnp.float32) * s, 'wv': jax.random.normal(ks[8], (D_MODEL, D_MODEL), jnp.float32) * s, 'bv': jax.random.normal(ks[9], (D_MODEL,), jnp.float32) * s, 'wo': jax.random.normal(ks[10], (D_MODEL, D_MODEL), jnp.float32) * s, 'bo': jax.random.normal(ks[11], (D_MODEL,), jnp.float32) * s}
    _L0_xattn_all = _L0_xattn_setup()
    _L0_xattn_in = {k: v for k, v in _L0_xattn_all.items() if k in ('wq', 'bq', 'wk', 'bk', 'wv', 'bv', 'wo', 'bo')}
    del _L0_xattn_all

    def _L0_ffn_setup():
        import jax, jax.numpy as jnp
        import numpy as np
        from jax import lax
        B, N, DIM = (4, 256, 128)
        HEADS = 8
        NUM_EXPERTS = 2048
        NUM_KEYS = 128
        DIM_KEY = DIM // 2
        DIM_INNER = 2 * DIM
        PK_TOPK = 16
        TOPK = 1
        key = jax.random.key(seed)
        ks = jax.random.split(key, 10)
        s = lambda k, shape, std=0.02: jax.random.normal(k, shape, dtype=jnp.float32) * std
        return {'x': jax.random.normal(ks[0], (B, N, DIM), dtype=jnp.float32), 'Wq': s(ks[1], (DIM_KEY * HEADS * 2, DIM)), 'keys': s(ks[2], (HEADS, NUM_KEYS, 2, DIM_KEY)), 'W_in': s(ks[3], (DIM_INNER, DIM)), 'W_out': s(ks[4], (DIM, DIM_INNER)), 'in_a': s(ks[5], (NUM_EXPERTS, DIM)), 'in_b': s(ks[6], (NUM_EXPERTS, DIM_INNER)), 'out_a': s(ks[7], (NUM_EXPERTS, DIM_INNER)), 'out_b': s(ks[8], (NUM_EXPERTS, DIM))}
    _L0_ffn_all = _L0_ffn_setup()
    _L0_ffn_in = {k: v for k, v in _L0_ffn_all.items() if k in ('Wq', 'keys', 'W_in', 'W_out', 'in_a', 'in_b', 'out_a', 'out_b')}
    del _L0_ffn_all

    def _L1_attn_setup():
        import jax, jax.numpy as jnp
        import numpy as np
        MAX_DIST = 8
        GUIDANCE_WEIGHT = 0.4
        EPS_MAG = 1e-06
        EPS_COS = 1e-08
        EPS_WSUM = 1e-08
        key = jax.random.key(seed)
        k1, k2 = jax.random.split(key)
        embeddings = jax.random.normal(k1, (4, 256, 128), dtype=jnp.float32)
        guidance_trajectories = jax.random.normal(k2, (64, 128), dtype=jnp.float32)
        return {'embeddings': embeddings, 'guidance_trajectories': guidance_trajectories}
    _L1_attn_all = _L1_attn_setup()
    _L1_attn_in = {k: v for k, v in _L1_attn_all.items() if k in ('guidance_trajectories',)}
    del _L1_attn_all

    def _L1_xattn_setup():
        import jax, jax.numpy as jnp
        import numpy as np
        import math
        NHEAD = 16
        EPS = 1e-05

        def _layernorm(x, g, b):
            m = jnp.mean(x, axis=-1, keepdims=True)
            v = jnp.var(x, axis=-1, keepdims=True)
            return (x - m) / jnp.sqrt(v + EPS) * g + b

        def _split_heads(t, H):
            B, L, D = t.shape
            return t.reshape(B, L, H, D // H).transpose(0, 2, 1, 3)

        def _merge_heads(t):
            B, H, L, hd = t.shape
            return t.transpose(0, 2, 1, 3).reshape(B, L, H * hd)

        def _prob_sparse_self_attn(x, out_w, out_b):
            B, L, D = x.shape
            H = NHEAD
            q = _split_heads(x, H)
            k = q
            v = q
            scores = jnp.einsum('bhqd,bhkd->bhqk', q, k) * (1.0 / math.sqrt(D))
            u = max(1, int(math.ceil(math.log(L + 1))))
            _, idx = jax.lax.top_k(scores, u)
            bi = jnp.arange(B)[:, None, None, None]
            hi = jnp.arange(H)[None, :, None, None]
            li = jnp.arange(L)[None, None, :, None]
            mask = jnp.zeros(scores.shape, bool).at[bi, hi, li, idx].set(True)
            scores = jnp.where(mask, scores, -jnp.inf)
            attn = jax.nn.softmax(scores, axis=-1)
            out = _merge_heads(jnp.einsum('bhqk,bhkd->bhqd', attn, v))
            return out @ out_w.T + out_b

        def _mha_cross(x, mem, in_w, in_b, out_w, out_b):
            B, L, D = x.shape
            H = NHEAD
            hd = D // H
            wq, wk, wv = (in_w[:D], in_w[D:2 * D], in_w[2 * D:])
            bq, bk, bv = (in_b[:D], in_b[D:2 * D], in_b[2 * D:])
            q = _split_heads(x @ wq.T + bq, H)
            k = _split_heads(mem @ wk.T + bk, H)
            v = _split_heads(mem @ wv.T + bv, H)
            scores = jnp.einsum('bhqd,bhkd->bhqk', q, k) * (1.0 / math.sqrt(hd))
            attn = jax.nn.softmax(scores, axis=-1)
            out = _merge_heads(jnp.einsum('bhqk,bhkd->bhqd', attn, v))
            return out @ out_w.T + out_b
        key = jax.random.key(seed)
        ks = jax.random.split(key, 16)
        B, L, S, D, F = (2, 256, 256, 128, 512)
        s = 0.02
        inp = {'x': jax.random.normal(ks[0], (B, L, D), jnp.float32), 'memory': jax.random.normal(ks[1], (B, S, D), jnp.float32), 'self_out_w': jax.random.normal(ks[2], (D, D), jnp.float32) * s, 'self_out_b': jnp.zeros((D,), jnp.float32), 'cross_in_w': jax.random.normal(ks[3], (3 * D, D), jnp.float32) * s, 'cross_in_b': jnp.zeros((3 * D,), jnp.float32), 'cross_out_w': jax.random.normal(ks[4], (D, D), jnp.float32) * s, 'cross_out_b': jnp.zeros((D,), jnp.float32), 'ln1_g': jnp.ones((D,), jnp.float32), 'ln1_b': jnp.zeros((D,), jnp.float32), 'ln2_g': jnp.ones((D,), jnp.float32), 'ln2_b': jnp.zeros((D,), jnp.float32), 'ln3_g': jnp.ones((D,), jnp.float32), 'ln3_b': jnp.zeros((D,), jnp.float32), 'ffn_w1': jax.random.normal(ks[5], (F, D), jnp.float32) * s, 'ffn_b1': jnp.zeros((F,), jnp.float32), 'ffn_w2': jax.random.normal(ks[6], (D, F), jnp.float32) * s, 'ffn_b2': jnp.zeros((D,), jnp.float32)}
        return inp
    _L1_xattn_all = _L1_xattn_setup()
    _L1_xattn_in = {k: v for k, v in _L1_xattn_all.items() if k in ('self_out_w', 'self_out_b', 'cross_in_w', 'cross_in_b', 'cross_out_w', 'cross_out_b', 'ln1_g', 'ln1_b', 'ln2_g', 'ln2_b', 'ln3_g', 'ln3_b', 'ffn_w1', 'ffn_b1', 'ffn_w2', 'ffn_b2')}
    del _L1_xattn_all

    def _L1_ffn_setup():
        import jax, jax.numpy as jnp
        import numpy as np
        HIDDEN = 128
        INNER = 512

        def _weight_quant(w):
            scale = 1.0 / jnp.clip(jnp.mean(jnp.abs(w)), 1e-05)
            wq = jnp.clip(jnp.round(w * scale), -1.0, 1.0) / scale
            return w + jax.lax.stop_gradient(wq - w)

        def _act_quant(x):
            scale = 127.0 / jnp.clip(jnp.max(jnp.abs(x), axis=-1, keepdims=True), 1e-05)
            xq = jnp.clip(jnp.round(x * scale), -128.0, 127.0) / scale
            return x + jax.lax.stop_gradient(xq - x)

        def _bitlinear(x, w):
            return jnp.einsum('bsi,oi->bso', _act_quant(x), _weight_quant(w))
        key = jax.random.key(seed)
        k0, k1, k2, k3 = jax.random.split(key, 4)
        x = jax.random.normal(k0, (4, 256, HIDDEN), dtype=jnp.float32)
        w_gate = jax.random.normal(k1, (INNER, HIDDEN), dtype=jnp.float32) / np.sqrt(HIDDEN)
        w_up = jax.random.normal(k2, (INNER, HIDDEN), dtype=jnp.float32) / np.sqrt(HIDDEN)
        w_down = jax.random.normal(k3, (HIDDEN, INNER), dtype=jnp.float32) / np.sqrt(INNER)
        return {'x': x, 'w_gate': w_gate, 'w_up': w_up, 'w_down': w_down}
    _L1_ffn_all = _L1_ffn_setup()
    _L1_ffn_in = {k: v for k, v in _L1_ffn_all.items() if k in ('w_gate', 'w_up', 'w_down')}
    del _L1_ffn_all
    return {'x': x, 'ctx_1024': ctx_1024, 'mask_Bx1x1xS2_ik0': mask_Bx1x1xS2_ik0, 'L0_attn_norm_w': _L0_attn_in['norm_w'], 'L0_attn_norm_b': _L0_attn_in['norm_b'], 'L0_attn_in_proj_w': _L0_attn_in['in_proj_w'], 'L0_attn_conv_w': _L0_attn_in['conv_w'], 'L0_attn_conv_b': _L0_attn_in['conv_b'], 'L0_attn_x_proj_w': _L0_attn_in['x_proj_w'], 'L0_attn_dt_proj_w': _L0_attn_in['dt_proj_w'], 'L0_attn_dt_proj_b': _L0_attn_in['dt_proj_b'], 'L0_attn_A_log': _L0_attn_in['A_log'], 'L0_attn_D': _L0_attn_in['D'], 'L0_attn_out_proj_w': _L0_attn_in['out_proj_w'], 'L0_attn_normf_w': _L0_attn_in['normf_w'], 'L0_attn_normf_b': _L0_attn_in['normf_b'], 'L0_xattn_wq': _L0_xattn_in['wq'], 'L0_xattn_bq': _L0_xattn_in['bq'], 'L0_xattn_wk': _L0_xattn_in['wk'], 'L0_xattn_bk': _L0_xattn_in['bk'], 'L0_xattn_wv': _L0_xattn_in['wv'], 'L0_xattn_bv': _L0_xattn_in['bv'], 'L0_xattn_wo': _L0_xattn_in['wo'], 'L0_xattn_bo': _L0_xattn_in['bo'], 'L0_ffn_Wq': _L0_ffn_in['Wq'], 'L0_ffn_keys': _L0_ffn_in['keys'], 'L0_ffn_W_in': _L0_ffn_in['W_in'], 'L0_ffn_W_out': _L0_ffn_in['W_out'], 'L0_ffn_in_a': _L0_ffn_in['in_a'], 'L0_ffn_in_b': _L0_ffn_in['in_b'], 'L0_ffn_out_a': _L0_ffn_in['out_a'], 'L0_ffn_out_b': _L0_ffn_in['out_b'], 'L1_attn_guidance_trajectories': _L1_attn_in['guidance_trajectories'], 'L1_xattn_self_out_w': _L1_xattn_in['self_out_w'], 'L1_xattn_self_out_b': _L1_xattn_in['self_out_b'], 'L1_xattn_cross_in_w': _L1_xattn_in['cross_in_w'], 'L1_xattn_cross_in_b': _L1_xattn_in['cross_in_b'], 'L1_xattn_cross_out_w': _L1_xattn_in['cross_out_w'], 'L1_xattn_cross_out_b': _L1_xattn_in['cross_out_b'], 'L1_xattn_ln1_g': _L1_xattn_in['ln1_g'], 'L1_xattn_ln1_b': _L1_xattn_in['ln1_b'], 'L1_xattn_ln2_g': _L1_xattn_in['ln2_g'], 'L1_xattn_ln2_b': _L1_xattn_in['ln2_b'], 'L1_xattn_ln3_g': _L1_xattn_in['ln3_g'], 'L1_xattn_ln3_b': _L1_xattn_in['ln3_b'], 'L1_xattn_ffn_w1': _L1_xattn_in['ffn_w1'], 'L1_xattn_ffn_b1': _L1_xattn_in['ffn_b1'], 'L1_xattn_ffn_w2': _L1_xattn_in['ffn_w2'], 'L1_xattn_ffn_b2': _L1_xattn_in['ffn_b2'], 'L1_ffn_w_gate': _L1_ffn_in['w_gate'], 'L1_ffn_w_up': _L1_ffn_in['w_up'], 'L1_ffn_w_down': _L1_ffn_in['w_down']}

def reference(x, ctx_1024, mask_Bx1x1xS2_ik0, L0_attn_norm_w, L0_attn_norm_b, L0_attn_in_proj_w, L0_attn_conv_w, L0_attn_conv_b, L0_attn_x_proj_w, L0_attn_dt_proj_w, L0_attn_dt_proj_b, L0_attn_A_log, L0_attn_D, L0_attn_out_proj_w, L0_attn_normf_w, L0_attn_normf_b, L0_xattn_wq, L0_xattn_bq, L0_xattn_wk, L0_xattn_bk, L0_xattn_wv, L0_xattn_bv, L0_xattn_wo, L0_xattn_bo, L0_ffn_Wq, L0_ffn_keys, L0_ffn_W_in, L0_ffn_W_out, L0_ffn_in_a, L0_ffn_in_b, L0_ffn_out_a, L0_ffn_out_b, L1_attn_guidance_trajectories, L1_xattn_self_out_w, L1_xattn_self_out_b, L1_xattn_cross_in_w, L1_xattn_cross_in_b, L1_xattn_cross_out_w, L1_xattn_cross_out_b, L1_xattn_ln1_g, L1_xattn_ln1_b, L1_xattn_ln2_g, L1_xattn_ln2_b, L1_xattn_ln3_g, L1_xattn_ln3_b, L1_xattn_ffn_w1, L1_xattn_ffn_b1, L1_xattn_ffn_w2, L1_xattn_ffn_b2, L1_ffn_w_gate, L1_ffn_w_up, L1_ffn_w_down):
    import jax
    import jax.numpy as jnp

    def _L0_attn_ref(input_ids, norm_w, norm_b, in_proj_w, conv_w, conv_b, x_proj_w, dt_proj_w, dt_proj_b, A_log, D, out_proj_w, normf_w, normf_b):
        import jax, jax.numpy as jnp
        import numpy as np
        B, L, DM = (4, 256, 128)
        NL = 4
        DI = 2 * DM
        DS = 16
        DR = DM // 16
        DC = 4
        EPS = 1e-05

        def _layernorm(x, w, b):
            m = jnp.mean(x, -1, keepdims=True)
            xc = x - m
            v = jnp.mean(xc * xc, -1, keepdims=True)
            return xc * jax.lax.rsqrt(v + EPS) * w + b

        def _causal_conv(x, w, b):
            xt = jnp.transpose(x, (0, 2, 1))
            out = jax.lax.conv_general_dilated(xt, w[:, None, :], (1,), [(DC - 1, 0)], feature_group_count=DI)
            return jnp.transpose(out + b[None, :, None], (0, 2, 1))

        def _selective_scan(u, dt, Bm, Cm, A, D):

            def step(h, inp):
                ut, dtt, bt, ct = inp
                dA = jnp.exp(dtt[..., None] * A)
                h = dA * h + (dtt * ut)[..., None] * bt[:, None, :]
                y = jnp.einsum('bdn,bn->bd', h, ct)
                return (h, y)
            h0 = jnp.zeros((u.shape[0], A.shape[0], A.shape[1]), u.dtype)
            xs = (u.swapaxes(0, 1), dt.swapaxes(0, 1), Bm.swapaxes(0, 1), Cm.swapaxes(0, 1))
            _, ys = jax.lax.scan(step, h0, xs)
            return ys.swapaxes(0, 1) + u * D

        def _mamba(h, in_w, cw, cb, xp_w, dtp_w, dtp_b, A_log, D, out_w):
            xz = jnp.einsum('bld,ed->ble', h, in_w)
            xin, z = jnp.split(xz, 2, axis=-1)
            xc = jax.nn.silu(_causal_conv(xin, cw, cb))
            dbc = jnp.einsum('bld,ed->ble', xc, xp_w)
            dtr, Bm, Cm = (dbc[..., :DR], dbc[..., DR:DR + DS], dbc[..., DR + DS:])
            dt = jax.nn.softplus(jnp.einsum('blr,dr->bld', dtr, dtp_w) + dtp_b)
            A = -jnp.exp(A_log)
            y = _selective_scan(xc, dt, Bm, Cm, A, D)
            y = y * jax.nn.silu(z)
            return jnp.einsum('bld,ed->ble', y, out_w)

        def _forward(input_ids, norm_w, norm_b, in_proj_w, conv_w, conv_b, x_proj_w, dt_proj_w, dt_proj_b, A_log, D, out_proj_w, normf_w, normf_b):
            hidden = input_ids
            residual = None
            for i in range(NL):
                residual = hidden + residual if residual is not None else hidden
                hidden = _layernorm(residual, norm_w[i], norm_b[i])
                hidden = _mamba(hidden, in_proj_w[i], conv_w[i], conv_b[i], x_proj_w[i], dt_proj_w[i], dt_proj_b[i], A_log[i], D[i], out_proj_w[i])
            residual = hidden + residual
            return _layernorm(residual, normf_w, normf_b)
        return _forward(input_ids, norm_w, norm_b, in_proj_w, conv_w, conv_b, x_proj_w, dt_proj_w, dt_proj_b, A_log, D, out_proj_w, normf_w, normf_b)

    def _L0_xattn_ref(value, key, query, mask, wq, bq, wk, bk, wv, bv, wo, bo):
        import jax, jax.numpy as jnp
        import numpy as np
        import math
        D_MODEL = 128
        HEADS = 16
        D_K = D_MODEL // HEADS
        N, L = (4, 256)
        n, qlen = (query.shape[0], query.shape[1])
        h, dk = (HEADS, D_K)
        v = (value @ wv.T + bv).reshape(n, -1, h, dk).transpose(0, 2, 1, 3)
        k = (key @ wk.T + bk).reshape(n, -1, h, dk).transpose(0, 2, 1, 3)
        q = (query @ wq.T + bq).reshape(n, qlen, h, dk).transpose(0, 2, 1, 3)
        scores = jnp.einsum('nhqd,nhkd->nhqk', q, k)
        scores = jnp.where(mask == 0, jnp.float32(-1000000000.0), scores)
        attn = jax.nn.softmax(scores / math.sqrt(dk), axis=-1)
        out = jnp.einsum('nhqk,nhkd->nhqd', attn, v)
        out = out.transpose(0, 2, 1, 3).reshape(n, qlen, h * dk)
        return out @ wo.T + bo

    def _L0_ffn_ref(x, Wq, keys, W_in, W_out, in_a, in_b, out_a, out_b):
        import jax, jax.numpy as jnp
        import numpy as np
        from jax import lax
        B, N, DIM = (4, 256, 128)
        HEADS = 8
        NUM_EXPERTS = 2048
        NUM_KEYS = 128
        DIM_KEY = DIM // 2
        DIM_INNER = 2 * DIM
        PK_TOPK = 16
        TOPK = 1
        b, n, d = x.shape
        q = (x @ Wq.T).reshape(b, n, 2, HEADS, DIM_KEY).transpose(2, 0, 1, 3, 4)
        sim = jnp.einsum('pbnhd,hkpd->pbnhk', q, keys)
        sx, ix = lax.top_k(sim[0], PK_TOPK)
        sy, iy = lax.top_k(sim[1], PK_TOPK)
        all_scores = (sx[..., :, None] + sy[..., None, :]).reshape(b, n, HEADS, PK_TOPK * PK_TOPK)
        all_indices = (ix[..., :, None] * NUM_KEYS + iy[..., None, :]).reshape(b, n, HEADS, PK_TOPK * PK_TOPK)
        scores, pk = lax.top_k(all_scores, TOPK)
        indices = jnp.take_along_axis(all_indices, pk, axis=-1)
        A_in = in_a[indices]
        B_in = in_b[indices]
        A_out = out_a[indices]
        B_out = out_b[indices]
        gate = jax.nn.relu(scores)
        hidden = x @ W_in.T
        lin = jnp.einsum('bnd,bnhkd->bnhk', x, A_in) * gate
        hidden = hidden + jnp.einsum('bnhk,bnhkd->bnd', lin, B_in)
        hidden = jax.nn.gelu(hidden, approximate=False)
        out = hidden @ W_out.T
        lout = jnp.einsum('bnd,bnhkd->bnhk', hidden, A_out) * gate
        out = out + jnp.einsum('bnhk,bnhkd->bnd', lout, B_out)
        return out

    def _L1_attn_ref(embeddings, guidance_trajectories):
        import jax, jax.numpy as jnp
        import numpy as np
        MAX_DIST = 8
        GUIDANCE_WEIGHT = 0.4
        EPS_MAG = 1e-06
        EPS_COS = 1e-08
        EPS_WSUM = 1e-08
        B, S, D = embeddings.shape
        W = min(MAX_DIST, S - 1)
        diffs = embeddings[:, 1:, :] - embeddings[:, :-1, :]
        pos = jnp.arange(S)[:, None]
        k = jnp.arange(W)[None, :]
        idx = pos - W + k
        valid = (idx >= 0) & (pos >= 1)
        windows = diffs[:, jnp.clip(idx, 0, S - 2), :]
        w = jnp.minimum(pos, W)
        j = k - (W - w)
        lin = jnp.where(w > 1, 0.1 + 0.9 * j / jnp.maximum(w - 1, 1), 0.1)
        pos_weights = jnp.where(valid, lin, 0.0).astype(embeddings.dtype)
        mag = jnp.linalg.norm(windows, axis=-1, keepdims=True)
        is_valid_mag = mag > EPS_MAG
        normed = jnp.where(is_valid_mag, windows / jnp.where(is_valid_mag, mag, 1.0), 0.0)
        mag_weights = jnp.tanh(mag * 2.0)
        combined = pos_weights[None, :, :, None] * mag_weights
        g_norm = jnp.linalg.norm(guidance_trajectories, axis=-1)
        a_norm = jnp.linalg.norm(normed, axis=-1)
        dots = jnp.einsum('bswd,gd->bswg', normed, guidance_trajectories)
        sims = dots / (jnp.maximum(a_norm, EPS_COS)[..., None] * jnp.maximum(g_norm, EPS_COS))
        g_weights = jax.nn.softmax(sims * 2.0, axis=-1)
        influence = jnp.einsum('bswg,gd->bswd', g_weights, guidance_trajectories)
        blended = (1.0 - GUIDANCE_WEIGHT) * normed + GUIDANCE_WEIGHT * influence
        weight_sum = jnp.maximum(combined.sum(axis=2), EPS_WSUM)
        trajectories = (blended * combined).sum(axis=2) / weight_sum
        return trajectories

    def _L1_xattn_ref(x, memory, self_out_w, self_out_b, cross_in_w, cross_in_b, cross_out_w, cross_out_b, ln1_g, ln1_b, ln2_g, ln2_b, ln3_g, ln3_b, ffn_w1, ffn_b1, ffn_w2, ffn_b2):
        import jax, jax.numpy as jnp
        import numpy as np
        import math
        NHEAD = 16
        EPS = 1e-05

        def _layernorm(x, g, b):
            m = jnp.mean(x, axis=-1, keepdims=True)
            v = jnp.var(x, axis=-1, keepdims=True)
            return (x - m) / jnp.sqrt(v + EPS) * g + b

        def _split_heads(t, H):
            B, L, D = t.shape
            return t.reshape(B, L, H, D // H).transpose(0, 2, 1, 3)

        def _merge_heads(t):
            B, H, L, hd = t.shape
            return t.transpose(0, 2, 1, 3).reshape(B, L, H * hd)

        def _prob_sparse_self_attn(x, out_w, out_b):
            B, L, D = x.shape
            H = NHEAD
            q = _split_heads(x, H)
            k = q
            v = q
            scores = jnp.einsum('bhqd,bhkd->bhqk', q, k) * (1.0 / math.sqrt(D))
            u = max(1, int(math.ceil(math.log(L + 1))))
            _, idx = jax.lax.top_k(scores, u)
            bi = jnp.arange(B)[:, None, None, None]
            hi = jnp.arange(H)[None, :, None, None]
            li = jnp.arange(L)[None, None, :, None]
            mask = jnp.zeros(scores.shape, bool).at[bi, hi, li, idx].set(True)
            scores = jnp.where(mask, scores, -jnp.inf)
            attn = jax.nn.softmax(scores, axis=-1)
            out = _merge_heads(jnp.einsum('bhqk,bhkd->bhqd', attn, v))
            return out @ out_w.T + out_b

        def _mha_cross(x, mem, in_w, in_b, out_w, out_b):
            B, L, D = x.shape
            H = NHEAD
            hd = D // H
            wq, wk, wv = (in_w[:D], in_w[D:2 * D], in_w[2 * D:])
            bq, bk, bv = (in_b[:D], in_b[D:2 * D], in_b[2 * D:])
            q = _split_heads(x @ wq.T + bq, H)
            k = _split_heads(mem @ wk.T + bk, H)
            v = _split_heads(mem @ wv.T + bv, H)
            scores = jnp.einsum('bhqd,bhkd->bhqk', q, k) * (1.0 / math.sqrt(hd))
            attn = jax.nn.softmax(scores, axis=-1)
            out = _merge_heads(jnp.einsum('bhqk,bhkd->bhqd', attn, v))
            return out @ out_w.T + out_b
        x_self = _prob_sparse_self_attn(x, self_out_w, self_out_b)
        x = _layernorm(x + x_self, ln1_g, ln1_b)
        x_cross = _mha_cross(x, memory, cross_in_w, cross_in_b, cross_out_w, cross_out_b)
        x = _layernorm(x + x_cross, ln2_g, ln2_b)
        h = jax.nn.gelu(x @ ffn_w1.T + ffn_b1, approximate=False)
        x_ffn = h @ ffn_w2.T + ffn_b2
        x = _layernorm(x + x_ffn, ln3_g, ln3_b)
        return x

    def _L1_ffn_ref(x, w_gate, w_up, w_down):
        import jax, jax.numpy as jnp
        import numpy as np
        HIDDEN = 128
        INNER = 512

        def _weight_quant(w):
            scale = 1.0 / jnp.clip(jnp.mean(jnp.abs(w)), 1e-05)
            wq = jnp.clip(jnp.round(w * scale), -1.0, 1.0) / scale
            return w + jax.lax.stop_gradient(wq - w)

        def _act_quant(x):
            scale = 127.0 / jnp.clip(jnp.max(jnp.abs(x), axis=-1, keepdims=True), 1e-05)
            xq = jnp.clip(jnp.round(x * scale), -128.0, 127.0) / scale
            return x + jax.lax.stop_gradient(xq - x)

        def _bitlinear(x, w):
            return jnp.einsum('bsi,oi->bso', _act_quant(x), _weight_quant(w))
        gate = jax.nn.silu(_bitlinear(x, w_gate))
        up = _bitlinear(x, w_up)
        return _bitlinear(gate * up, w_down)
    x = _layernorm(x + _L0_attn_ref(x, L0_attn_norm_w, L0_attn_norm_b, L0_attn_in_proj_w, L0_attn_conv_w, L0_attn_conv_b, L0_attn_x_proj_w, L0_attn_dt_proj_w, L0_attn_dt_proj_b, L0_attn_A_log, L0_attn_D, L0_attn_out_proj_w, L0_attn_normf_w, L0_attn_normf_b), axis=-1)
    x = _layernorm(x + _L0_xattn_ref(ctx_1024, ctx_1024, x, mask_Bx1x1xS2_ik0, L0_xattn_wq, L0_xattn_bq, L0_xattn_wk, L0_xattn_bk, L0_xattn_wv, L0_xattn_bv, L0_xattn_wo, L0_xattn_bo), axis=-1)
    x = _layernorm(x + _L0_ffn_ref(x, L0_ffn_Wq, L0_ffn_keys, L0_ffn_W_in, L0_ffn_W_out, L0_ffn_in_a, L0_ffn_in_b, L0_ffn_out_a, L0_ffn_out_b), axis=-1)
    x = _layernorm(x + _L1_attn_ref(x, L1_attn_guidance_trajectories), axis=-1)
    x = _layernorm(x + _L1_xattn_ref(x, ctx_1024, L1_xattn_self_out_w, L1_xattn_self_out_b, L1_xattn_cross_in_w, L1_xattn_cross_in_b, L1_xattn_cross_out_w, L1_xattn_cross_out_b, L1_xattn_ln1_g, L1_xattn_ln1_b, L1_xattn_ln2_g, L1_xattn_ln2_b, L1_xattn_ln3_g, L1_xattn_ln3_b, L1_xattn_ffn_w1, L1_xattn_ffn_b1, L1_xattn_ffn_w2, L1_xattn_ffn_b2), axis=-1)
    x = _layernorm(x + _L1_ffn_ref(x, L1_ffn_w_gate, L1_ffn_w_up, L1_ffn_w_down), axis=-1)
    return x

_drawn_inputs = setup_inputs


def setup_inputs(seed=0):
    import zlib

    import numpy as np

    out = dict(_drawn_inputs(seed))
    spreads = {'L0_attn_norm_w': (1.0, 0.6),
     'L0_attn_norm_b': (0.0, 0.8),
     'L0_attn_conv_b': (0.0, 0.8),
     'L0_attn_D': (1.0, 0.6),
     'L0_attn_normf_w': (1.0, 0.2),
     'L0_attn_normf_b': (0.0, 0.1),
     'L1_xattn_self_out_b': (0.0, 0.1),
     'L1_xattn_cross_in_b': (0.0, 0.708),
     'L1_xattn_cross_out_b': (0.0, 0.1),
     'L1_xattn_ln1_g': (1.0, 0.2),
     'L1_xattn_ln1_b': (0.0, 0.1),
     'L1_xattn_ln2_g': (1.0, 0.2),
     'L1_xattn_ln2_b': (0.0, 0.1),
     'L1_xattn_ln3_g': (1.0, 0.2),
     'L1_xattn_ln3_b': (0.0, 0.1),
     'L1_xattn_ffn_b1': (0.0, 0.614),
     'L1_xattn_ffn_b2': (0.0, 0.1)}
    factors = {'L0_attn_in_proj_w': 8.0,
     'L0_attn_conv_w': 8.0,
     'L0_attn_x_proj_w': 8.0,
     'L0_attn_dt_proj_w': 8.0,
     'L0_attn_dt_proj_b': 8.0,
     'L0_attn_A_log': 8.0,
     'L0_attn_out_proj_w': 8.0,
     'L0_xattn_bk': 64.0,
     'L0_ffn_Wq': 8.0,
     'L0_ffn_keys': 8.0,
     'L0_ffn_in_a': 8.0,
     'L0_ffn_in_b': 8.0,
     'L0_ffn_out_a': 8.0,
     'L0_ffn_out_b': 8.0,
     'L1_xattn_cross_in_w': 4.33,
     'L1_xattn_cross_out_w': 3.257,
     'L0_ffn_W_out': 4.098}
    for name, (base, spread) in spreads.items():
        noise = np.random.default_rng([zlib.crc32(name.encode()), seed]).standard_normal(out[name].shape)
        drawn = base * np.exp(spread * noise) if base else spread * noise
        out[name] = jnp.asarray(drawn.astype(out[name].dtype))
    for name, factor in factors.items():
        out[name] = (out[name] * factor).astype(out[name].dtype)
    return out
```

```python
from contextlib import ExitStack

import numpy as np
import concourse.bass as bass
from concourse import mybir

F32 = mybir.dt.float32
BF16 = mybir.dt.bfloat16
I32 = mybir.dt.int32
U32 = mybir.dt.uint32
ALU = mybir.AluOpType
ACT = mybir.ActivationFunctionType
AX = mybir.AxisListType

P = 128
BATCH, SEQ, D = 64, 128, 128
GB = 4
TOK = GB * SEQ
GROUPS = BATCH // GB
LN_EPS = 1e-5

NL, DI, DS, DC = 4, 256, 16, 4
DR = D // 16
CH = DI // P
PADT = SEQ + 1
KW = SEQ + DC - 1


def tile_rows(ap, g):
    v = ap.rearrange("(g b t) d -> g t b d", b=GB, t=SEQ)
    return v[bass.ds(g, 1)].rearrange("g t b d -> (g t) b d")


class Sems:

    def __init__(self, nc, stack, names):
        self.nc = nc
        self.by = {n: stack.enter_context(nc.semaphore(n)) for n in names}
        self.runs = []
        for num in sorted(s.num for s in self.by.values()):
            if self.runs and self.runs[-1][1] == num:
                self.runs[-1][1] += 1
            else:
                self.runs.append([num, num + 1])

    def __getitem__(self, name):
        return self.by[name]

    def clear(self):
        for first, end in self.runs:
            self.nc.sync.sem_clear(range(first, end))
        self.nc.all_engine_barrier()


def mamba_stage(nc, w, consts, res):
    ident, selcol_dram = consts["ident"], w["selcol"]
    with ExitStack() as ctx:
        def sb(name, shape, dt=F32):
            return ctx.enter_context(nc.sbuf_tensor("mb_" + name, shape, dt))

        bank = ctx.enter_context(nc.psum_tensor("mb_bank", [P, 8, 512], F32))
        w_in = sb("w_in", [P, 2 * DI])
        conv_row = sb("conv_row", [P, DC, DI])
        w_conv = sb("w_conv", [P, DC, DI])
        w_x = sb("w_x", [P, CH, 2 * DS + DR])
        w_dt = sb("w_dt", [2 * DS + DR, DI])
        w_out = sb("w_out", [P, CH, D])
        vec = sb("vec", [P, 2 + 3 * CH + CH * DS])
        a_neg = sb("a_neg", [P, CH * DS])
        conv_bh = sb("conv_bh", [P, CH])
        selcol = sb("selcol", [96, 2 * DS])
        sel = sb("sel", [96, 2 * DS, P], BF16)
        half_neg = sb("half_neg", [P, GB])
        r_tok = sb("r_tok", [P, GB, D])
        stats = sb("stats", [P, GB, 6])
        mv = sb("mv", [P, GB, 2])
        rstd = sb("rstd", [P, GB])
        xh = sb("xh", [P, GB, D])
        h_ch = sb("h_ch", [P, GB, KW])
        v_sb = sb("v_sb", [P, CH, TOK])
        th = sb("th", [P, CH, TOK])
        u2 = sb("u2", [P, CH, TOK])
        z_sb = sb("z_sb", [P, CH, TOK])
        zg = sb("zg", [P, CH, TOK])
        bc_r = sb("bc_r", [2 * DS, TOK])
        bc_m = sb("bc_m", [2 * DS, TOK], BF16)
        bc_s = sb("bc_s", [96, TOK], BF16)
        dtr = sb("dtr", [2 * DS + DR, TOK])
        ab = sb("ab", [P, CH, TOK])
        ey = sb("ey", [P, CH, TOK])
        ln1 = sb("ln1", [P, CH, TOK])
        poly = sb("poly", [P, CH, TOK])
        small = sb("small", [P, CH, TOK], I32)
        relu = sb("relu", [P, CH, TOK])
        dt = sb("dt", [P, CH, TOK])
        dtu = sb("dtu", [P, CH, TOK])
        dA = [sb(f"dA{i}", [P, CH * GB, PADT]) for i in range(2)]
        dBu = [sb(f"dBu{i}", [P, CH * GB, PADT]) for i in range(2)]
        hs = [sb(f"hs{i}", [P, CH * GB, PADT]) for i in range(2)]
        b_sb = [sb(f"b_sb{i}", [P, TOK]) for i in range(2)]
        hc = [sb(f"hc{i}", [P, CH, TOK]) for i in range(2)]
        yg = sb("yg", [P, CH, TOK])

        NW, NB, CB, DB, DD, AL = 0, 1, 2, 2 + CH, 2 + 2 * CH, 2 + 3 * CH
        B_TR, B_X, B_Z, B_BC, B_C, B_Y = 0, 0, 2, 4, 5, 6

        def heads(ap):
            return ap.rearrange("p c (b t) -> p (c b) t", t=SEQ)

        s0 = Sems(nc, ctx, ["mbc_sel", "mbc_rdy"])
        with nc.Block() as block:
            @block.sync
            def _(sp):
                sp.dma_start(selcol[:], selcol_dram).then_inc(s0["mbc_sel"], 16)

            @block.vector
            def _(dve):
                nc.vector.memset(half_neg[:], -0.5)
                nc.vector.memset(h_ch[:], 0.0)
                for i in range(2):
                    nc.vector.memset(dA[i][:], 0.0)
                    nc.vector.memset(dBu[i][:], 0.0)
                dve.wait_ge(s0["mbc_sel"], 16)
                nc.vector.tensor_copy(sel[:], selcol[:].unsqueeze(2).to_broadcast([96, 2 * DS, P]))
        s0.clear()

        sw = Sems(nc, ctx, ["mbw_dma", "mbw_a", "mbw_v"])
        s = Sems(nc, ctx, ["mb_res", "mb_var", "mb_rstd", "mb_xh", "mb_tr", "mb_h", "mb_conv", "mb_z", "mb_th",
                      "mb_v", "mb_u", "mb_xp", "mb_split", "mb_r", "mb_dtr", "mb_dtp", "mb_abs", "mb_ey", "mb_ln1", "mb_relu",
                      "mb_zth", "mb_dt", "mb_dtu", "mb_bps", "mb_cps", "mb_bsb", "mb_dbu", "mb_da",
                      "mb_scan", "mb_hc", "mb_sum", "mb_yg", "mb_out", "mb_new", "mb_store", "mb_lo"])
        with nc.Fori(0, NL) as layer:
            with nc.Block() as block:
                @block.sync
                def _(sp):
                    def load(dst, src):
                        sp.dma_start(dst, src).then_inc(sw["mbw_dma"], 16)
                    load(w_in[:], w["w_in"][bass.ds(layer, 1)].rearrange("l p e -> (l p) e"))
                    load(conv_row[:].rearrange("p k e -> p (k e)"),
                         w["conv_row"][bass.ds(layer, 1)].rearrange("l k e -> l (k e)").to_broadcast([P, DC * DI]))
                    load(w_x[:], w["w_x"][bass.ds(layer, 1)].rearrange("l p c m -> (l p) c m"))
                    load(w_dt[2 * DS:2 * DS + DR, :], w["w_dt"][bass.ds(layer, 1)].rearrange("l r e -> (l r) e"))
                    load(w_out[:], w["w_out"][bass.ds(layer, 1)].rearrange("l p c e -> (l p) c e"))
                    load(vec[:], w["vec"][bass.ds(layer, 1)].rearrange("l p v -> (l p) v"))

                @block.scalar
                def _(act):
                    act.wait_ge(sw["mbw_dma"], 6 * 16)
                    nc.scalar.activation(a_neg[:], vec[:, AL:AL + CH * DS], ACT.Exp).then_inc(sw["mbw_a"], 1)

                @block.vector
                def _(dve):
                    dve.wait_ge(sw["mbw_dma"], 6 * 16)
                    for k in range(DC):
                        nc.vector.tensor_tensor(w_conv[:, k, :], w_in[:, 0:DI], conv_row[:, k, :], ALU.mult)
                    nc.vector.tensor_scalar(conv_bh[:], vec[:, CB:CB + CH], 0.5, None, ALU.mult)
                    nc.vector.tensor_scalar(w_x[:], w_x[:], 0.5, None, ALU.mult)
                    nc.vector.tensor_scalar(w_out[:], w_out[:], 0.25, None, ALU.mult)
                    dve.wait_ge(sw["mbw_a"], 1)
                    nc.vector.tensor_scalar(a_neg[:], a_neg[:], -1.0, None, ALU.mult)
            sw.clear()

            with nc.Fori(0, GROUPS) as g:
                with nc.Block() as block:
                    @block.sync
                    def _(sp):
                        sp.dma_start(r_tok[:], tile_rows(res, g)).then_inc(s["mb_res"], 16)
                        sp.wait_ge(s["mb_new"], 1)
                        sp.dma_start(tile_rows(res, g), r_tok[:]).then_inc(s["mb_store"], 16)
                        sp.wait_ge(s["mb_store"], 16)

                    @block.gpsimd
                    def _(pool):
                        pool.wait_ge(s["mb_var"], 1)
                        nc.gpsimd.tensor_tensor(rstd[:], mv[:, :, 1], half_neg[:], ALU.pow).then_inc(s["mb_rstd"], 1)
                        pool.wait_ge(s["mb_dtu"], 1)
                        for n in range(DS):
                            i = n % 2
                            pool.wait_ge(s["mb_bsb"], n + 1)
                            if n >= 2:
                                pool.wait_ge(s["mb_scan"], n - 1)
                            nc.gpsimd.tensor_tensor(
                                dBu[i][:, :, 1:].rearrange("p (c b) t -> p c b t", c=CH),
                                dtu[:].rearrange("p c (b t) -> p c b t", b=GB),
                                b_sb[i][:].rearrange("p (b t) -> p b t", b=GB).unsqueeze(1).to_broadcast([P, CH, GB, SEQ]),
                                ALU.mult).then_inc(s["mb_dbu"], 1)

                    @block.scalar
                    def _(act):
                        act.wait_ge(s["mb_tr"], 1)
                        nc.scalar.activation(h_ch[:, :, DC - 1:], bank[:, B_TR].rearrange("p (b t) -> p b t", b=GB),
                                             ACT.Identity, bias=vec[:, NB:NB + 1], scale=vec[:, NW:NW + 1]).then_inc(s["mb_h"], 1)
                        for c in range(CH):
                            act.wait_ge(s["mb_conv"], c + 1)
                            nc.scalar.activation(th[:, c], bank[:, B_X + c], ACT.Tanh, bias=conv_bh[:, c:c + 1],
                                                 scale=0.5).then_inc(s["mb_th"], 1)
                        act.wait_ge(s["mb_xp"], 1)
                        nc.scalar.activation(bc_s[0:32, :], bank[0:32, B_TR], ACT.Copy).then_inc(s["mb_split"], 1)
                        nc.scalar.activation(dtr[32:40, :], bank[32:40, B_TR], ACT.Copy).then_inc(s["mb_dtr"], 1)
                        act.wait_ge(s["mb_r"], 1)
                        nc.scalar.activation(bc_s[32:64, :], bc_r[:], ACT.Copy).then_inc(s["mb_split"], 1)
                        for c in range(CH):
                            act.wait_ge(s["mb_z"], c + 1)
                            nc.scalar.activation(z_sb[:, c], bank[:, B_Z + c], ACT.Copy).then_inc(s["mb_zth"], 1)
                            nc.scalar.activation(v_sb[:, c], bank[:, B_Z + c], ACT.Tanh, scale=0.5).then_inc(s["mb_zth"], 1)
                        for c in range(CH):
                            act.wait_ge(s["mb_dtp"], c + 1)
                            nc.scalar.activation(ab[:, c], bank[:, B_BC + c], ACT.Abs,
                                                 bias=vec[:, DB + c:DB + c + 1]).then_inc(s["mb_abs"], 1)
                        act.wait_ge(s["mb_abs"], CH)
                        nc.scalar.activation(ey[:], ab[:], ACT.Exp, scale=-1.0).then_inc(s["mb_ey"], 1)
                        act.wait_ge(s["mb_ey"], 1)
                        nc.scalar.activation(ln1[:], ey[:], ACT.Ln, bias=1.0).then_inc(s["mb_ln1"], 1)
                        act.wait_ge(s["mb_dt"], 1)
                        for n in range(DS):
                            i = n % 2
                            act.wait_ge(s["mb_bps"], n + 1)
                            if n >= 2:
                                act.wait_ge(s["mb_dbu"], n - 1)
                            nc.scalar.activation(b_sb[i][:], bank[:, B_BC], ACT.Copy).then_inc(s["mb_bsb"], 1)
                            if n >= 2:
                                act.wait_ge(s["mb_scan"], n - 1)
                            for c in range(CH):
                                k = c * DS + n
                                nc.scalar.activation(dA[i][:, c * GB:(c + 1) * GB, 1:],
                                                     dt[:, c].rearrange("p (b t) -> p b t", b=GB), ACT.Exp,
                                                     scale=a_neg[:, k:k + 1]).then_inc(s["mb_da"], 1)

                    @block.vector
                    def _(dve):
                        dve.wait_ge(s["mb_res"], 16)
                        for b in range(GB):
                            nc.vector.bn_stats(stats[:, b], r_tok[:, b])
                        dve.drain()
                        for b in range(GB):
                            nc.vector.bn_aggr(mv[:, b], stats[:, b])
                        dve.drain()
                        nc.vector.tensor_scalar(mv[:, :, 1], mv[:, :, 1], LN_EPS, None, ALU.add).then_inc(s["mb_var"], 1)
                        dve.wait_ge(s["mb_rstd"], 1)
                        for b in range(GB):
                            nc.vector.tensor_scalar(xh[:, b], r_tok[:, b], mv[:, b, 0:1], rstd[:, b:b + 1],
                                                    ALU.subtract, ALU.mult).then_inc(s["mb_xh"], 1)
                        for c in range(CH):
                            dve.wait_ge(s["mb_th"], c + 1)
                            nc.vector.tensor_scalar(ab[:, c], bank[:, B_X + c], vec[:, CB + c:CB + c + 1], None,
                                                    ALU.add).then_inc(s["mb_v"], 1)
                            dve.wait_ge(s["mb_v"], c + 1)
                            nc.vector.scalar_tensor_tensor(out=u2[:, c], in0=th[:, c], scalar=1.0, in1=ab[:, c],
                                                           op0=ALU.add, op1=ALU.mult).then_inc(s["mb_u"], 1)
                        dve.wait_ge(s["mb_split"], 1)
                        dve.wait_ge(s["mb_dtr"], 1)
                        nc.vector.tensor_tensor(bc_r[:], bank[0:32, B_TR], bc_s[0:32, :], ALU.subtract).then_inc(s["mb_r"], 1)
                        dve.wait_ge(s["mb_split"], 2)
                        dve.wait_ge(s["mb_r"], 1)
                        nc.vector.tensor_copy(bc_m[:], bc_s[32:64, :])
                        dve.drain()
                        nc.vector.tensor_tensor(bc_s[64:96, :], bc_r[:], bc_m[:],
                                                ALU.subtract).then_inc(s["mb_lo"], 1)
                        dve.wait_ge(s["mb_zth"], 2 * CH)
                        nc.vector.scalar_tensor_tensor(out=zg[:], in0=v_sb[:], scalar=1.0, in1=z_sb[:],
                                                       op0=ALU.add, op1=ALU.mult)
                        for c in range(CH):
                            dve.wait_ge(s["mb_abs"], c + 1)
                            nc.vector.tensor_scalar(relu[:, c], bank[:, B_BC + c], vec[:, DB + c:DB + c + 1], 0.0,
                                                    ALU.add, ALU.max).then_inc(s["mb_relu"], 1)
                        dve.wait_ge(s["mb_ey"], 1)
                        nc.vector.tensor_scalar(poly[:], ey[:], -0.25, 1.0 / 3, ALU.mult, ALU.add)
                        nc.vector.tensor_scalar(small[:], ey[:], 2.0 ** -6, None, ALU.is_lt)
                        dve.drain()
                        for k in (-0.5, 1.0):
                            nc.vector.tensor_tensor(poly[:], poly[:], ey[:], ALU.mult)
                            dve.drain()
                            nc.vector.tensor_scalar(poly[:], poly[:], k, None, ALU.add)
                            dve.drain()
                        nc.vector.tensor_tensor(poly[:], poly[:], ey[:], ALU.mult)
                        dve.drain()
                        dve.wait_ge(s["mb_ln1"], 1)
                        nc.vector.copy_predicated(ln1[:], small[:], poly[:])
                        dve.drain()
                        dve.wait_ge(s["mb_relu"], CH)
                        nc.vector.tensor_tensor(dt[:], ln1[:], relu[:], ALU.add).then_inc(s["mb_dt"], 1)
                        dve.wait_ge(s["mb_dt"], 1)
                        nc.vector.tensor_tensor(dtu[:], dt[:], u2[:], ALU.mult).then_inc(s["mb_dtu"], 1)
                        for n in range(DS):
                            i = n % 2
                            dve.wait_ge(s["mb_da"], CH * (n + 1))
                            dve.wait_ge(s["mb_dbu"], n + 1)
                            nc.vector.tensor_tensor_scan(hs[i][:].rearrange("p c t -> p (c t)"),
                                                         dA[i][:].rearrange("p c t -> p (c t)"),
                                                         dBu[i][:].rearrange("p c t -> p (c t)"),
                                                         0.0, ALU.mult, ALU.add).then_inc(s["mb_scan"], 1)
                            dve.wait_ge(s["mb_scan"], n + 1)
                            dve.wait_ge(s["mb_cps"], n + 1)
                            if n >= 2:
                                dve.wait_ge(s["mb_sum"], n - 1)
                            nc.vector.tensor_tensor(
                                hc[i][:].rearrange("p c (b t) -> p c b t", b=GB),
                                hs[i][:, :, 1:].rearrange("p (c b) t -> p c b t", c=CH),
                                bank[:, B_C].rearrange("p (b t) -> p b t", b=GB).unsqueeze(1).to_broadcast([P, CH, GB, SEQ]),
                                ALU.mult).then_inc(s["mb_hc"], 1)
                        dve.wait_ge(s["mb_sum"], DS)
                        for c in range(CH):
                            nc.vector.scalar_tensor_tensor(out=u2[:, c], in0=u2[:, c], scalar=vec[:, DD + c:DD + c + 1],
                                                           in1=bank[:, B_Y + c], op0=ALU.mult, op1=ALU.add)
                        dve.drain()
                        nc.vector.tensor_tensor(yg[:], u2[:], zg[:], ALU.mult).then_inc(s["mb_yg"], 1)
                        dve.wait_ge(s["mb_out"], 1)
                        nc.vector.tensor_tensor(r_tok[:], r_tok[:], bank[:, B_TR].rearrange("p (b d) -> p b d", b=GB),
                                                ALU.add).then_inc(s["mb_new"], 1)

                    @block.tensor
                    def _(pe):
                        for b in range(GB):
                            pe.wait_ge(s["mb_xh"], b + 1)
                            m = nc.tensor.transpose(bank[:, B_TR, b * SEQ:(b + 1) * SEQ], xh[:, b], ident[:])
                        m.then_inc(s["mb_tr"], 1)
                        pe.wait_ge(s["mb_h"], 1)
                        for c in range(CH):
                            for k in range(DC):
                                m = nc.tensor.matmul(bank[:, B_X + c], w_conv[:, k, c * P:(c + 1) * P],
                                                     h_ch[:, :, k:k + SEQ], start=(k == 0), stop=(k == DC - 1))
                            m.then_inc(s["mb_conv"], 1)
                        for c in range(CH):
                            nc.tensor.matmul(bank[:, B_Z + c], w_in[:, DI + c * P:DI + (c + 1) * P],
                                             h_ch[:, :, DC - 1:], start=True, stop=True).then_inc(s["mb_z"], 1)
                        pe.wait_ge(s["mb_th"], 2)
                        for c in range(CH):
                            pe.wait_ge(s["mb_u"], c + 1)
                            m = nc.tensor.matmul(bank[0:2 * DS + DR, B_TR], w_x[:, c], u2[:, c], start=(c == 0), stop=(c == CH - 1))
                        m.then_inc(s["mb_xp"], 1)
                        pe.wait_ge(s["mb_dtr"], 1)
                        for c in range(CH):
                            nc.tensor.matmul(bank[:, B_BC + c], w_dt[32:40, c * P:(c + 1) * P], dtr[32:40, :],
                                             start=True, stop=True).then_inc(s["mb_dtp"], 1)
                        pe.wait_ge(s["mb_abs"], CH)
                        pe.wait_ge(s["mb_relu"], CH)
                        pe.wait_ge(s["mb_lo"], 1)

                        def spread(n):
                            if n:
                                pe.wait_ge(s["mb_bsb"], n)
                            nc.tensor.matmul(bank[:, B_BC], sel[:, n], bc_s[:], start=True, stop=True).then_inc(s["mb_bps"], 1)
                            if n:
                                pe.wait_ge(s["mb_hc"], n)
                            nc.tensor.matmul(bank[:, B_C], sel[:, DS + n], bc_s[:], start=True, stop=True).then_inc(s["mb_cps"], 1)

                        spread(0)
                        for n in range(DS):
                            if n + 1 < DS:
                                spread(n + 1)
                            pe.wait_ge(s["mb_hc"], n + 1)
                            for c in range(CH):
                                m = nc.tensor.matmul(bank[:, B_Y + c], ident[:], hc[n % 2][:, c], start=(n == 0), stop=(n == DS - 1))
                            m.then_inc(s["mb_sum"], 1)
                        pe.wait_ge(s["mb_yg"], 1)
                        for b in range(GB):
                            for c in range(CH):
                                m = nc.tensor.matmul(bank[:, B_TR, b * D:(b + 1) * D], yg[:, c, b * SEQ:(b + 1) * SEQ],
                                                     w_out[:, c], start=(c == 0), stop=(c == CH - 1))
                        m.then_inc(s["mb_out"], 1)
                s.clear()


def mamba_host(i):
    A = lambda k: np.asarray(i["L0_attn_" + k])
    xp = A("x_proj_w")
    xp = np.concatenate([xp[:, DR:], xp[:, :DR]], axis=1)
    ch = lambda a: a.reshape(NL, CH, P).transpose(0, 2, 1)
    vec = np.concatenate([
        A("norm_w")[:, :, None], A("norm_b")[:, :, None], ch(A("conv_b")), ch(A("dt_proj_b")), ch(A("D")),
        A("A_log").reshape(NL, CH, P, DS).transpose(0, 2, 1, 3).reshape(NL, P, CH * DS)], axis=2)
    return {
        "w_in": A("in_proj_w").transpose(0, 2, 1),
        "conv_row": A("conv_w").transpose(0, 2, 1),
        "w_x": xp.reshape(NL, 2 * DS + DR, CH, P).transpose(0, 3, 2, 1),
        "w_dt": A("dt_proj_w").transpose(0, 2, 1),
        "w_out": A("out_proj_w").reshape(NL, D, CH, P).transpose(0, 3, 2, 1),
        "vec": vec,
        "selcol": np.tile(np.eye(2 * DS, dtype=np.float32), (3, 1)),
    }

H, DK = 16, 8
NC = 77
HH = H // 2
VW = DK + 1
TOPK = 5
PAD = 4
LOW, PICKED = -3.0e38, -2.0e38
BIG = -1.0e9


class Prefixed:

    def __init__(self, s, prefix):
        self.s, self.prefix, self.nc = s, prefix, s.nc

    def __getitem__(self, name):
        return self.s[self.prefix + name]


class Norm:

    def __init__(self, sb, s, pre, half_neg):
        self.s, self.var, self.rst, self.half_neg = s, pre + "_var", pre + "_rstd", half_neg
        self.stats = sb(pre + "_stats", [P, GB, 6])
        self.mv = sb(pre + "_mv", [P, GB, 2])
        self.rstd = sb(pre + "_rs", [P, GB])
        self.on_dve = self.on_pool = 0

    def dve(self, dve, src, dst):
        nc = self.s.nc
        for b in range(GB):
            nc.vector.bn_stats(self.stats[:, b], src[:, b])
        dve.drain()
        for b in range(GB):
            nc.vector.bn_aggr(self.mv[:, b], self.stats[:, b])
        dve.drain()
        nc.vector.tensor_scalar(self.mv[:, :, 1], self.mv[:, :, 1], LN_EPS, None, ALU.add).then_inc(self.s[self.var], 1)
        self.on_dve += 1
        dve.wait_ge(self.s[self.rst], self.on_dve)
        for b in range(GB):
            last = nc.vector.tensor_scalar(dst[:, b], src[:, b], self.mv[:, b, 0:1], self.rstd[:, b:b + 1],
                                           ALU.subtract, ALU.mult)
        return last

    def pool(self, pool):
        self.on_pool += 1
        pool.wait_ge(self.s[self.var], self.on_pool)
        self.s.nc.gpsimd.tensor_tensor(self.rstd[:], self.mv[:, :, 1], self.half_neg[:], ALU.pow).then_inc(self.s[self.rst], 1)


ATTN_SEMS = ["km", "vx", "score", "shift", "exp", "tr", "pta", "ptv", "pv", "o", "otp", "ot", "proj",
             "cp", "mx", "mr", "pick"]


class Attention:

    UNITS = 2 * GB

    def __init__(self, nc, sb, s, pre, bank, ident, hmask, nk, scale, topk=False, bias=None):
        self.nc, self.s, self.bank, self.ident, self.hmask = nc, s, bank, ident, hmask
        self.nk, self.scale, self.topk, self.bias, self.pre = nk, scale, topk, bias, pre
        self.km = [sb(f"{pre}_km{i}", [P, H, nk]) for i in range(2)]
        self.e = [sb(f"{pre}_e{i}", [P, HH, nk]) for i in range(2)]
        self.mx = sb(pre + "_mx", [P, 2, HH])
        self.pt = sb(pre + "_pt", [nk, HH, P])
        self.rs = sb(pre + "_rs", [P, H])
        self.o = sb(pre + "_o", [P, 2, D])
        self.ot = sb(pre + "_ot", [P, 2, D])
        if topk:
            self.sp = [sb(f"{pre}_sp{i}", [P, HH, nk + PAD]) for i in range(2)]
            self.mr = sb(pre + "_mr", [P, HH, nk + PAD])
            self.m8 = sb(pre + "_m8", [P, 2, HH, 8])
            self.nb = sb(pre + "_nb", [P, 2, HH])
            self.m5 = sb(pre + "_m5", [P, HH, 8])

    def sem(self, name):
        return self.s[self.pre + "_" + name]

    def scores_at(self, u, j):
        return self.bank[:, 2 * (u % 2) + j, 0:4 * self.nk].rearrange("p (h k) -> p h k", h=4)

    def scores_of(self, u):
        return self.bank[:, 2 * (u % 2):2 * (u % 2) + 2, 0:4 * self.nk].rearrange("p j (h k) -> p j h k", h=4)

    def pool(self, pool, kT):
        nk = self.nk
        for b in range(GB):
            if b >= 2:
                pool.wait_ge(self.sem("score"), 2 * (b - 1))
            self.nc.gpsimd.tensor_tensor(self.km[b % 2][:], kT(b).unsqueeze(1).to_broadcast([P, H, nk]),
                                         self.hmask[:].unsqueeze(2).to_broadcast([P, H, nk]), ALU.mult).then_inc(self.sem("km"), 1)

    def pe(self, pe, qT, vx, w_o):
        nc, nk = self.nc, self.nk

        def scores(u):
            b, hf = divmod(u, 2)
            pe.wait_ge(self.sem("km"), b + 1)
            if u >= 2:
                pe.wait_ge(self.sem("cp" if self.topk else "shift"), u - 1)
            for j in range(2):
                h0 = hf * HH + 4 * j
                m = nc.tensor.matmul(self.scores_at(u, j), qT(b), self.km[b % 2][:, h0:h0 + 4, :],
                                     start=True, stop=self.bias is None)
                if self.bias is not None:
                    ones3, parts = self.bias
                    m = nc.tensor.matmul(self.scores_at(u, j), ones3[:], parts(b).unsqueeze(1).to_broadcast([3, 4, nk]),
                                         start=False, stop=True)
            m.then_inc(self.sem("score"), 1)

        def project(b):
            pe.wait_ge(self.sem("o"), b + 1)
            nc.tensor.transpose(self.bank[:, 7, 0:P], self.o[:, b % 2], self.ident[:]).then_inc(self.sem("otp"), 1)
            pe.wait_ge(self.sem("ot"), b + 1)
            nc.tensor.matmul(self.bank[:, 7, P:2 * P], self.ot[:, b % 2], w_o[:], start=True, stop=True).then_inc(self.sem("proj"), 1)

        scores(0)
        scores(1)
        for u in range(self.UNITS):
            b, hf = divmod(u, 2)
            pe.wait_ge(self.sem("pick" if self.topk else "exp"), u + 1)
            if u:
                pe.wait_ge(self.sem("pta"), u)
                pe.wait_ge(self.sem("ptv"), u)
            for h in range(HH):
                m = nc.tensor.transpose(self.bank[0:nk, 4 + h // 4, (h % 4) * P:(h % 4 + 1) * P], self.e[u % 2][:, h], self.ident[:])
            m.then_inc(self.sem("tr"), 1)
            if u + 2 < self.UNITS:
                scores(u + 2)
            if hf == 0 and b >= 1:
                project(b - 1)
            pe.wait_ge(self.sem("pta"), u + 1)
            pe.wait_ge(self.sem("ptv"), u + 1)
            if hf == 0 and b >= 1:
                pe.wait_ge(self.sem("o"), b)
            for h in range(HH):
                at = (hf * HH + h) * VW
                m = nc.tensor.matmul(self.bank[:, 6, at:at + VW], self.pt[:, h], vx(b, hf * HH + h), start=True, stop=True)
            m.then_inc(self.sem("pv"), 1)
        project(GB - 1)

    def act(self, act):
        nc, nk = self.nc, self.nk

        def evac(u):
            act.wait_ge(self.sem("tr"), u + 1)
            if u:
                act.wait_ge(self.sem("pv"), u)
            nc.scalar.activation(self.pt[:, 0:4].rearrange("p h q -> p (h q)"), self.bank[0:nk, 4], ACT.Copy).then_inc(self.sem("pta"), 1)

        def turned(b):
            act.wait_ge(self.sem("otp"), b + 1)
            nc.scalar.activation(self.ot[:, b % 2], self.bank[:, 7, 0:P], ACT.Copy).then_inc(self.sem("ot"), 1)

        for u in range(self.UNITS):
            if self.topk:
                act.wait_ge(self.sem("score"), u + 1)
                if u >= 2:
                    act.wait_ge(self.sem("exp"), HH * (u - 1))
                    act.wait_ge(self.sem("mr"), u - 1)
                nc.scalar.activation(self.sp[u % 2][:, :, 0:nk].rearrange("p (j h) k -> p j h k", j=2), self.scores_of(u),
                                     ACT.Copy).then_inc(self.sem("cp"), 1)
                act.wait_ge(self.sem("mx"), u + 1)
                act.wait_ge(self.sem("cp"), u + 1)
                if u >= 2:
                    act.wait_ge(self.sem("tr"), u - 1)
                for h in range(HH):
                    nc.scalar.activation(self.e[u % 2][:, h], self.sp[u % 2][:, h, 0:nk], ACT.Exp, scale=self.scale,
                                         bias=self.nb[:, u % 2, h:h + 1]).then_inc(self.sem("exp"), 1)
            else:
                act.wait_ge(self.sem("shift"), u + 1)
                nc.scalar.activation(self.e[u % 2][:], self.e[u % 2][:], ACT.Exp, scale=self.scale).then_inc(self.sem("exp"), 1)
            if u:
                evac(u - 1)
            if u % 2 == 1 and u > 1:
                turned(u // 2 - 1)
        evac(self.UNITS - 1)
        turned(GB - 1)

    def dve(self, dve, after):
        nc, nk = self.nc, self.nk

        def evac(u):
            dve.wait_ge(self.sem("tr"), u + 1)
            if u:
                dve.wait_ge(self.sem("pv"), u)
            nc.vector.tensor_copy(self.pt[:, 4:8].rearrange("p h q -> p (h q)"), self.bank[0:nk, 5]).then_inc(self.sem("ptv"), 1)

        def normalise(b):
            heads = self.bank[:, 6, 0:H * VW].rearrange("p (h v) -> p h v", v=VW)
            dve.wait_ge(self.sem("pv"), 2 * b + 2)
            nc.vector.reciprocal(self.rs[:], heads[:, :, DK])
            if b >= 2:
                dve.wait_ge(self.sem("otp"), b - 1)
            dve.drain()
            nc.vector.tensor_tensor(self.o[:, b % 2].rearrange("p (h v) -> p h v", v=DK), heads[:, :, 0:DK],
                                    self.rs[:].unsqueeze(2).to_broadcast([P, H, DK]), ALU.mult).then_inc(self.sem("o"), 1)

        def finish(b):
            dve.wait_ge(self.sem("proj"), b + 1)
            after(b, self.bank[:, 7, P:2 * P])

        for u in range(self.UNITS):
            i = u % 2
            if self.topk:
                dve.wait_ge(self.sem("cp"), u + 1)
                for h in range(HH):
                    nc.vector.max(self.m8[:, i, h], self.sp[i][:, h, 0:nk])
                dve.drain()
                if u >= 2:
                    dve.wait_ge(self.sem("exp"), HH * (u - 1))
                nc.vector.tensor_scalar(self.nb[:, i], self.m8[:, i, :, 0], -self.scale, None, ALU.mult).then_inc(self.sem("mx"), 1)
                nc.vector.memset(self.m8[:, i, :, TOPK:], LOW)
                dve.drain()
                for h in range(HH):
                    m = nc.vector.match_replace(self.mr[:, h], self.m8[:, i, h], self.sp[i][:, h], PICKED)
                m.then_inc(self.sem("mr"), 1)
                dve.wait_ge(self.sem("mr"), u + 1)
                dve.wait_ge(self.sem("exp"), HH * (u + 1))
                nc.vector.scalar_tensor_tensor(out=self.e[i][:], in0=self.mr[:, :, 0:nk], scalar=PICKED, in1=self.e[i][:],
                                               op0=ALU.is_equal, op1=ALU.mult).then_inc(self.sem("pick"), 1)
            else:
                dve.wait_ge(self.sem("score"), u + 1)
                nc.vector.tensor_reduce(self.mx[:, i].rearrange("p (j h) -> p j h", j=2), self.scores_of(u), AX.X, ALU.max)
                if u >= 2:
                    dve.wait_ge(self.sem("tr"), u - 1)
                dve.drain()
                nc.vector.tensor_tensor(self.e[i][:].rearrange("p (j h) k -> p j h k", j=2), self.scores_of(u),
                                        self.mx[:, i].rearrange("p (j h) -> p j h", j=2).unsqueeze(3).to_broadcast([P, 2, 4, nk]),
                                        ALU.subtract).then_inc(self.sem("shift"), 1)
            if u:
                evac(u - 1)
            if u % 2 == 0 and u:
                normalise(u // 2 - 1)
            if u % 2 == 1 and u > 1:
                finish(u // 2 - 1)
        evac(self.UNITS - 1)
        normalise(GB - 1)
        finish(GB - 1)


def row(ap, parts):
    return ap.unsqueeze(0).to_broadcast([parts, ap.shape[0]])


def ctx_rows(ap, g):
    v = ap.rearrange("(g b) t d -> g t b d", b=GB)
    return v[bass.ds(g, 1)].rearrange("g t b d -> (g t) b d")


def xattn_stage(nc, w, consts, x_in, res, ctx_in, mask_in, x_out):
    ident, hmask, half_neg = consts["ident"], consts["hmask"], consts["half_neg"]
    with ExitStack() as st:
        def sb(name, shape, dt=F32):
            return st.enter_context(nc.sbuf_tensor("xa_" + name, shape, dt))

        bank = st.enter_context(nc.psum_tensor("xa_bank", [P, 8, 512], F32))
        s = Sems(nc, st, ["xa_" + n for n in ["n_var", "n_rstd", "in", "ctx", "xt", "xts", "ct", "cts", "q", "qs", "k", "ks", "kb",
                                          "mk", "v", "vb", "out", "store"] + ["a_" + n for n in ATTN_SEMS]])

        p = Prefixed(s, "xa_")
        wq, wk, wv, wo = (sb(n, [P, D]) for n in ("wq", "wk", "wv", "wo"))
        vecs = sb("vecs", [P, 2])
        rows = sb("rows", [P, 4, D])
        part = sb("part", [3, 1])
        ones3 = sb("ones3", [3, P], BF16)
        r_tok, x_tok, y_tok, z_tok = (sb(n, [P, GB, D]) for n in ("r_tok", "x_tok", "y_tok", "z_tok"))
        c_tok = sb("c_tok", [NC, GB, D])
        xT, qT = sb("xT", [P, GB, SEQ]), sb("qT", [P, GB, SEQ])
        cT, kT = sb("cT", [P, GB, NC]), sb("kT", [P, GB, NC])
        m_int = sb("m_int", [P, GB, NC], I32)
        keep = sb("keep", [P, GB, NC])
        mbias = sb("mbias", [3, GB, NC], BF16)
        vx = sb("vx", [NC, GB, H, VW])
        norm = Norm(sb, p, "n", half_neg)
        at = Attention(nc, sb, p, "a", bank, ident, hmask, NC, DK ** -0.5, bias=(ones3, lambda b: mbias[:, b]))

        s0 = Sems(nc, st, ["xa0_w"])
        with nc.Block() as block:
            @block.sync
            def _(sp):
                loads = [(wq, w["wq"]), (wk, w["wk"]), (wv, w["wv"]), (wo, w["wo"]), (vecs, w["vecs"]), (part, w["part"])]
                for t, d in loads:
                    sp.dma_start(t[:], d).then_inc(s0["xa0_w"], 16)
                sp.dma_start(rows[:].rearrange("p r d -> p (r d)"), w["rows"].rearrange("r d -> (r d)").unsqueeze(0)
                             .to_broadcast([P, 4 * D])).then_inc(s0["xa0_w"], 16)
                sp.wait_ge(s0["xa0_w"], 16 * (len(loads) + 1))

            @block.vector
            def _(dve):
                nc.vector.memset(ones3[:], 1.0)
                nc.vector.memset(vx[:], 1.0)
        s0.clear()

        with nc.Fori(0, GROUPS) as g:
            norm.on_dve = norm.on_pool = 0
            with nc.Block() as block:
                @block.sync
                def _(sp):
                    sp.dma_start(c_tok[:], ctx_rows(ctx_in, g)).then_inc(p["ctx"], 16)
                    sp.dma_start(m_int[:].rearrange("p b k -> p (b k)"),
                                 mask_in.rearrange("(g b) k -> g (b k)", b=GB)[bass.ds(g, 1)].to_broadcast([P, GB * NC])).then_inc(p["ctx"], 16)
                    sp.dma_start(r_tok[:], tile_rows(res, g)).then_inc(p["in"], 16)
                    sp.dma_start(x_tok[:], tile_rows(x_in, g)).then_inc(p["in"], 16)
                    sp.wait_ge(p["out"], 1)
                    sp.dma_start(tile_rows(x_out, g), y_tok[:]).then_inc(p["store"], 16)
                    sp.wait_ge(p["store"], 16)

                @block.gpsimd
                def _(pool):
                    norm.pool(pool)
                    norm.pool(pool)
                    pool.wait_ge(p["kb"], 1)
                    at.pool(pool, lambda b: kT[:, b])
                    norm.pool(pool)

                @block.tensor
                def _(pe):
                    pe.wait_ge(p["ctx"], 32)
                    for b in range(GB):
                        m = nc.tensor.transpose(bank[:, 0, b * NC:(b + 1) * NC], c_tok[:, b], ident[0:NC, 0:NC])
                    m.then_inc(p["ct"], 1)
                    pe.wait_ge(p["cts"], 1)
                    nc.tensor.matmul(bank[:, 1, 0:GB * NC], wk[:], cT[:], start=True, stop=True).then_inc(p["k"], 1)
                    for b in range(GB):
                        m = nc.tensor.matmul(bank[0:NC, 2, b * D:(b + 1) * D], cT[:, b], wv[:], start=True, stop=True)
                    m.then_inc(p["v"], 1)
                    pe.wait_ge(p["xt"], 1)
                    for b in range(GB):
                        m = nc.tensor.transpose(bank[:, 3, b * P:(b + 1) * P], x_tok[:, b], ident[:])
                    m.then_inc(p["xts"], 1)
                    pe.wait_ge(p["q"], 1)
                    nc.tensor.matmul(bank[:, 4], wq[:], xT[:].rearrange("p b t -> p (b t)"), start=True, stop=True).then_inc(p["q"], 1)
                    pe.wait_ge(p["qs"], 1)
                    pe.wait_ge(p["ks"], 1)
                    pe.wait_ge(p["vb"], 1)
                    pe.wait_ge(p["mk"], 1)
                    at.pe(pe, lambda b: qT[:, b], lambda b, h: vx[:, b, h], wo)

                @block.scalar
                def _(act):
                    act.wait_ge(p["ct"], 1)
                    nc.scalar.activation(cT[:].rearrange("p b k -> p (b k)"), bank[:, 0, 0:GB * NC], ACT.Copy).then_inc(p["cts"], 1)
                    act.wait_ge(p["k"], 1)
                    nc.scalar.activation(kT[:].rearrange("p b k -> p (b k)"), bank[:, 1, 0:GB * NC], ACT.Identity,
                                         bias=vecs[:, 1:2]).then_inc(p["ks"], 1)
                    act.wait_ge(p["xts"], 1)
                    nc.scalar.activation(xT[:].rearrange("p b t -> p (b t)"), bank[:, 3], ACT.Copy).then_inc(p["q"], 1)
                    act.wait_ge(p["q"], 2)
                    nc.scalar.activation(qT[:].rearrange("p b t -> p (b t)"), bank[:, 4], ACT.Identity,
                                         bias=vecs[:, 0:1]).then_inc(p["qs"], 1)
                    at.act(act)

                @block.vector
                def _(dve):
                    dve.wait_ge(p["in"], 32)
                    norm.dve(dve, r_tok, z_tok)
                    dve.drain()
                    nc.vector.tensor_tensor(z_tok[:], z_tok[:], rows[:, 0].unsqueeze(1).to_broadcast([P, GB, D]), ALU.mult)
                    nc.vector.tensor_tensor(r_tok[:], x_tok[:], rows[:, 1].unsqueeze(1).to_broadcast([P, GB, D]), ALU.add)
                    dve.drain()
                    nc.vector.tensor_tensor(z_tok[:], z_tok[:], r_tok[:], ALU.add)
                    dve.drain()
                    norm.dve(dve, z_tok, x_tok).then_inc(p["xt"], 1)
                    dve.wait_ge(p["ctx"], 32)
                    nc.vector.tensor_scalar(keep[:], m_int[:], 0.0, None, ALU.not_equal)
                    dve.drain()
                    nc.vector.tensor_scalar(mbias[:], keep[0:3], 1.0, part[:, 0:1], ALU.subtract, ALU.mult).then_inc(p["mk"], 1)
                    dve.wait_ge(p["ks"], 1)
                    nc.vector.tensor_tensor(kT[:], kT[:], keep[:], ALU.mult).then_inc(p["kb"], 1)
                    dve.wait_ge(p["v"], 1)
                    nc.vector.tensor_tensor(vx[:, :, :, 0:DK], bank[0:NC, 2].rearrange("p (b h v) -> p b h v", b=GB, h=H),
                                            rows[0:NC, 2].rearrange("p (h v) -> p h v", h=H).unsqueeze(1).to_broadcast([NC, GB, H, DK]),
                                            ALU.add).then_inc(p["vb"], 1)
                    nc.vector.tensor_tensor(z_tok[:], x_tok[:], rows[:, 3].unsqueeze(1).to_broadcast([P, GB, D]), ALU.add)
                    dve.drain()

                    def add(b, psum):
                        nc.vector.tensor_tensor(r_tok[:, b], z_tok[:, b], psum, ALU.add)
                    at.dve(dve, add)
                    dve.drain()
                    norm.dve(dve, r_tok, y_tok).then_inc(p["out"], 1)
            s.clear()


def bf16_parts(v, n=3):
    out, rest = [], np.float32(v)
    for _ in range(n):
        bits = np.array([rest], np.float32).view(np.uint32) & np.uint32(0xFFFF0000)
        hi = bits.view(np.float32)[0]
        out.append(hi)
        rest = np.float32(rest - hi)
    return np.array(out, np.float32)


def xattn_host(i):
    A = lambda k: np.asarray(i["L0_xattn_" + k])
    return {"wq": A("wq").T, "wk": A("wk").T, "wv": A("wv").T, "wo": A("wo").T,
            "vecs": np.stack([A("bq"), A("bk")], 1),
            "rows": np.stack([np.asarray(i["L0_attn_normf_w"]), np.asarray(i["L0_attn_normf_b"]), A("bv"), A("bo")]),
            "part": -bf16_parts(BIG)[:, None]}

PH, NK, KD, EXPERTS = 8, 128, 64, 2048
FI = 2 * D
ROW = 2 * D + 2 * FI
IA, IB, OA, OB = 0, D, D + FI, D + 2 * FI


PER_GROUP = 16 * PH * GB // 2


def experts_stage(nc, w, consts, x_in, x_out):
    ident, half_neg = consts["ident"], consts["half_neg"]
    with ExitStack() as st:
        def sb(name, shape, dt=F32):
            return st.enter_context(nc.sbuf_tensor("ex_" + name, shape, dt))

        bank = st.enter_context(nc.psum_tensor("ex_bank", [P, 8, 512], F32))
        s = Sems(nc, st, ["ex_" + n for n in [
            "n_var", "n_rstd", "in", "xt", "xts", "sim", "top", "idx", "lin", "dgi", "hid", "gelu", "ht",
            "hts", "lout", "dgo", "y", "sum", "out", "store"]])
        p = Prefixed(s, "ex_")
        got = [st.enter_context(nc.semaphore(f"ex_got{i}")) for i in range(2)]
        w_sim = sb("w_sim", [P, 2 * PH, NK])
        w_in = sb("w_in", [P, FI])
        w_out = sb("w_out", [P, 2, D])
        x_tok, y_tok = sb("x_tok", [P, GB, D]), sb("y_tok", [P, GB, D])
        xT = sb("xT", [P, GB, SEQ])
        m8 = sb("m8", [P, 2 * PH, 8])
        i8 = sb("i8", [P, 2 * PH, 8], U32)
        iy = sb("iy", [P, PH])
        idx = [sb(f"idx{i}", [P, PH], U32) for i in range(2)]
        gate = [sb(f"gate{i}", [P, PH]) for i in range(2)]
        rowsb = [sb(f"rows{i}", [P, PH, ROW]) for i in range(2)]
        junk = sb("junk", [P, PH, FI])
        lin, lout = sb("lin", [P, PH]), sb("lout", [P, PH])
        dg_in = sb("dg_in", [P, PH, P])
        dg_out = sb("dg_out", [P, PH, P])
        hid = sb("hid", [P, FI])
        hidT = sb("hidT", [P, 2, P])
        norm = Norm(sb, p, "n", half_neg)

        s0 = Sems(nc, st, ["ex0_w", "ex0_m", "ex0_c"])
        wq = sb("wq", [KD, 2 * PH, D])
        keys = sb("keys", [KD, 2 * PH, NK])
        with nc.Block() as block:
            @block.sync
            def _(sp):
                for t, d in ((wq, w["wq"]), (keys, w["keys"]), (w_in, w["w_in"]), (w_out, w["w_out"])):
                    sp.dma_start(t[:], d).then_inc(s0["ex0_w"], 16)

            @block.tensor
            def _(pe):
                pe.wait_ge(s0["ex0_w"], 64)
                for j in range(2 * PH):
                    m = nc.tensor.matmul(bank[:, j // 4, (j % 4) * P:(j % 4 + 1) * P], wq[:, j], keys[:, j], start=True, stop=True)
                m.then_inc(s0["ex0_m"], 1)

            @block.scalar
            def _(act):
                act.wait_ge(s0["ex0_m"], 1)
                nc.scalar.activation(w_sim[:].rearrange("p (a h) k -> p a (h k)", a=4), bank[:, 0:4], ACT.Copy)
        s0.clear()

        with nc.Fori(0, GROUPS) as g:
            norm.on_dve = norm.on_pool = 0
            with nc.Block() as block:
                @block.sync
                def _(sp):
                    sp.dma_start(x_tok[:], tile_rows(x_in, g)).then_inc(p["in"], 16)
                    sp.wait_ge(p["out"], 1)
                    sp.dma_start(tile_rows(x_out, g), y_tok[:]).then_inc(p["store"], 16)
                    sp.wait_ge(p["store"], 16)

                @block.gpsimd
                def _(pool):
                    for b in range(GB):
                        pool.wait_ge(p["idx"], b + 1)
                        if b >= 2:
                            pool.wait_ge(p["y"], b - 1)
                        for h in range(PH):
                            nc.gpsimd.indirect_dma_start(rowsb[b % 2][:, h], None, w["table"],
                                                         bass.IndirectOffsetOnAxis(idx[b % 2][:, h:h + 1], 0)).then_inc(got[b % 2], 16)
                    norm.pool(pool)

                @block.tensor
                def _(pe):
                    pe.wait_ge(p["in"], 16)
                    for b in range(GB):
                        m = nc.tensor.transpose(bank[:, 7, b * P:(b + 1) * P], x_tok[:, b], ident[:])
                    m.then_inc(p["xt"], 1)
                    pe.wait_ge(p["xts"], 1)

                    def sims(b):
                        for j in range(4):
                            if b:
                                pe.wait_ge(p["top"], 4 * (b - 1) + j + 1)
                            nc.tensor.matmul(bank[:, j], xT[:, b], w_sim[:, 4 * j:4 * j + 4], start=True, stop=True).then_inc(p["sim"], 1)

                    sims(0)
                    for b in range(GB):
                        if b + 1 < GB:
                            sims(b + 1)
                        if b:
                            pe.wait_ge(p["gelu"], b)
                        pe.wait_ge(p["dgi"], b + 1)
                        nc.tensor.matmul(bank[:, 4, 0:FI], xT[:, b], w_in[:], start=True, stop=False)
                        for h in range(PH):
                            m = nc.tensor.matmul(bank[:, 4, 0:FI], dg_in[:, h], rowsb[b % 2][:, h, IB:IB + FI], start=False, stop=(h == PH - 1))
                        m.then_inc(p["hid"], 1)
                        pe.wait_ge(p["gelu"], b + 1)
                        for c in range(2):
                            m = nc.tensor.transpose(bank[:, 5, c * P:(c + 1) * P], hid[:, c * P:(c + 1) * P], ident[:])
                        m.then_inc(p["ht"], 1)
                        pe.wait_ge(p["hts"], b + 1)
                        pe.wait_ge(p["dgo"], b + 1)
                        if b:
                            pe.wait_ge(p["sum"], b)
                        for c in range(2):
                            nc.tensor.matmul(bank[:, 6, 0:D], hidT[:, c], w_out[:, c], start=(c == 0), stop=False)
                        for h in range(PH):
                            m = nc.tensor.matmul(bank[:, 6, 0:D], dg_out[:, h], rowsb[b % 2][:, h, OB:OB + D], start=False, stop=(h == PH - 1))
                        m.then_inc(p["y"], 1)

                @block.scalar
                def _(act):
                    act.wait_ge(p["xt"], 1)
                    nc.scalar.activation(xT[:].rearrange("p b t -> p (b t)"), bank[:, 7], ACT.Copy).then_inc(p["xts"], 1)
                    for b in range(GB):
                        act.wait_ge(p["lin"], b + 1)
                        if b:
                            act.wait_ge(p["hid"], b)
                        for h in range(PH):
                            m = nc.scalar.activation(dg_in[:, h], ident[:], ACT.Copy, scale=lin[:, h:h + 1])
                        m.then_inc(p["dgi"], 1)
                        act.wait_ge(p["hid"], b + 1)
                        if b:
                            act.wait_ge(p["ht"], b)
                            act.wait_ge(p["lout"], b)
                        nc.scalar.activation(hid[:], bank[:, 4, 0:FI], ACT.Gelu).then_inc(p["gelu"], 1)
                        act.wait_ge(p["ht"], b + 1)
                        if b:
                            act.wait_ge(p["y"], b)
                        nc.scalar.activation(hidT[:].rearrange("p c t -> p (c t)"), bank[:, 5, 0:2 * P], ACT.Copy).then_inc(p["hts"], 1)
                        act.wait_ge(p["lout"], b + 1)
                        for h in range(PH):
                            m = nc.scalar.activation(dg_out[:, h], ident[:], ACT.Copy, scale=lout[:, h:h + 1])
                        m.then_inc(p["dgo"], 1)

                @block.vector
                def _(dve):
                    def top(b):
                        i = b % 2
                        for j in range(4):
                            dve.wait_ge(p["sim"], 4 * b + j + 1)
                            for k in range(4):
                                nc.vector.max(m8[:, 4 * j + k], bank[:, j, k * NK:(k + 1) * NK])
                            dve.drain()
                            for k in range(4):
                                m = nc.vector.max_index(i8[:, 4 * j + k], m8[:, 4 * j + k], bank[:, j, k * NK:(k + 1) * NK])
                            m.then_inc(p["top"], 1)
                        dve.drain()
                        nc.vector.tensor_tensor(gate[i][:], m8[:, 0:PH, 0], m8[:, PH:, 0], ALU.add)
                        nc.vector.tensor_copy(iy[:], i8[:, PH:, 0])
                        dve.drain()
                        nc.vector.tensor_scalar(gate[i][:], gate[i][:], 0.0, None, ALU.max)
                        nc.vector.scalar_tensor_tensor(out=iy[:], in0=i8[:, 0:PH, 0], scalar=float(NK), in1=iy[:],
                                                       op0=ALU.mult, op1=ALU.add)
                        dve.drain()
                        if b >= 2:
                            dve.wait_ge(got[i], g * PER_GROUP + 16 * PH * (b // 2))
                        nc.vector.tensor_scalar(idx[i][:], iy[:], float(EXPERTS - 1), None, ALU.min).then_inc(p["idx"], 1)

                    top(0)
                    for b in range(GB):
                        i = b % 2
                        if b + 1 < GB:
                            top(b + 1)
                        dve.wait_ge(got[i], g * PER_GROUP + 16 * PH * (b // 2 + 1))
                        if b:
                            dve.wait_ge(p["dgi"], b)
                        nc.vector.tensor_tensor(junk[:, :, 0:D], rowsb[i][:, :, IA:IA + D], x_tok[:, b].unsqueeze(1).to_broadcast([P, PH, D]), ALU.mult)
                        dve.drain()
                        nc.vector.tensor_reduce(lin[:], junk[:, :, 0:D], AX.X, ALU.add)
                        dve.drain()
                        nc.vector.tensor_tensor(lin[:], lin[:], gate[i][:], ALU.mult).then_inc(p["lin"], 1)
                        dve.wait_ge(p["gelu"], b + 1)
                        if b:
                            dve.wait_ge(p["dgo"], b)
                        nc.vector.tensor_tensor(junk[:], rowsb[i][:, :, OA:OA + FI], hid[:].unsqueeze(1).to_broadcast([P, PH, FI]), ALU.mult)
                        dve.drain()
                        nc.vector.tensor_reduce(lout[:], junk[:], AX.X, ALU.add)
                        dve.drain()
                        nc.vector.tensor_tensor(lout[:], lout[:], gate[i][:], ALU.mult).then_inc(p["lout"], 1)
                        dve.wait_ge(p["y"], b + 1)
                        nc.vector.tensor_tensor(y_tok[:, b], x_tok[:, b], bank[:, 6, 0:D], ALU.add).then_inc(p["sum"], 1)
                    dve.drain()
                    norm.dve(dve, y_tok, y_tok).then_inc(p["out"], 1)
            s.clear()


def experts_host(i):
    A = lambda k: np.asarray(i["L0_ffn_" + k])
    return {"wq": A("Wq").reshape(2 * PH, KD, D).transpose(1, 0, 2),
            "keys": A("keys").transpose(3, 2, 0, 1).reshape(KD, 2 * PH, NK),
            "w_in": A("W_in").T, "w_out": A("W_out").T.reshape(2, P, D).transpose(1, 0, 2),
            "table": np.concatenate([A("in_a"), A("in_b"), A("out_a"), A("out_b")], axis=1)}

GN, WIN = 64, 8
GUIDE = 0.4
EPS_MAG, EPS_COS, EPS_WSUM = 1e-6, 1e-8, 1e-8


def trajectory_stage(nc, w, consts, x_in, x_out):
    ident, half_neg = consts["ident"], consts["half_neg"]
    with ExitStack() as st:
        def sb(name, shape, dt=F32):
            return st.enter_context(nc.sbuf_tensor("tj_" + name, shape, dt))

        bank = st.enter_context(nc.psum_tensor("tj_bank", [P, 8, 512], F32))
        s = Sems(nc, st, ["tj_" + n for n in [
            "n_var", "n_rstd", "in", "diff", "ds", "sq", "mag", "nrm", "sq2", "mag2", "mw", "nt", "nts", "sim", "sh",
            "ex", "gw", "gt", "gts", "inf", "cb", "tr", "out", "store"]])
        p = Prefixed(s, "tj_")
        shiftm, band = sb("shiftm", [P, P]), sb("band", [P, P])
        guide = sb("guide", [GN, D])
        gsq = sb("gsq", [GN, D])
        gr = sb("gr", [GN, 1])
        gr2 = sb("gr2", [GN, 1])
        half = sb("half", [P, GB])
        gnT = sb("gnT", [P, GN])
        x_tok, y_tok = sb("x_tok", [P, GB, D]), sb("y_tok", [P, GB, D])
        diff, nrm, sq = sb("diff", [P, GB, D]), sb("nrm", [P, GB, D]), sb("sq", [P, GB, D])
        m2, mag, ok, t4, inv, a2, an, mx, mw, sm = (sb(n, [P, GB]) for n in
                                                    ("m2", "mag", "ok", "t4", "inv", "a2", "an", "mx", "mw", "sm"))
        nT = sb("nT", [P, GB, P])
        sim = sb("sim", [P, GB, GN])
        gwT = sb("gwT", [GN, GB, P])
        cb = sb("cb", [P, GB, D])
        ws = sb("ws", [P, GB])
        norm = Norm(sb, p, "n", half_neg)

        s0 = Sems(nc, st, ["tj0_w", "tj0_a", "tj0_b", "tj0_c", "tj0_d"])
        with nc.Block() as block:
            @block.sync
            def _(sp):
                for t, d in ((shiftm, w["shiftm"]), (band, w["band"]), (guide, w["guide"])):
                    sp.dma_start(t[:], d).then_inc(s0["tj0_w"], 16)

            @block.vector
            def _(dve):
                nc.vector.memset(half[:], 0.5)
                dve.wait_ge(s0["tj0_w"], 48)
                nc.vector.tensor_tensor(gsq[:], guide[:], guide[:], ALU.mult)
                dve.drain()
                nc.vector.tensor_reduce(gr[:], gsq[:], AX.X, ALU.add).then_inc(s0["tj0_a"], 1)
                dve.wait_ge(s0["tj0_b"], 1)
                nc.vector.tensor_scalar(gr2[:], gr2[:], EPS_COS, None, ALU.max)
                dve.drain()
                nc.vector.reciprocal(gr[:], gr2[:])
                dve.drain()
                nc.vector.tensor_scalar(gsq[:], guide[:], gr[:, 0:1], None, ALU.mult).then_inc(s0["tj0_c"], 1)

            @block.gpsimd
            def _(pool):
                pool.wait_ge(s0["tj0_a"], 1)
                nc.gpsimd.tensor_tensor(gr2[:], gr[:], half[0:GN, 0:1], ALU.pow).then_inc(s0["tj0_b"], 1)

            @block.tensor
            def _(pe):
                pe.wait_ge(s0["tj0_c"], 1)
                nc.tensor.transpose(bank[:, 0, 0:GN], gsq[:], ident[0:GN, 0:GN]).then_inc(s0["tj0_d"], 1)

            @block.scalar
            def _(act):
                act.wait_ge(s0["tj0_d"], 1)
                nc.scalar.activation(gnT[:], bank[:, 0, 0:GN], ACT.Copy)
        s0.clear()

        def flat(t):
            return t[:].rearrange("p b d -> p (b d)")

        def wide(t, n=D):
            return t[:].unsqueeze(2).to_broadcast([P, GB, n])

        with nc.Fori(0, GROUPS) as g:
            norm.on_dve = norm.on_pool = 0
            with nc.Block() as block:
                @block.sync
                def _(sp):
                    sp.dma_start(x_tok[:], tile_rows(x_in, g)).then_inc(p["in"], 16)
                    sp.wait_ge(p["out"], 1)
                    sp.dma_start(tile_rows(x_out, g), y_tok[:]).then_inc(p["store"], 16)
                    sp.wait_ge(p["store"], 16)

                @block.gpsimd
                def _(pool):
                    pool.wait_ge(p["sq"], 1)
                    nc.gpsimd.tensor_tensor(mag[:], m2[:], half[:], ALU.pow).then_inc(p["mag"], 1)
                    pool.wait_ge(p["sq2"], 1)
                    nc.gpsimd.tensor_tensor(an[:], a2[:], half[:], ALU.pow).then_inc(p["mag2"], 1)
                    norm.pool(pool)

                @block.tensor
                def _(pe):
                    pe.wait_ge(p["in"], 16)
                    nc.tensor.matmul(bank[:, 0], shiftm[:], flat(x_tok), start=True, stop=True).then_inc(p["diff"], 1)
                    pe.wait_ge(p["nrm"], 1)
                    for b in range(GB):
                        m = nc.tensor.transpose(bank[:, 1, b * P:(b + 1) * P], nrm[:, b], ident[:])
                    m.then_inc(p["nt"], 1)
                    pe.wait_ge(p["nts"], 1)
                    for b in range(GB):
                        m = nc.tensor.matmul(bank[:, 2, b * GN:(b + 1) * GN], nT[:, b], gnT[:], start=True, stop=True)
                    m.then_inc(p["sim"], 1)
                    pe.wait_ge(p["gw"], 1)
                    for b in range(GB):
                        m = nc.tensor.transpose(bank[0:GN, 3, b * P:(b + 1) * P], sim[:, b], ident[:])
                    m.then_inc(p["gt"], 1)
                    pe.wait_ge(p["gts"], 1)
                    for b in range(GB):
                        m = nc.tensor.matmul(bank[:, 4, b * D:(b + 1) * D], gwT[:, b], guide[:], start=True, stop=True)
                    m.then_inc(p["inf"], 1)
                    pe.wait_ge(p["cb"], 1)
                    nc.tensor.matmul(bank[:, 5], band[:], flat(cb), start=True, stop=True)
                    nc.tensor.matmul(bank[:, 6, 0:GB], band[:], mw[:], start=True, stop=True).then_inc(p["tr"], 1)

                @block.scalar
                def _(act):
                    act.wait_ge(p["diff"], 1)
                    nc.scalar.activation(flat(diff), bank[:, 0], ACT.Copy).then_inc(p["ds"], 1)
                    act.wait_ge(p["mag"], 1)
                    nc.scalar.activation(mw[:], mag[:], ACT.Tanh, scale=2.0).then_inc(p["mw"], 1)
                    act.wait_ge(p["nt"], 1)
                    nc.scalar.activation(flat(nT), bank[:, 1], ACT.Copy).then_inc(p["nts"], 1)
                    act.wait_ge(p["sh"], 1)
                    nc.scalar.activation(flat(sim), flat(sim), ACT.Exp, scale=2.0).then_inc(p["ex"], 1)
                    act.wait_ge(p["gt"], 1)
                    nc.scalar.activation(flat(gwT), bank[0:GN, 3], ACT.Copy).then_inc(p["gts"], 1)

                @block.vector
                def _(dve):
                    dve.wait_ge(p["ds"], 1)
                    nc.vector.tensor_tensor(sq[:], diff[:], diff[:], ALU.mult)
                    dve.drain()
                    nc.vector.tensor_reduce(m2[:], sq[:], AX.X, ALU.add).then_inc(p["sq"], 1)
                    dve.wait_ge(p["mag"], 1)
                    nc.vector.tensor_scalar(ok[:], mag[:], EPS_MAG, None, ALU.is_gt)
                    dve.drain()
                    nc.vector.tensor_tensor(t4[:], mag[:], ok[:], ALU.mult)
                    nc.vector.tensor_scalar(inv[:], ok[:], -1.0, 1.0, ALU.mult, ALU.add)
                    dve.drain()
                    nc.vector.tensor_tensor(t4[:], t4[:], inv[:], ALU.add)
                    dve.drain()
                    nc.vector.reciprocal(inv[:], t4[:])
                    dve.drain()
                    nc.vector.tensor_tensor(inv[:], inv[:], ok[:], ALU.mult)
                    dve.drain()
                    nc.vector.tensor_tensor(nrm[:], diff[:], wide(inv), ALU.mult).then_inc(p["nrm"], 1)
                    dve.drain()
                    nc.vector.tensor_tensor(sq[:], nrm[:], nrm[:], ALU.mult)
                    dve.drain()
                    nc.vector.tensor_reduce(a2[:], sq[:], AX.X, ALU.add).then_inc(p["sq2"], 1)
                    dve.wait_ge(p["mag2"], 1)
                    nc.vector.tensor_scalar(an[:], an[:], EPS_COS, None, ALU.max)
                    dve.drain()
                    nc.vector.reciprocal(a2[:], an[:])
                    dve.drain()
                    dve.wait_ge(p["sim"], 1)
                    nc.vector.tensor_tensor(sim[:], bank[:, 2, 0:GB * GN].rearrange("p (b k) -> p b k", b=GB), wide(a2, GN), ALU.mult)
                    dve.drain()
                    nc.vector.tensor_reduce(mx[:], sim[:], AX.X, ALU.max)
                    dve.drain()
                    nc.vector.tensor_tensor(sim[:], sim[:], wide(mx, GN), ALU.subtract).then_inc(p["sh"], 1)
                    dve.wait_ge(p["ex"], 1)
                    nc.vector.tensor_reduce(sm[:], sim[:], AX.X, ALU.add)
                    dve.drain()
                    nc.vector.reciprocal(mx[:], sm[:])
                    dve.drain()
                    nc.vector.tensor_tensor(sim[:], sim[:], wide(mx, GN), ALU.mult).then_inc(p["gw"], 1)
                    nc.vector.tensor_scalar(sq[:], nrm[:], 1.0 - GUIDE, None, ALU.mult)
                    dve.drain()
                    dve.wait_ge(p["inf"], 1)
                    nc.vector.scalar_tensor_tensor(out=flat(sq), in0=bank[:, 4], scalar=GUIDE, in1=flat(sq), op0=ALU.mult, op1=ALU.add)
                    dve.drain()
                    dve.wait_ge(p["mw"], 1)
                    nc.vector.tensor_tensor(cb[:], sq[:], wide(mw), ALU.mult).then_inc(p["cb"], 1)
                    dve.wait_ge(p["tr"], 1)
                    nc.vector.tensor_scalar(ws[:], bank[:, 6, 0:GB], EPS_WSUM, None, ALU.max)
                    dve.drain()
                    nc.vector.reciprocal(sm[:], ws[:])
                    dve.drain()
                    nc.vector.tensor_tensor(cb[:], bank[:, 5].rearrange("p (b d) -> p b d", b=GB), wide(sm), ALU.mult)
                    dve.drain()
                    nc.vector.tensor_tensor(sq[:], cb[:], x_tok[:], ALU.add)
                    dve.drain()
                    norm.dve(dve, sq, y_tok).then_inc(p["out"], 1)
            s.clear()


def trajectory_host(i):
    shift = np.zeros((SEQ, SEQ), np.float32)
    band = np.zeros((SEQ, SEQ), np.float32)
    for j in range(SEQ - 1):
        shift[j + 1, j], shift[j, j] = 1.0, -1.0
    for pos in range(1, SEQ):
        width = min(pos, WIN)
        for k in range(WIN):
            j, at = k - (WIN - width), pos - WIN + k
            if at >= 0:
                band[at, pos] = 0.1 + 0.9 * j / max(width - 1, 1) if width > 1 else 0.1
    return {"shiftm": shift, "band": band, "guide": np.asarray(i["L1_attn_guidance_trajectories"])}

FF, FC = 512, 512 // P


def decoder_stage(nc, w, consts, x_in, ctx_in, x_out):
    ident, hmask, half_neg = consts["ident"], consts["hmask"], consts["half_neg"]
    with ExitStack() as st:
        def sb(name, shape, dt=F32):
            return st.enter_context(nc.sbuf_tensor("de_" + name, shape, dt))

        bank = st.enter_context(nc.psum_tensor("de_bank", [P, 8, 512], F32))
        s = Sems(nc, st, ["de_" + n for n in [
            "n_var", "n_rstd", "in", "ctx", "ct", "cts", "k", "ks", "v", "vb", "xt", "xts", "vx", "x1", "x1t", "x1s",
            "q", "qs", "x2", "x2t", "x2s", "f1", "f1s", "f2", "out", "store"]
            + ["s_" + n for n in ATTN_SEMS] + ["c_" + n for n in ATTN_SEMS]])
        p = Prefixed(s, "de_")
        wq, wk, wv, wo, ws = (sb(n, [P, D]) for n in ("wq", "wk", "wv", "wo", "ws"))
        w1, w2 = sb("w1", [P, FF]), sb("w2", [P, FC, D])
        vecs = sb("vecs", [P, 2 + FC])
        rows = sb("rows", [P, 10, D])
        SO, BV, CO, B2, G1 = 0, 1, 2, 3, 4
        x_tok, a_tok, b_tok, y_tok = (sb(n, [P, GB, D]) for n in ("x_tok", "a_tok", "b_tok", "y_tok"))
        c_tok = sb("c_tok", [NC, GB, D])
        xT, qT = sb("xT", [P, GB, SEQ]), sb("qT", [P, GB, SEQ])
        cT, kT = sb("cT", [P, GB, NC]), sb("kT", [P, GB, NC])
        vself = sb("vself", [P, GB, H, VW])
        vx = sb("vx", [NC, GB, H, VW])
        hT = sb("hT", [P, FC, TOK])
        norm = Norm(sb, p, "n", half_neg)
        own = Attention(nc, sb, p, "s", bank, ident, hmask, SEQ, D ** -0.5, topk=True)
        cross = Attention(nc, sb, p, "c", bank, ident, hmask, NC, DK ** -0.5)

        s0 = Sems(nc, st, ["de0_w"])
        with nc.Block() as block:
            @block.sync
            def _(sp):
                loads = [(wq, "wq"), (wk, "wk"), (wv, "wv"), (wo, "wo"), (ws, "ws"), (w1, "w1"), (w2, "w2"), (vecs, "vecs")]
                for t, k in loads:
                    sp.dma_start(t[:], w[k]).then_inc(s0["de0_w"], 16)
                sp.dma_start(rows[:].rearrange("p r d -> p (r d)"), w["rows"].rearrange("r d -> (r d)").unsqueeze(0)
                             .to_broadcast([P, 10 * D])).then_inc(s0["de0_w"], 16)
                sp.wait_ge(s0["de0_w"], 16 * (len(loads) + 1))

            @block.vector
            def _(dve):
                nc.vector.memset(vx[:], 1.0)
                nc.vector.memset(vself[:], 1.0)
                for i in range(2):
                    nc.vector.memset(own.sp[i][:], LOW)
        s0.clear()

        def flat(t):
            return t[:].rearrange("p b d -> p (b d)")

        def wide_row(r):
            return rows[:, r].unsqueeze(1).to_broadcast([P, GB, D])

        with nc.Fori(0, GROUPS) as g:
            norm.on_dve = norm.on_pool = 0
            with nc.Block() as block:
                @block.sync
                def _(sp):
                    sp.dma_start(x_tok[:], tile_rows(x_in, g)).then_inc(p["in"], 16)
                    sp.dma_start(c_tok[:], ctx_rows(ctx_in, g)).then_inc(p["ctx"], 16)
                    sp.wait_ge(p["out"], 1)
                    sp.dma_start(tile_rows(x_out, g), y_tok[:]).then_inc(p["store"], 16)
                    sp.wait_ge(p["store"], 16)

                @block.gpsimd
                def _(pool):
                    pool.wait_ge(p["xts"], 1)
                    own.pool(pool, lambda b: xT[:, b])
                    norm.pool(pool)
                    pool.wait_ge(p["ks"], 1)
                    cross.pool(pool, lambda b: kT[:, b])
                    for _ in range(3):
                        norm.pool(pool)

                @block.tensor
                def _(pe):
                    pe.wait_ge(p["in"], 16)
                    for b in range(GB):
                        m = nc.tensor.transpose(bank[:, 0, b * P:(b + 1) * P], x_tok[:, b], ident[:])
                    m.then_inc(p["xt"], 1)
                    pe.wait_ge(p["ctx"], 16)
                    for b in range(GB):
                        m = nc.tensor.transpose(bank[:, 1, b * NC:(b + 1) * NC], c_tok[:, b], ident[0:NC, 0:NC])
                    m.then_inc(p["ct"], 1)
                    pe.wait_ge(p["cts"], 1)
                    nc.tensor.matmul(bank[:, 2, 0:GB * NC], wk[:], flat(cT), start=True, stop=True).then_inc(p["k"], 1)
                    for b in range(GB):
                        m = nc.tensor.matmul(bank[0:NC, 3, b * D:(b + 1) * D], cT[:, b], wv[:], start=True, stop=True)
                    m.then_inc(p["v"], 1)
                    pe.wait_ge(p["xts"], 1)
                    pe.wait_ge(p["ks"], 1)
                    pe.wait_ge(p["vb"], 1)
                    pe.wait_ge(p["vx"], 1)
                    own.pe(pe, lambda b: xT[:, b], lambda b, h: vself[:, b, h], ws)
                    pe.wait_ge(p["x1"], 1)
                    for b in range(GB):
                        m = nc.tensor.transpose(bank[:, 0, b * P:(b + 1) * P], a_tok[:, b], ident[:])
                    m.then_inc(p["x1t"], 1)
                    pe.wait_ge(p["x1s"], 1)
                    nc.tensor.matmul(bank[:, 1], wq[:], flat(xT), start=True, stop=True).then_inc(p["q"], 1)
                    pe.wait_ge(p["qs"], 1)
                    cross.pe(pe, lambda b: qT[:, b], lambda b, h: vx[:, b, h], wo)
                    pe.wait_ge(p["x2"], 1)
                    for b in range(GB):
                        m = nc.tensor.transpose(bank[:, 0, b * P:(b + 1) * P], a_tok[:, b], ident[:])
                    m.then_inc(p["x2t"], 1)
                    pe.wait_ge(p["x2s"], 1)
                    for c in range(FC):
                        nc.tensor.matmul(bank[:, 1 + c], w1[:, c * P:(c + 1) * P], flat(xT), start=True, stop=True).then_inc(p["f1"], 1)
                    pe.wait_ge(p["f1s"], FC)
                    for b in range(GB):
                        for c in range(FC):
                            m = nc.tensor.matmul(bank[:, 5, b * D:(b + 1) * D], hT[:, c, b * SEQ:(b + 1) * SEQ], w2[:, c],
                                                 start=(c == 0), stop=(c == FC - 1))
                    m.then_inc(p["f2"], 1)

                @block.scalar
                def _(act):
                    act.wait_ge(p["xt"], 1)
                    nc.scalar.activation(flat(xT), bank[:, 0], ACT.Copy).then_inc(p["xts"], 1)
                    act.wait_ge(p["ct"], 1)
                    nc.scalar.activation(flat(cT), bank[:, 1, 0:GB * NC], ACT.Copy).then_inc(p["cts"], 1)
                    act.wait_ge(p["k"], 1)
                    nc.scalar.activation(flat(kT), bank[:, 2, 0:GB * NC], ACT.Identity, bias=vecs[:, 1:2]).then_inc(p["ks"], 1)
                    own.act(act)
                    act.wait_ge(p["x1t"], 1)
                    nc.scalar.activation(flat(xT), bank[:, 0], ACT.Copy).then_inc(p["x1s"], 1)
                    act.wait_ge(p["q"], 1)
                    nc.scalar.activation(flat(qT), bank[:, 1], ACT.Identity, bias=vecs[:, 0:1]).then_inc(p["qs"], 1)
                    cross.act(act)
                    act.wait_ge(p["x2t"], 1)
                    nc.scalar.activation(flat(xT), bank[:, 0], ACT.Copy).then_inc(p["x2s"], 1)
                    for c in range(FC):
                        act.wait_ge(p["f1"], c + 1)
                        nc.scalar.activation(hT[:, c], bank[:, 1 + c], ACT.Gelu, bias=vecs[:, 2 + c:3 + c]).then_inc(p["f1s"], 1)

                @block.vector
                def _(dve):
                    dve.wait_ge(p["in"], 16)
                    nc.vector.tensor_copy(vself[:, :, :, 0:DK], x_tok[:].rearrange("p b (h v) -> p b h v", v=DK)).then_inc(p["vx"], 1)
                    nc.vector.tensor_tensor(b_tok[:], x_tok[:], wide_row(SO), ALU.add)
                    dve.wait_ge(p["v"], 1)
                    nc.vector.tensor_tensor(vx[:, :, :, 0:DK], bank[0:NC, 3].rearrange("p (b h v) -> p b h v", b=GB, h=H),
                                            rows[0:NC, BV].rearrange("p (h v) -> p h v", h=H).unsqueeze(1).to_broadcast([NC, GB, H, DK]),
                                            ALU.add).then_inc(p["vb"], 1)
                    dve.drain()

                    def add(b, psum):
                        nc.vector.tensor_tensor(a_tok[:, b], b_tok[:, b], psum, ALU.add)

                    def affine_norm(k, src, dst):
                        norm.dve(dve, src, y_tok)
                        dve.drain()
                        nc.vector.tensor_tensor(y_tok[:], y_tok[:], wide_row(G1 + 2 * k), ALU.mult)
                        dve.drain()
                        return nc.vector.tensor_tensor(dst[:], y_tok[:], wide_row(G1 + 2 * k + 1), ALU.add)

                    own.dve(dve, add)
                    dve.drain()
                    affine_norm(0, a_tok, a_tok).then_inc(p["x1"], 1)
                    dve.wait_ge(p["x1"], 1)
                    nc.vector.tensor_tensor(b_tok[:], a_tok[:], wide_row(CO), ALU.add)
                    dve.wait_ge(p["x1t"], 1)
                    dve.drain()
                    cross.dve(dve, add)
                    dve.drain()
                    affine_norm(1, a_tok, a_tok).then_inc(p["x2"], 1)
                    dve.wait_ge(p["x2"], 1)
                    nc.vector.tensor_tensor(b_tok[:], a_tok[:], wide_row(B2), ALU.add)
                    dve.drain()
                    dve.wait_ge(p["f2"], 1)
                    nc.vector.tensor_tensor(a_tok[:], b_tok[:], bank[:, 5].rearrange("p (b d) -> p b d", b=GB), ALU.add)
                    dve.drain()
                    affine_norm(2, a_tok, b_tok)
                    dve.drain()
                    nc.vector.tensor_tensor(a_tok[:], b_tok[:], x_tok[:], ALU.add)
                    dve.drain()
                    norm.dve(dve, a_tok, y_tok).then_inc(p["out"], 1)
            s.clear()


def decoder_host(i):
    A = lambda k: np.asarray(i["L1_xattn_" + k])
    iw, ib = A("cross_in_w"), A("cross_in_b")
    return {"wq": iw[:D].T, "wk": iw[D:2 * D].T, "wv": iw[2 * D:].T, "wo": A("cross_out_w").T, "ws": A("self_out_w").T,
            "w1": A("ffn_w1").T, "w2": A("ffn_w2").T.reshape(FC, P, D).transpose(1, 0, 2),
            "vecs": np.concatenate([ib[:D, None], ib[D:2 * D, None], A("ffn_b1").reshape(FC, P).T], axis=1),
            "rows": np.stack([A("self_out_b"), ib[2 * D:], A("cross_out_b"), A("ffn_b2"), A("ln1_g"), A("ln1_b"),
                              A("ln2_g"), A("ln2_b"), A("ln3_g"), A("ln3_b")])}


ROUND = 1.5 * 2.0 ** 23
QMAX, QMIN, EPS_Q = 127.0, -128.0, 1e-5


def bitlinear_stage(nc, w, consts, x_in, x_out):
    ident, half_neg = consts["ident"], consts["half_neg"]
    with ExitStack() as st:
        def sb(name, shape, dt=F32):
            return st.enter_context(nc.sbuf_tensor("bl_" + name, shape, dt))

        bank = st.enter_context(nc.psum_tensor("bl_bank", [P, 6, 512], F32))
        bankb = st.enter_context(nc.psum_tensor("bl_bankb", [P, 2, 1024], BF16))
        s = Sems(nc, st, ["bl_" + n for n in [
            "n_var", "n_rstd", "in", "xq", "xt", "xts", "gu", "sg", "hq", "ht", "hts", "y", "sum", "out", "store"]])
        p = Prefixed(s, "bl_")
        wts = [sb(f"w{k}", [P, FF]) for k in range(3)]
        wa = sb("wa", [P, FF])
        wb = [sb(f"wb{k}", [P, FF], BF16) for k in range(3)]
        identb = sb("identb", [P, P], BF16)
        ones = sb("ones", [P, P])
        asum, mean, wsc = (sb(n, [P, 3]) for n in ("asum", "mean", "wsc"))
        x_tok, y_tok = sb("x_tok", [P, GB, D]), sb("y_tok", [P, GB, D])
        t_tok = sb("t_tok", [P, GB, D])
        xq = sb("xq", [P, GB, D], BF16)
        xqT = sb("xqT", [P, GB, P], BF16)
        mx, sc, rg, ru = (sb(n, [P, GB]) for n in ("mx", "sc", "rg", "ru"))
        sg = [sb(f"sg{i}", [P, FF]) for i in range(2)]
        hh = [sb(f"hh{i}", [P, FF]) for i in range(2)]
        hm, hs, hr = (sb(n, [P, GB]) for n in ("hm", "hs", "hr"))
        hq = [sb(f"hq{i}", [P, FF], BF16) for i in range(2)]
        hqT = [sb(f"hqT{i}", [P, FF], BF16) for i in range(2)]
        norm = Norm(sb, p, "n", half_neg)

        s0 = Sems(nc, st, ["bl0_w", "bl0_s", "bl0_m"])
        with nc.Block() as block:
            @block.sync
            def _(sp):
                for t, k in zip(wts, ("gate", "up", "down")):
                    sp.dma_start(t[:], w[k]).then_inc(s0["bl0_w"], 16)

            @block.tensor
            def _(pe):
                pe.wait_ge(s0["bl0_s"], 1)
                nc.tensor.matmul(bank[:, 0, 0:3], ones[:], asum[:], start=True, stop=True).then_inc(s0["bl0_m"], 1)

            @block.vector
            def _(dve):
                nc.vector.memset(ones[:], 1.0)
                nc.vector.tensor_copy(identb[:], ident[:])
                dve.wait_ge(s0["bl0_w"], 48)
                for k in range(3):
                    nc.vector.tensor_reduce(asum[:, k:k + 1], wts[k][:], AX.X, ALU.add, apply_absolute_value=True)
                    dve.drain()
                nc.vector.tensor_copy(mean[:], asum[:]).then_inc(s0["bl0_s"], 1)
                dve.wait_ge(s0["bl0_m"], 1)
                nc.vector.tensor_scalar(mean[:], bank[:, 0, 0:3], 1.0 / (P * FF), EPS_Q, ALU.mult, ALU.max)
                dve.drain()
                nc.vector.reciprocal(wsc[:], mean[:])
                dve.drain()
                for k in range(3):
                    nc.vector.tensor_scalar(wa[:], wts[k][:], wsc[:, k:k + 1], ROUND, ALU.mult, ALU.add)
                    dve.drain()
                    nc.vector.tensor_scalar(wa[:], wa[:], -ROUND, 1.0, ALU.add, ALU.min)
                    dve.drain()
                    nc.vector.tensor_scalar(wb[k][:], wa[:], -1.0, None, ALU.max)
                    dve.drain()
        s0.clear()

        def flat(t):
            return t[:].rearrange("p b d -> p (b d)")

        with nc.Fori(0, GROUPS) as g:
            norm.on_dve = norm.on_pool = 0
            with nc.Block() as block:
                @block.sync
                def _(sp):
                    sp.dma_start(x_tok[:], tile_rows(x_in, g)).then_inc(p["in"], 16)
                    sp.wait_ge(p["out"], 1)
                    sp.dma_start(tile_rows(x_out, g), y_tok[:]).then_inc(p["store"], 16)
                    sp.wait_ge(p["store"], 16)

                @block.gpsimd
                def _(pool):
                    norm.pool(pool)

                @block.tensor
                def _(pe):
                    pe.wait_ge(p["xq"], 1)
                    for b in range(GB):
                        m = nc.tensor.transpose(bankb[:, 0, b * P:(b + 1) * P], xq[:, b], identb[:])
                    m.then_inc(p["xt"], 1)
                    pe.wait_ge(p["xts"], 1)

                    def gate_up(b):
                        if b >= 2:
                            pe.wait_ge(p["hq"], b - 1)
                        for k in range(2):
                            nc.tensor.matmul(bank[:, 2 * (b % 2) + k], xqT[:, b], wb[k][:], start=True, stop=True).then_inc(p["gu"], 1)

                    gate_up(0)
                    for b in range(GB):
                        if b + 1 < GB:
                            gate_up(b + 1)
                        pe.wait_ge(p["hq"], b + 1)
                        if b:
                            pe.wait_ge(p["hts"], b)
                        for c in range(FC):
                            m = nc.tensor.transpose(bankb[:, 1, c * P:(c + 1) * P], hq[b % 2][:, c * P:(c + 1) * P], identb[:])
                        m.then_inc(p["ht"], 1)
                        pe.wait_ge(p["hts"], b + 1)
                        if b:
                            pe.wait_ge(p["sum"], b)
                        for c in range(FC):
                            m = nc.tensor.matmul(bank[:, 4, 0:D], hqT[b % 2][:, c * P:(c + 1) * P], wb[2][:, c * D:(c + 1) * D],
                                                 start=(c == 0), stop=(c == FC - 1))
                        m.then_inc(p["y"], 1)

                @block.scalar
                def _(act):
                    act.wait_ge(p["xt"], 1)
                    nc.scalar.activation(flat(xqT), bankb[:, 0, 0:TOK], ACT.Copy).then_inc(p["xts"], 1)

                    def silu(b):
                        act.wait_ge(p["gu"], 2 * b + 1)
                        if b >= 2:
                            act.wait_ge(p["hq"], b - 1)
                        nc.scalar.activation(sg[b % 2][:], bank[:, 2 * (b % 2)], ACT.Silu, scale=rg[:, b:b + 1]).then_inc(p["sg"], 1)

                    silu(0)
                    for b in range(GB):
                        if b + 1 < GB:
                            silu(b + 1)
                        act.wait_ge(p["ht"], b + 1)
                        if b >= 2:
                            act.wait_ge(p["y"], b - 1)
                        nc.scalar.activation(hqT[b % 2][:], bankb[:, 1, 0:FF], ACT.Copy).then_inc(p["hts"], 1)

                @block.vector
                def _(dve):
                    def magnitude(dst, src):
                        nc.vector.tensor_reduce(dst, src, AX.X, ALU.max, apply_absolute_value=True)
                        dve.drain()
                        nc.vector.tensor_scalar(dst, dst, EPS_Q, 1.0 / QMAX, ALU.max, ALU.mult)
                        dve.drain()

                    dve.wait_ge(p["in"], 16)
                    magnitude(mx[:], x_tok[:])
                    nc.vector.reciprocal(sc[:], mx[:])
                    nc.vector.tensor_scalar(rg[:], mx[:], mean[:, 0:1], None, ALU.mult)
                    nc.vector.tensor_scalar(ru[:], mx[:], mean[:, 1:2], None, ALU.mult)
                    dve.drain()
                    for b in range(GB):
                        nc.vector.tensor_scalar(t_tok[:, b], x_tok[:, b], sc[:, b:b + 1], ROUND, ALU.mult, ALU.add)
                    dve.drain()
                    nc.vector.tensor_scalar(t_tok[:], t_tok[:], -ROUND, QMAX, ALU.add, ALU.min)
                    dve.drain()
                    nc.vector.tensor_scalar(xq[:], t_tok[:], QMIN, None, ALU.max).then_inc(p["xq"], 1)
                    for b in range(GB):
                        i = b % 2
                        dve.wait_ge(p["sg"], b + 1)
                        dve.wait_ge(p["gu"], 2 * b + 2)
                        nc.vector.scalar_tensor_tensor(out=hh[i][:], in0=bank[:, 2 * i + 1], scalar=ru[:, b:b + 1], in1=sg[i][:],
                                                       op0=ALU.mult, op1=ALU.mult)
                        dve.drain()
                        magnitude(hm[:, b:b + 1], hh[i][:])
                        nc.vector.reciprocal(hs[:, b:b + 1], hm[:, b:b + 1])
                        nc.vector.tensor_scalar(hr[:, b:b + 1], hm[:, b:b + 1], mean[:, 2:3], None, ALU.mult)
                        dve.drain()
                        nc.vector.tensor_scalar(hh[i][:], hh[i][:], hs[:, b:b + 1], ROUND, ALU.mult, ALU.add)
                        dve.drain()
                        nc.vector.tensor_scalar(hh[i][:], hh[i][:], -ROUND, QMAX, ALU.add, ALU.min)
                        dve.drain()
                        if b >= 2:
                            dve.wait_ge(p["ht"], b - 1)
                        nc.vector.tensor_scalar(hq[i][:], hh[i][:], QMIN, None, ALU.max).then_inc(p["hq"], 1)
                        if b:
                            dve.wait_ge(p["y"], b)
                            nc.vector.scalar_tensor_tensor(out=t_tok[:, b - 1], in0=bank[:, 4, 0:D], scalar=hr[:, b - 1:b],
                                                           in1=x_tok[:, b - 1], op0=ALU.mult, op1=ALU.add).then_inc(p["sum"], 1)
                    dve.wait_ge(p["y"], GB)
                    nc.vector.scalar_tensor_tensor(out=t_tok[:, GB - 1], in0=bank[:, 4, 0:D], scalar=hr[:, GB - 1:GB],
                                                   in1=x_tok[:, GB - 1], op0=ALU.mult, op1=ALU.add)
                    dve.drain()
                    norm.dve(dve, t_tok, y_tok).then_inc(p["out"], 1)
            s.clear()


def bitlinear_host(i):
    A = lambda k: np.asarray(i["L1_ffn_w_" + k])
    return {"gate": A("gate").T, "up": A("up").T, "down": A("down").T.reshape(FC, P, D).transpose(1, 0, 2).reshape(P, FC * D)}


WEIGHTS = {"mb": mamba_host, "xa": xattn_host, "ex": experts_host, "tj": trajectory_host, "de": decoder_host, "bl": bitlinear_host}


def build(nc, a, out):
    of = lambda pre: {k[len(pre) + 1:]: v for k, v in a.items() if k.startswith(pre + "_")}
    with ExitStack() as st:
        consts = {"ident": st.enter_context(nc.sbuf_tensor("ident", [P, P], F32)),
                  "hmask": st.enter_context(nc.sbuf_tensor("hmask", [P, H], F32)),
                  "half_neg": st.enter_context(nc.sbuf_tensor("minus_half", [P, GB], F32))}
        stream = [nc.dram_tensor(f"stream{k}", [BATCH * SEQ, D], F32).ap() for k in range(5)]
        loaded = st.enter_context(nc.semaphore("consts_loaded"))
        with nc.Block() as block:
            @block.sync
            def _(sp):
                sp.dma_start(consts["ident"][:], a["ident"]).then_inc(loaded, 16)
                sp.dma_start(consts["hmask"][:], a["hmask"]).then_inc(loaded, 16)
                sp.dma_start(stream[0], a["x"]).then_inc(loaded, 16)
                sp.wait_ge(loaded, 48)

            @block.vector
            def _(dve):
                nc.vector.memset(consts["half_neg"][:], -0.5)
        mamba_stage(nc, of("mb"), consts, stream[0])
        xattn_stage(nc, of("xa"), consts, a["x"], stream[0], a["ctx"], a["mask"], stream[1])
        experts_stage(nc, of("ex"), consts, stream[1], stream[2])
        trajectory_stage(nc, of("tj"), consts, stream[2], stream[3])
        decoder_stage(nc, of("de"), consts, stream[3], a["ctx"], stream[4])
        bitlinear_stage(nc, of("bl"), consts, stream[4], out)


def kernel(**inputs):
    import concourse.bacc as bacc
    from concourse.bass_utils import run_bass_kernel_spmd

    host = {"x": np.asarray(inputs["x"]).reshape(BATCH * SEQ, D), "ctx": np.asarray(inputs["ctx_1024"]),
            "mask": np.asarray(inputs["mask_Bx1x1xS2_ik0"]).reshape(BATCH, NC),
            "ident": np.eye(P, dtype=np.float32), "hmask": np.repeat(np.eye(H, dtype=np.float32), DK, axis=0)}
    for pre, lay in WEIGHTS.items():
        host.update({f"{pre}_{k}": v for k, v in lay(inputs).items()})
    nc = bacc.Bacc("TRN2", target_bir_lowering=False, num_devices=1)
    arrays, a = {}, {}
    for k, v in host.items():
        arrays["in_" + k] = np.ascontiguousarray(v)
        a[k] = nc.dram_tensor("in_" + k, v.shape, mybir.dt.from_np(v.dtype), kind="ExternalInput").ap()
    out = nc.dram_tensor("out", [BATCH * SEQ, D], F32, kind="ExternalOutput").ap()
    build(nc, a, out)
    r = run_bass_kernel_spmd(nc, [arrays], core_ids=[0])
    return r.results[0]["out"].reshape(BATCH, SEQ, D)
```

```python
from contextlib import ExitStack

import numpy as np
import concourse.bass as bass
from concourse import mybir

F32 = mybir.dt.float32
BF16 = mybir.dt.bfloat16
I32 = mybir.dt.int32
U32 = mybir.dt.uint32
ALU = mybir.AluOpType
ACT = mybir.ActivationFunctionType
AX = mybir.AxisListType

P = 128
BATCH, SEQ, D = 64, 128, 128
GB = 4
TOK = GB * SEQ
GROUPS = BATCH // GB
LN_EPS = 1e-5

NL, DI, DS, DC = 4, 256, 16, 4
DR = D // 16
CH = DI // P
PADT = SEQ + 1
SMALL_Y = 2.0 ** -7
KW = SEQ + DC - 1


def tile_rows(ap, g):
    v = ap.rearrange("(g b t) d -> g t b d", b=GB, t=SEQ)
    return v[bass.ds(g, 1)].rearrange("g t b d -> (g t) b d")


class Sems:

    def __init__(self, nc, stack, names):
        self.nc = nc
        self.by = {n: stack.enter_context(nc.semaphore(n)) for n in names}
        self.runs = []
        for num in sorted(s.num for s in self.by.values()):
            if self.runs and self.runs[-1][1] == num:
                self.runs[-1][1] += 1
            else:
                self.runs.append([num, num + 1])

    def __getitem__(self, name):
        return self.by[name]

    def clear(self):
        for first, end in self.runs:
            self.nc.sync.sem_clear(range(first, end))
        self.nc.all_engine_barrier()


def mamba_stage(nc, w, consts, res):
    ident = consts["ident"]
    with ExitStack() as ctx:
        def sb(name, shape, dt=F32):
            return ctx.enter_context(nc.sbuf_tensor("mb_" + name, shape, dt))

        def pair(name, shape, dt=F32, n=2):
            return [sb(f"{name}{i}", shape, dt) for i in range(n)]

        bank = ctx.enter_context(nc.psum_tensor("mb_bank", [P, 8, 512], F32))
        w_in = sb("w_in", [P, 2 * DI])
        conv_row = sb("conv_row", [P, DC, DI])
        w_conv = sb("w_conv", [P, DC, DI])
        w_x = sb("w_x", [P, CH, 2 * DS + DR])
        w_dt = sb("w_dt", [2 * DS + DR, DI])
        w_out = sb("w_out", [P, CH, D])
        vec = sb("vec", [P, 2 + 3 * CH + CH * DS])
        a_neg = sb("a_neg", [P, CH * DS])
        conv_bh = sb("conv_bh", [P, CH])
        selcol = sb("selcol", [96, 2 * DS])
        sel = sb("sel", [96, 2 * DS, P], BF16)
        half_neg = sb("half_neg", [P, GB])
        small_at = sb("small_at", [P, 1])
        r_tok = sb("r_tok", [P, GB, D])
        stats = sb("stats", [P, GB, 6])
        mv = sb("mv", [P, GB, 2])
        rstd = sb("rstd", [P, GB])
        xh = sb("xh", [P, GB, D])
        h_ch = sb("h_ch", [P, GB, KW])
        th, zth = sb("th", [P, CH, TOK]), sb("zth", [P, CH, TOK])
        bc_f, bc_r = sb("bc_f", [2 * DS, TOK]), sb("bc_r", [2 * DS, TOK])
        bc_m = sb("bc_m", [2 * DS, TOK], BF16)
        dtr = sb("dtr", [2 * DS + DR, TOK])
        ab, ey, ey3, ln1, poly, small, relu = (sb(n, [P, CH, TOK]) for n in ("ab", "ey", "ey3", "ln1", "poly", "small", "relu"))
        bc_s = pair("bc_s", [96, TOK], BF16)
        dt, dtu, u2, zg = (pair(n, [P, CH, TOK]) for n in ("dt", "dtu", "u2", "zg"))
        dA, dBu = (pair(n, [P, CH * GB, PADT], n=3) for n in ("dA", "dBu"))
        hs = pair("hs", [P, CH * GB, PADT])
        b_sb = pair("b_sb", [P, TOK], n=3)
        hc = pair("hc", [P, CH, TOK])
        yv, yg, r_post = sb("yv", [P, CH, TOK]), sb("yg", [P, CH, TOK]), sb("r_post", [P, GB, D])

        NW, NB, CB, DB, DD, AL = 0, 1, 2, 2 + CH, 2 + 2 * CH, 2 + 3 * CH
        B_TR, B_X, B_Z, B_DT, B_OUT, B_B, B_C, B_Y = 0, 0, 2, 1, 3, 4, 5, 6

        s0 = Sems(nc, ctx, ["mbc_sel"])
        with nc.Block() as block:
            @block.sync
            def _(sp):
                sp.dma_start(selcol[:], w["selcol"]).then_inc(s0["mbc_sel"], 16)

            @block.vector
            def _(dve):
                nc.vector.memset(half_neg[:], -0.5)
                nc.vector.memset(small_at[:], SMALL_Y)
                nc.vector.memset(h_ch[:], 0.0)
                for i in range(3):
                    nc.vector.memset(dA[i][:], 0.0)
                    nc.vector.memset(dBu[i][:], 0.0)
                nc.vector.memset(bank[:, B_Y:B_Y + 2], 0.0)
                nc.vector.memset(u2[1][:], 0.0)
                nc.vector.memset(zg[1][:], 0.0)
                dve.wait_ge(s0["mbc_sel"], 16)
                nc.vector.tensor_copy(sel[:], selcol[:].unsqueeze(2).to_broadcast([96, 2 * DS, P]))
        s0.clear()

        sw = Sems(nc, ctx, ["mbw_dma", "mbw_a"])
        s = Sems(nc, ctx, ["mb_" + n for n in [
            "res", "var", "rstd", "xh", "tr", "h", "conv", "z", "th", "th1", "zth", "u", "zg", "xp", "hi", "bcf", "r1",
            "mid", "lo", "dtr", "dtp", "abs", "relu", "ey", "ln", "dt", "dtu",
            "bps", "cps", "bsb", "dbu", "da", "scan", "hc", "sum", "yv", "yg", "rp", "out", "new", "store"]])

        class Ahead:
            def __init__(self, q):
                self.q = q

            def load(self, sp, g):
                sp.dma_start(r_tok[:], tile_rows(res, g)).then_inc(s["mb_res"], 16)

            def dve(self, dve, n):
                q = self.q
                if n == 0:
                    dve.wait_ge(s["mb_res"], 16)
                    for b in range(GB):
                        nc.vector.bn_stats(stats[:, b], r_tok[:, b])
                    dve.drain()
                    for b in range(GB):
                        nc.vector.bn_aggr(mv[:, b], stats[:, b])
                    dve.drain()
                    nc.vector.tensor_scalar(mv[:, :, 1], mv[:, :, 1], LN_EPS, None, ALU.add).then_inc(s["mb_var"], 1)
                if n == 1:
                    dve.wait_ge(s["mb_rstd"], 1)
                    for b in range(GB):
                        m = nc.vector.tensor_scalar(xh[:, b], r_tok[:, b], mv[:, b, 0:1], rstd[:, b:b + 1],
                                                    ALU.subtract, ALU.mult)
                    m.then_inc(s["mb_xh"], 1)
                if n in (5, 6):
                    c = n - 5
                    dve.wait_ge(s["mb_th1"], c + 1)
                    nc.vector.scalar_tensor_tensor(out=u2[q][:, c], in0=bank[:, B_X + c], scalar=vec[:, CB + c:CB + c + 1],
                                                   in1=th[:, c], op0=ALU.add, op1=ALU.mult).then_inc(s["mb_u"], 1)
                if n == 7:
                    for c in range(CH):
                        dve.wait_ge(s["mb_zth"], c + 1)
                        nc.vector.scalar_tensor_tensor(out=zg[q][:, c], in0=zth[:, c], scalar=1.0, in1=bank[:, B_Z + c],
                                                       op0=ALU.add, op1=ALU.mult).then_inc(s["mb_zg"], 1)
                if n == 11:
                    dve.wait_ge(s["mb_ey"], 1)
                    nc.vector.scalar_tensor_tensor(out=poly[:], in0=ey[:], scalar=-1.5, in1=ey[:], op0=ALU.add, op1=ALU.mult)
                    dve.drain()
                    dve.wait_ge(s["mb_ey"], 2)
                    nc.vector.scalar_tensor_tensor(out=poly[:], in0=poly[:], scalar=3.0, in1=ey3[:], op0=ALU.add, op1=ALU.mult)
                if n == 12:
                    dve.drain()
                    dve.wait_ge(s["mb_ln"], 2)
                    nc.vector.copy_predicated(ln1[:], small[:].bitcast(I32), poly[:])
                    dve.drain()
                    dve.wait_ge(s["mb_relu"], CH)
                    nc.vector.tensor_tensor(dt[q][:], ln1[:], relu[:], ALU.add).then_inc(s["mb_dt"], 1)

            def pool(self, pool, n):
                q = self.q
                if n == 0:
                    pool.wait_ge(s["mb_var"], 1)
                    nc.gpsimd.tensor_tensor(rstd[:], mv[:, :, 1], half_neg[:], ALU.pow).then_inc(s["mb_rstd"], 1)
                if n in (4, 5):
                    c = n - 4
                    pool.wait_ge(s["mb_th"], c + 1)
                    nc.gpsimd.tensor_scalar(th[:, c], th[:, c], 1.0, 1.0, ALU.mult, ALU.add).then_inc(s["mb_th1"], 1)
                if n == 9:
                    pool.wait_ge(s["mb_bcf"], 1)
                    pool.wait_ge(s["mb_hi"], 1)
                    nc.gpsimd.tensor_tensor(bc_r[:], bc_f[:], bc_s[q][0:32, :], ALU.subtract).then_inc(s["mb_r1"], 1)
                if n == 10:
                    pool.wait_ge(s["mb_mid"], 2)
                    nc.gpsimd.tensor_tensor(bc_f[:], bc_r[:], bc_m[:], ALU.subtract).then_inc(s["mb_lo"], 1)
                if n == 13:
                    pool.wait_ge(s["mb_dt"], 1)
                    nc.gpsimd.tensor_tensor(dtu[q][:], dt[q][:], u2[q][:], ALU.mult).then_inc(s["mb_dtu"], 1)

            def act(self, act, n):
                q = self.q
                if n == 2:
                    act.wait_ge(s["mb_tr"], 1)
                    nc.scalar.activation(h_ch[:, :, DC - 1:], bank[:, B_TR].rearrange("p (b t) -> p b t", b=GB),
                                         ACT.Identity, bias=vec[:, NB:NB + 1], scale=vec[:, NW:NW + 1]).then_inc(s["mb_h"], 1)
                if n in (4, 5):
                    c = n - 4
                    act.wait_ge(s["mb_conv"], c + 1)
                    nc.scalar.activation(th[:, c], bank[:, B_X + c], ACT.Tanh, bias=conv_bh[:, c:c + 1],
                                         scale=0.5).then_inc(s["mb_th"], 1)
                if n == 6:
                    for c in range(CH):
                        act.wait_ge(s["mb_z"], c + 1)
                        nc.scalar.activation(zth[:, c], bank[:, B_Z + c], ACT.Tanh, scale=0.5).then_inc(s["mb_zth"], 1)
                if n == 8:
                    act.wait_ge(s["mb_xp"], 1)
                    nc.scalar.activation(bc_f[:], bank[0:32, B_TR], ACT.Copy).then_inc(s["mb_bcf"], 1)
                    nc.scalar.activation(bc_s[q][0:32, :], bank[0:32, B_TR], ACT.Copy).then_inc(s["mb_hi"], 1)
                    nc.scalar.activation(dtr[32:40, :], bank[32:40, B_TR], ACT.Copy).then_inc(s["mb_dtr"], 1)
                if n == 9:
                    for c in range(CH):
                        act.wait_ge(s["mb_dtp"], c + 1)
                        bias = vec[:, DB + c:DB + c + 1]
                        nc.scalar.activation(ab[:, c], bank[:, B_DT + c], ACT.Abs, bias=bias).then_inc(s["mb_abs"], 1)
                        nc.scalar.activation(relu[:, c], bank[:, B_DT + c], ACT.Relu, bias=bias).then_inc(s["mb_relu"], 1)
                if n == 10:
                    act.wait_ge(s["mb_r1"], 1)
                    nc.scalar.activation(bc_m[:], bc_r[:], ACT.Copy).then_inc(s["mb_mid"], 1)
                    nc.scalar.activation(bc_s[q][32:64, :], bc_r[:], ACT.Copy).then_inc(s["mb_mid"], 1)
                    act.wait_ge(s["mb_abs"], CH)
                    nc.scalar.activation(ey[:], ab[:], ACT.Exp, scale=-1.0).then_inc(s["mb_ey"], 1)
                if n == 11:
                    act.wait_ge(s["mb_ey"], 1)
                    nc.scalar.activation(ey3[:], ey[:], ACT.Copy, scale=1.0 / 3).then_inc(s["mb_ey"], 1)
                    nc.scalar.activation(ln1[:], ey[:], ACT.Ln, bias=1.0).then_inc(s["mb_ln"], 1)
                    nc.scalar.activation(small[:], ey[:], ACT.Relu, scale=-1.0, bias=small_at[:, 0:1]).then_inc(s["mb_ln"], 1)
                if n == 12:
                    act.wait_ge(s["mb_lo"], 1)
                    nc.scalar.activation(bc_s[q][64:96, :], bc_f[:], ACT.Copy)

            def pe(self, pe, n, after_out=True):
                if n == 1:
                    pe.wait_ge(s["mb_xh"], 1)
                    for b in range(GB):
                        m = nc.tensor.transpose(bank[:, B_TR, b * SEQ:(b + 1) * SEQ], xh[:, b], ident[:])
                    m.then_inc(s["mb_tr"], 1)
                if n in (3, 4):
                    c = n - 3
                    pe.wait_ge(s["mb_h"], 1)
                    for k in range(DC):
                        m = nc.tensor.matmul(bank[:, B_X + c], w_conv[:, k, c * P:(c + 1) * P],
                                             h_ch[:, :, k:k + SEQ], start=(k == 0), stop=(k == DC - 1))
                    m.then_inc(s["mb_conv"], 1)
                if n == 5:
                    if after_out:
                        pe.wait_ge(s["mb_new"], 1)
                    for c in range(CH):
                        nc.tensor.matmul(bank[:, B_Z + c], w_in[:, DI + c * P:DI + (c + 1) * P],
                                         h_ch[:, :, DC - 1:], start=True, stop=True).then_inc(s["mb_z"], 1)
                if n == 7:
                    pe.wait_ge(s["mb_u"], CH)
                    for c in range(CH):
                        m = nc.tensor.matmul(bank[0:2 * DS + DR, B_TR], w_x[:, c], u2[self.q][:, c], start=(c == 0), stop=(c == CH - 1))
                    m.then_inc(s["mb_xp"], 1)
                if n == 8:
                    pe.wait_ge(s["mb_dtr"], 1)
                    pe.wait_ge(s["mb_zg"], 1)
                    for c in range(CH):
                        nc.tensor.matmul(bank[:, B_DT + c], w_dt[32:40, c * P:(c + 1) * P], dtr[32:40, :],
                                         start=True, stop=True).then_inc(s["mb_dtp"], 1)

        class Behind:
            def __init__(self, q):
                self.q = q

            def dve(self, dve, n):
                if n == -1:
                    for c in range(CH):
                        nc.vector.scalar_tensor_tensor(out=yv[:, c], in0=u2[self.q][:, c], scalar=vec[:, DD + c:DD + c + 1],
                                                       in1=bank[:, B_Y + c], op0=ALU.mult, op1=ALU.add).then_inc(s["mb_yv"], 1)
                    dve.wait_ge(s["mb_yv"], CH)
                    nc.vector.tensor_tensor(yg[:], yv[:], zg[self.q][:], ALU.mult).then_inc(s["mb_yg"], 1)
                if n == 2:
                    dve.wait_ge(s["mb_out"], 1)
                    dve.wait_ge(s["mb_rp"], 16)
                    nc.vector.tensor_tensor(r_post[:], r_post[:], bank[:, B_OUT].rearrange("p (b d) -> p b d", b=GB),
                                            ALU.add).then_inc(s["mb_new"], 1)

            def pe(self, pe, n):
                if n == 0:
                    pe.wait_ge(s["mb_yg"], 1)
                    for b in range(GB):
                        for c in range(CH):
                            m = nc.tensor.matmul(bank[:, B_OUT, b * D:(b + 1) * D], yg[:, c, b * SEQ:(b + 1) * SEQ],
                                                 w_out[:, c], start=(c == 0), stop=(c == CH - 1))
                    m.then_inc(s["mb_out"], 1)

            def store(self, sp, g):
                sp.dma_start(r_post[:], tile_rows(res, g)).then_inc(s["mb_rp"], 16)
                sp.wait_ge(s["mb_new"], 1)
                sp.dma_start(tile_rows(res, g), r_post[:]).then_inc(s["mb_store"], 16)
                sp.wait_ge(s["mb_store"], 16)

        class Scan:
            def __init__(self, q):
                self.q = q

            def pool(self, pool, m):
                i = m % 3
                pool.wait_ge(s["mb_bsb"], m + 1)
                if m >= 3:
                    pool.wait_ge(s["mb_scan"], m - 2)
                nc.gpsimd.tensor_tensor(
                    dBu[i][:, :, 1:].rearrange("p (c b) t -> p c b t", c=CH),
                    dtu[self.q][:].rearrange("p c (b t) -> p c b t", b=GB),
                    b_sb[i][:].rearrange("p (b t) -> p b t", b=GB).unsqueeze(1).to_broadcast([P, CH, GB, SEQ]),
                    ALU.mult).then_inc(s["mb_dbu"], 1)

            def act(self, act, m):
                i = m % 3
                act.wait_ge(s["mb_bps"], m + 1)
                if m >= 3:
                    act.wait_ge(s["mb_dbu"], m - 2)
                nc.scalar.activation(b_sb[i][:], bank[:, B_B], ACT.Copy).then_inc(s["mb_bsb"], 1)
                if m >= 3:
                    act.wait_ge(s["mb_scan"], m - 2)
                for c in range(CH):
                    k = c * DS + m
                    nc.scalar.activation(dA[i][:, c * GB:(c + 1) * GB, 1:],
                                         dt[self.q][:, c].rearrange("p (b t) -> p b t", b=GB), ACT.Exp,
                                         scale=a_neg[:, k:k + 1]).then_inc(s["mb_da"], 1)

            def scan(self, dve, m):
                i = m % 3
                dve.wait_ge(s["mb_da"], CH * (m + 1))
                dve.wait_ge(s["mb_dbu"], m + 1)
                if m >= 2:
                    dve.wait_ge(s["mb_hc"], m - 1)
                nc.vector.tensor_tensor_scan(hs[m % 2][:].rearrange("p c t -> p (c t)"), dA[i][:].rearrange("p c t -> p (c t)"),
                                             dBu[i][:].rearrange("p c t -> p (c t)"), 0.0, ALU.mult, ALU.add).then_inc(s["mb_scan"], 1)

            def read_out(self, dve, n):
                i = n % 2
                dve.wait_ge(s["mb_scan"], n + 1)
                dve.wait_ge(s["mb_cps"], n + 1)
                if n >= 2:
                    dve.wait_ge(s["mb_sum"], n - 1)
                nc.vector.tensor_tensor(
                    hc[i][:].rearrange("p c (b t) -> p c b t", b=GB),
                    hs[i][:, :, 1:].rearrange("p (c b) t -> p c b t", c=CH),
                    bank[:, B_C].rearrange("p (b t) -> p b t", b=GB).unsqueeze(1).to_broadcast([P, CH, GB, SEQ]),
                    ALU.mult).then_inc(s["mb_hc"], 1)

            def spread_b(self, pe, m):
                if m:
                    pe.wait_ge(s["mb_bsb"], m)
                nc.tensor.matmul(bank[:, B_B], sel[:, m], bc_s[self.q][:], start=True, stop=True).then_inc(s["mb_bps"], 1)

            def spread_c(self, pe, m):
                if m:
                    pe.wait_ge(s["mb_hc"], m)
                nc.tensor.matmul(bank[:, B_C], sel[:, DS + m], bc_s[self.q][:], start=True, stop=True).then_inc(s["mb_cps"], 1)

            def sum(self, pe, n):
                pe.wait_ge(s["mb_hc"], n + 1)
                if n == 0:
                    pe.wait_ge(s["mb_yv"], CH)
                for c in range(CH):
                    m = nc.tensor.matmul(bank[:, B_Y + c], ident[:], hc[n % 2][:, c], start=(n == 0), stop=(n == DS - 1))
                m.then_inc(s["mb_sum"], 1)

        with nc.Fori(0, NL) as layer:
            with nc.Block() as block:
                @block.sync
                def _(sp):
                    def load(dst, src):
                        sp.dma_start(dst, src).then_inc(sw["mbw_dma"], 16)
                    load(w_in[:], w["w_in"][bass.ds(layer, 1)].rearrange("l p e -> (l p) e"))
                    load(conv_row[:].rearrange("p k e -> p (k e)"),
                         w["conv_row"][bass.ds(layer, 1)].rearrange("l k e -> l (k e)").to_broadcast([P, DC * DI]))
                    load(w_x[:], w["w_x"][bass.ds(layer, 1)].rearrange("l p c m -> (l p) c m"))
                    load(w_dt[2 * DS:2 * DS + DR, :], w["w_dt"][bass.ds(layer, 1)].rearrange("l r e -> (l r) e"))
                    load(w_out[:], w["w_out"][bass.ds(layer, 1)].rearrange("l p c e -> (l p) c e"))
                    load(vec[:], w["vec"][bass.ds(layer, 1)].rearrange("l p v -> (l p) v"))

                @block.scalar
                def _(act):
                    act.wait_ge(sw["mbw_dma"], 6 * 16)
                    nc.scalar.activation(a_neg[:], vec[:, AL:AL + CH * DS], ACT.Exp).then_inc(sw["mbw_a"], 1)

                @block.vector
                def _(dve):
                    dve.wait_ge(sw["mbw_dma"], 6 * 16)
                    for k in range(DC):
                        nc.vector.tensor_tensor(w_conv[:, k, :], w_in[:, 0:DI], conv_row[:, k, :], ALU.mult)
                    nc.vector.tensor_scalar(conv_bh[:], vec[:, CB:CB + CH], 0.5, None, ALU.mult)
                    nc.vector.tensor_scalar(w_x[:], w_x[:], 0.5, None, ALU.mult)
                    nc.vector.tensor_scalar(w_out[:], w_out[:], 0.25, None, ALU.mult)
                    dve.wait_ge(sw["mbw_a"], 1)
                    nc.vector.tensor_scalar(a_neg[:], a_neg[:], -1.0, None, ALU.mult)
            sw.clear()

            first = Ahead(0)
            with nc.Block() as block:
                @block.sync
                def _(sp):
                    first.load(sp, 1)

                @block.gpsimd
                def _(pool):
                    for n in range(DS):
                        first.pool(pool, n)

                @block.scalar
                def _(act):
                    for n in range(DS):
                        first.act(act, n)

                @block.vector
                def _(dve):
                    for n in range(DS):
                        first.dve(dve, n)

                @block.tensor
                def _(pe):
                    for n in range(DS):
                        first.pe(pe, n, after_out=False)
            s.clear()

            with nc.Fori(0, GROUPS // 2) as pairs:
                for q in range(2):
                    ahead, scan, behind = Ahead(1 - q), Scan(q), Behind(1 - q)
                    with nc.Block() as block:
                        @block.sync
                        def _(sp):
                            ahead.load(sp, 2 * pairs + q + 2)
                            behind.store(sp, 2 * pairs + q)

                        @block.gpsimd
                        def _(pool):
                            scan.pool(pool, 0)
                            scan.pool(pool, 1)
                            for n in range(DS):
                                if n + 2 < DS:
                                    scan.pool(pool, n + 2)
                                ahead.pool(pool, n)

                        @block.scalar
                        def _(act):
                            scan.act(act, 0)
                            scan.act(act, 1)
                            for n in range(DS):
                                if n + 2 < DS:
                                    scan.act(act, n + 2)
                                ahead.act(act, n)

                        @block.vector
                        def _(dve):
                            behind.dve(dve, -1)
                            scan.scan(dve, 0)
                            for n in range(DS):
                                if n + 1 < DS:
                                    scan.scan(dve, n + 1)
                                scan.read_out(dve, n)
                                behind.dve(dve, n)
                                ahead.dve(dve, n)

                        @block.tensor
                        def _(pe):
                            scan.spread_b(pe, 0)
                            scan.spread_c(pe, 0)
                            scan.spread_b(pe, 1)
                            for n in range(DS):
                                if n + 2 < DS:
                                    scan.spread_b(pe, n + 2)
                                if n + 1 < DS:
                                    scan.spread_c(pe, n + 1)
                                scan.sum(pe, n)
                                behind.pe(pe, n)
                                ahead.pe(pe, n)
                    s.clear()

            last = Behind(1)
            with nc.Block() as block:
                @block.sync
                def _(sp):
                    last.store(sp, GROUPS)

                @block.vector
                def _(dve):
                    last.dve(dve, -1)
                    last.dve(dve, 2)

                @block.tensor
                def _(pe):
                    last.pe(pe, 0)
            s.clear()


def mamba_host(i):
    A = lambda k: np.asarray(i["L0_attn_" + k])
    xp = A("x_proj_w")
    xp = np.concatenate([xp[:, DR:], xp[:, :DR]], axis=1)
    ch = lambda a: a.reshape(NL, CH, P).transpose(0, 2, 1)
    vec = np.concatenate([
        A("norm_w")[:, :, None], A("norm_b")[:, :, None], ch(A("conv_b")), ch(A("dt_proj_b")), ch(A("D")),
        A("A_log").reshape(NL, CH, P, DS).transpose(0, 2, 1, 3).reshape(NL, P, CH * DS)], axis=2)
    return {
        "w_in": A("in_proj_w").transpose(0, 2, 1),
        "conv_row": A("conv_w").transpose(0, 2, 1),
        "w_x": xp.reshape(NL, 2 * DS + DR, CH, P).transpose(0, 3, 2, 1),
        "w_dt": A("dt_proj_w").transpose(0, 2, 1),
        "w_out": A("out_proj_w").reshape(NL, D, CH, P).transpose(0, 3, 2, 1),
        "vec": vec,
        "selcol": np.tile(np.eye(2 * DS, dtype=np.float32), (3, 1)),
    }

H, DK = 16, 8
NC = 77
HH = H // 2
VW = DK + 1
TOPK = 5
PAD = 4
LOW, PICKED = -3.0e38, -2.0e38
BIG = -1.0e9


class Prefixed:

    def __init__(self, s, prefix):
        self.s, self.prefix, self.nc = s, prefix, s.nc

    def __getitem__(self, name):
        return self.s[self.prefix + name]


class Norm:

    def __init__(self, sb, s, pre, half_neg):
        self.s, self.var, self.rst, self.half_neg = s, pre + "_var", pre + "_rstd", half_neg
        self.stats = sb(pre + "_stats", [P, GB, 6])
        self.mv = sb(pre + "_mv", [P, GB, 2])
        self.rstd = sb(pre + "_rs", [P, GB])
        self.on_dve = self.on_pool = 0

    def dve(self, dve, src, dst):
        nc = self.s.nc
        for b in range(GB):
            nc.vector.bn_stats(self.stats[:, b], src[:, b])
        dve.drain()
        for b in range(GB):
            nc.vector.bn_aggr(self.mv[:, b], self.stats[:, b])
        dve.drain()
        nc.vector.tensor_scalar(self.mv[:, :, 1], self.mv[:, :, 1], LN_EPS, None, ALU.add).then_inc(self.s[self.var], 1)
        self.on_dve += 1
        dve.wait_ge(self.s[self.rst], self.on_dve)
        for b in range(GB):
            last = nc.vector.tensor_scalar(dst[:, b], src[:, b], self.mv[:, b, 0:1], self.rstd[:, b:b + 1],
                                           ALU.subtract, ALU.mult)
        return last

    def pool(self, pool):
        self.on_pool += 1
        pool.wait_ge(self.s[self.var], self.on_pool)
        self.s.nc.gpsimd.tensor_tensor(self.rstd[:], self.mv[:, :, 1], self.half_neg[:], ALU.pow).then_inc(self.s[self.rst], 1)


ATTN_SEMS = ["km", "vx", "score", "shift", "exp", "tr", "pta", "ptv", "pv", "o", "otp", "ot", "proj",
             "cp", "mx", "mr", "pick"]


class Attention:

    UNITS = 2 * GB

    def __init__(self, nc, sb, s, pre, bank, ident, hmask, nk, scale, topk=False, bias=None):
        self.nc, self.s, self.bank, self.ident, self.hmask = nc, s, bank, ident, hmask
        self.nk, self.scale, self.topk, self.bias, self.pre = nk, scale, topk, bias, pre
        self.km = [sb(f"{pre}_km{i}", [P, H, nk]) for i in range(2)]
        self.e = [sb(f"{pre}_e{i}", [P, HH, nk]) for i in range(2)]
        self.mx = sb(pre + "_mx", [P, 2, HH])
        self.pt = sb(pre + "_pt", [nk, HH, P])
        self.rs = sb(pre + "_rs", [P, H])
        self.o = sb(pre + "_o", [P, 2, D])
        self.ot = sb(pre + "_ot", [P, 2, D])
        if topk:
            self.sp = [sb(f"{pre}_sp{i}", [P, HH, nk + PAD]) for i in range(2)]
            self.mr = sb(pre + "_mr", [P, HH, nk + PAD])
            self.m8 = sb(pre + "_m8", [P, 2, HH, 8])
            self.nb = sb(pre + "_nb", [P, 2, HH])
            self.m5 = sb(pre + "_m5", [P, HH, 8])

    def sem(self, name):
        return self.s[self.pre + "_" + name]

    def scores_at(self, u, j):
        return self.bank[:, 2 * (u % 2) + j, 0:4 * self.nk].rearrange("p (h k) -> p h k", h=4)

    def scores_of(self, u):
        return self.bank[:, 2 * (u % 2):2 * (u % 2) + 2, 0:4 * self.nk].rearrange("p j (h k) -> p j h k", h=4)

    def pool(self, pool, kT):
        nk = self.nk
        for b in range(GB):
            if b >= 2:
                pool.wait_ge(self.sem("score"), 2 * (b - 1))
            self.nc.gpsimd.tensor_tensor(self.km[b % 2][:], kT(b).unsqueeze(1).to_broadcast([P, H, nk]),
                                         self.hmask[:].unsqueeze(2).to_broadcast([P, H, nk]), ALU.mult).then_inc(self.sem("km"), 1)

    def pe(self, pe, qT, vx, w_o):
        nc, nk = self.nc, self.nk

        def scores(u):
            b, hf = divmod(u, 2)
            pe.wait_ge(self.sem("km"), b + 1)
            if u >= 2:
                pe.wait_ge(self.sem("cp" if self.topk else "shift"), u - 1)
            for j in range(2):
                h0 = hf * HH + 4 * j
                m = nc.tensor.matmul(self.scores_at(u, j), qT(b), self.km[b % 2][:, h0:h0 + 4, :],
                                     start=True, stop=self.bias is None)
                if self.bias is not None:
                    ones3, parts = self.bias
                    m = nc.tensor.matmul(self.scores_at(u, j), ones3[:], parts(b).unsqueeze(1).to_broadcast([3, 4, nk]),
                                         start=False, stop=True)
            m.then_inc(self.sem("score"), 1)

        def project(b):
            pe.wait_ge(self.sem("o"), b + 1)
            nc.tensor.transpose(self.bank[:, 7, 0:P], self.o[:, b % 2], self.ident[:]).then_inc(self.sem("otp"), 1)
            pe.wait_ge(self.sem("ot"), b + 1)
            nc.tensor.matmul(self.bank[:, 7, P:2 * P], self.ot[:, b % 2], w_o[:], start=True, stop=True).then_inc(self.sem("proj"), 1)

        scores(0)
        scores(1)
        for u in range(self.UNITS):
            b, hf = divmod(u, 2)
            pe.wait_ge(self.sem("pick" if self.topk else "exp"), u + 1)
            if u:
                pe.wait_ge(self.sem("pta"), u)
                pe.wait_ge(self.sem("ptv"), u)
            for h in range(HH):
                m = nc.tensor.transpose(self.bank[0:nk, 4 + h // 4, (h % 4) * P:(h % 4 + 1) * P], self.e[u % 2][:, h], self.ident[:])
            m.then_inc(self.sem("tr"), 1)
            if u + 2 < self.UNITS:
                scores(u + 2)
            if hf == 0 and b >= 1:
                project(b - 1)
            pe.wait_ge(self.sem("pta"), u + 1)
            pe.wait_ge(self.sem("ptv"), u + 1)
            if hf == 0 and b >= 1:
                pe.wait_ge(self.sem("o"), b)
            for h in range(HH):
                at = (hf * HH + h) * VW
                m = nc.tensor.matmul(self.bank[:, 6, at:at + VW], self.pt[:, h], vx(b, hf * HH + h), start=True, stop=True)
            m.then_inc(self.sem("pv"), 1)
        project(GB - 1)

    def act(self, act):
        nc, nk = self.nc, self.nk

        def evac(u):
            act.wait_ge(self.sem("tr"), u + 1)
            if u:
                act.wait_ge(self.sem("pv"), u)
            nc.scalar.activation(self.pt[:, 0:4].rearrange("p h q -> p (h q)"), self.bank[0:nk, 4], ACT.Copy).then_inc(self.sem("pta"), 1)

        def turned(b):
            act.wait_ge(self.sem("otp"), b + 1)
            nc.scalar.activation(self.ot[:, b % 2], self.bank[:, 7, 0:P], ACT.Copy).then_inc(self.sem("ot"), 1)

        for u in range(self.UNITS):
            if self.topk:
                act.wait_ge(self.sem("score"), u + 1)
                if u >= 2:
                    act.wait_ge(self.sem("exp"), HH * (u - 1))
                    act.wait_ge(self.sem("mr"), u - 1)
                nc.scalar.activation(self.sp[u % 2][:, :, 0:nk].rearrange("p (j h) k -> p j h k", j=2), self.scores_of(u),
                                     ACT.Copy).then_inc(self.sem("cp"), 1)
                act.wait_ge(self.sem("mx"), u + 1)
                act.wait_ge(self.sem("cp"), u + 1)
                if u >= 2:
                    act.wait_ge(self.sem("tr"), u - 1)
                for h in range(HH):
                    nc.scalar.activation(self.e[u % 2][:, h], self.sp[u % 2][:, h, 0:nk], ACT.Exp, scale=self.scale,
                                         bias=self.nb[:, u % 2, h:h + 1]).then_inc(self.sem("exp"), 1)
            else:
                act.wait_ge(self.sem("shift"), u + 1)
                nc.scalar.activation(self.e[u % 2][:], self.e[u % 2][:], ACT.Exp, scale=self.scale).then_inc(self.sem("exp"), 1)
            if u:
                evac(u - 1)
            if u % 2 == 1 and u > 1:
                turned(u // 2 - 1)
        evac(self.UNITS - 1)
        turned(GB - 1)

    def dve(self, dve, after):
        nc, nk = self.nc, self.nk

        def evac(u):
            dve.wait_ge(self.sem("tr"), u + 1)
            if u:
                dve.wait_ge(self.sem("pv"), u)
            nc.vector.tensor_copy(self.pt[:, 4:8].rearrange("p h q -> p (h q)"), self.bank[0:nk, 5]).then_inc(self.sem("ptv"), 1)

        def normalise(b):
            heads = self.bank[:, 6, 0:H * VW].rearrange("p (h v) -> p h v", v=VW)
            dve.wait_ge(self.sem("pv"), 2 * b + 2)
            nc.vector.reciprocal(self.rs[:], heads[:, :, DK])
            if b >= 2:
                dve.wait_ge(self.sem("otp"), b - 1)
            dve.drain()
            nc.vector.tensor_tensor(self.o[:, b % 2].rearrange("p (h v) -> p h v", v=DK), heads[:, :, 0:DK],
                                    self.rs[:].unsqueeze(2).to_broadcast([P, H, DK]), ALU.mult).then_inc(self.sem("o"), 1)

        def finish(b):
            dve.wait_ge(self.sem("proj"), b + 1)
            after(b, self.bank[:, 7, P:2 * P])

        for u in range(self.UNITS):
            i = u % 2
            if self.topk:
                dve.wait_ge(self.sem("cp"), u + 1)
                for h in range(HH):
                    nc.vector.max(self.m8[:, i, h], self.sp[i][:, h, 0:nk])
                dve.drain()
                if u >= 2:
                    dve.wait_ge(self.sem("exp"), HH * (u - 1))
                nc.vector.tensor_scalar(self.nb[:, i], self.m8[:, i, :, 0], -self.scale, None, ALU.mult).then_inc(self.sem("mx"), 1)
                nc.vector.memset(self.m8[:, i, :, TOPK:], LOW)
                dve.drain()
                for h in range(HH):
                    m = nc.vector.match_replace(self.mr[:, h], self.m8[:, i, h], self.sp[i][:, h], PICKED)
                m.then_inc(self.sem("mr"), 1)
                dve.wait_ge(self.sem("mr"), u + 1)
                dve.wait_ge(self.sem("exp"), HH * (u + 1))
                nc.vector.scalar_tensor_tensor(out=self.e[i][:], in0=self.mr[:, :, 0:nk], scalar=PICKED, in1=self.e[i][:],
                                               op0=ALU.is_equal, op1=ALU.mult).then_inc(self.sem("pick"), 1)
            else:
                dve.wait_ge(self.sem("score"), u + 1)
                nc.vector.tensor_reduce(self.mx[:, i].rearrange("p (j h) -> p j h", j=2), self.scores_of(u), AX.X, ALU.max)
                if u >= 2:
                    dve.wait_ge(self.sem("tr"), u - 1)
                dve.drain()
                nc.vector.tensor_tensor(self.e[i][:].rearrange("p (j h) k -> p j h k", j=2), self.scores_of(u),
                                        self.mx[:, i].rearrange("p (j h) -> p j h", j=2).unsqueeze(3).to_broadcast([P, 2, 4, nk]),
                                        ALU.subtract).then_inc(self.sem("shift"), 1)
            if u:
                evac(u - 1)
            if u % 2 == 0 and u:
                normalise(u // 2 - 1)
            if u % 2 == 1 and u > 1:
                finish(u // 2 - 1)
        evac(self.UNITS - 1)
        normalise(GB - 1)
        finish(GB - 1)


def row(ap, parts):
    return ap.unsqueeze(0).to_broadcast([parts, ap.shape[0]])


def ctx_rows(ap, g):
    v = ap.rearrange("(g b) t d -> g t b d", b=GB)
    return v[bass.ds(g, 1)].rearrange("g t b d -> (g t) b d")


def xattn_stage(nc, w, consts, x_in, res, ctx_in, mask_in, x_out):
    ident, hmask, half_neg = consts["ident"], consts["hmask"], consts["half_neg"]
    with ExitStack() as st:
        def sb(name, shape, dt=F32):
            return st.enter_context(nc.sbuf_tensor("xa_" + name, shape, dt))

        bank = st.enter_context(nc.psum_tensor("xa_bank", [P, 8, 512], F32))
        s = Sems(nc, st, ["xa_" + n for n in ["n_var", "n_rstd", "in", "ctx", "xt", "xts", "ct", "cts", "q", "qs", "k", "ks", "kb",
                                          "mk", "v", "vb", "out", "store"] + ["a_" + n for n in ATTN_SEMS]])

        p = Prefixed(s, "xa_")
        wq, wk, wv, wo = (sb(n, [P, D]) for n in ("wq", "wk", "wv", "wo"))
        vecs = sb("vecs", [P, 2])
        rows = sb("rows", [P, 4, D])
        part = sb("part", [3, 1])
        ones3 = sb("ones3", [3, P], BF16)
        r_tok, x_tok, y_tok, z_tok = (sb(n, [P, GB, D]) for n in ("r_tok", "x_tok", "y_tok", "z_tok"))
        c_tok = sb("c_tok", [NC, GB, D])
        xT, qT = sb("xT", [P, GB, SEQ]), sb("qT", [P, GB, SEQ])
        cT, kT = sb("cT", [P, GB, NC]), sb("kT", [P, GB, NC])
        m_int = sb("m_int", [P, GB, NC], I32)
        keep = sb("keep", [P, GB, NC])
        mbias = sb("mbias", [3, GB, NC], BF16)
        vx = sb("vx", [NC, GB, H, VW])
        norm = Norm(sb, p, "n", half_neg)
        at = Attention(nc, sb, p, "a", bank, ident, hmask, NC, DK ** -0.5, bias=(ones3, lambda b: mbias[:, b]))

        s0 = Sems(nc, st, ["xa0_w"])
        with nc.Block() as block:
            @block.sync
            def _(sp):
                loads = [(wq, w["wq"]), (wk, w["wk"]), (wv, w["wv"]), (wo, w["wo"]), (vecs, w["vecs"]), (part, w["part"])]
                for t, d in loads:
                    sp.dma_start(t[:], d).then_inc(s0["xa0_w"], 16)
                sp.dma_start(rows[:].rearrange("p r d -> p (r d)"), w["rows"].rearrange("r d -> (r d)").unsqueeze(0)
                             .to_broadcast([P, 4 * D])).then_inc(s0["xa0_w"], 16)
                sp.wait_ge(s0["xa0_w"], 16 * (len(loads) + 1))

            @block.vector
            def _(dve):
                nc.vector.memset(ones3[:], 1.0)
                nc.vector.memset(vx[:], 1.0)
        s0.clear()

        with nc.Fori(0, GROUPS) as g:
            norm.on_dve = norm.on_pool = 0
            with nc.Block() as block:
                @block.sync
                def _(sp):
                    sp.dma_start(c_tok[:], ctx_rows(ctx_in, g)).then_inc(p["ctx"], 16)
                    sp.dma_start(m_int[:].rearrange("p b k -> p (b k)"),
                                 mask_in.rearrange("(g b) k -> g (b k)", b=GB)[bass.ds(g, 1)].to_broadcast([P, GB * NC])).then_inc(p["ctx"], 16)
                    sp.dma_start(r_tok[:], tile_rows(res, g)).then_inc(p["in"], 16)
                    sp.dma_start(x_tok[:], tile_rows(x_in, g)).then_inc(p["in"], 16)
                    sp.wait_ge(p["out"], 1)
                    sp.dma_start(tile_rows(x_out, g), y_tok[:]).then_inc(p["store"], 16)
                    sp.wait_ge(p["store"], 16)

                @block.gpsimd
                def _(pool):
                    norm.pool(pool)
                    norm.pool(pool)
                    pool.wait_ge(p["kb"], 1)
                    at.pool(pool, lambda b: kT[:, b])
                    norm.pool(pool)

                @block.tensor
                def _(pe):
                    pe.wait_ge(p["ctx"], 32)
                    for b in range(GB):
                        m = nc.tensor.transpose(bank[:, 0, b * NC:(b + 1) * NC], c_tok[:, b], ident[0:NC, 0:NC])
                    m.then_inc(p["ct"], 1)
                    pe.wait_ge(p["cts"], 1)
                    nc.tensor.matmul(bank[:, 1, 0:GB * NC], wk[:], cT[:], start=True, stop=True).then_inc(p["k"], 1)
                    for b in range(GB):
                        m = nc.tensor.matmul(bank[0:NC, 2, b * D:(b + 1) * D], cT[:, b], wv[:], start=True, stop=True)
                    m.then_inc(p["v"], 1)
                    pe.wait_ge(p["xt"], 1)
                    for b in range(GB):
                        m = nc.tensor.transpose(bank[:, 3, b * P:(b + 1) * P], x_tok[:, b], ident[:])
                    m.then_inc(p["xts"], 1)
                    pe.wait_ge(p["q"], 1)
                    nc.tensor.matmul(bank[:, 4], wq[:], xT[:].rearrange("p b t -> p (b t)"), start=True, stop=True).then_inc(p["q"], 1)
                    pe.wait_ge(p["qs"], 1)
                    pe.wait_ge(p["ks"], 1)
                    pe.wait_ge(p["vb"], 1)
                    pe.wait_ge(p["mk"], 1)
                    at.pe(pe, lambda b: qT[:, b], lambda b, h: vx[:, b, h], wo)

                @block.scalar
                def _(act):
                    act.wait_ge(p["ct"], 1)
                    nc.scalar.activation(cT[:].rearrange("p b k -> p (b k)"), bank[:, 0, 0:GB * NC], ACT.Copy).then_inc(p["cts"], 1)
                    act.wait_ge(p["k"], 1)
                    nc.scalar.activation(kT[:].rearrange("p b k -> p (b k)"), bank[:, 1, 0:GB * NC], ACT.Identity,
                                         bias=vecs[:, 1:2]).then_inc(p["ks"], 1)
                    act.wait_ge(p["xts"], 1)
                    nc.scalar.activation(xT[:].rearrange("p b t -> p (b t)"), bank[:, 3], ACT.Copy).then_inc(p["q"], 1)
                    act.wait_ge(p["q"], 2)
                    nc.scalar.activation(qT[:].rearrange("p b t -> p (b t)"), bank[:, 4], ACT.Identity,
                                         bias=vecs[:, 0:1]).then_inc(p["qs"], 1)
                    at.act(act)

                @block.vector
                def _(dve):
                    dve.wait_ge(p["in"], 32)
                    norm.dve(dve, r_tok, z_tok)
                    dve.drain()
                    nc.vector.tensor_tensor(z_tok[:], z_tok[:], rows[:, 0].unsqueeze(1).to_broadcast([P, GB, D]), ALU.mult)
                    nc.vector.tensor_tensor(r_tok[:], x_tok[:], rows[:, 1].unsqueeze(1).to_broadcast([P, GB, D]), ALU.add)
                    dve.drain()
                    nc.vector.tensor_tensor(z_tok[:], z_tok[:], r_tok[:], ALU.add)
                    dve.drain()
                    norm.dve(dve, z_tok, x_tok).then_inc(p["xt"], 1)
                    dve.wait_ge(p["ctx"], 32)
                    nc.vector.tensor_scalar(keep[:], m_int[:], 0.0, None, ALU.not_equal)
                    dve.drain()
                    nc.vector.tensor_scalar(mbias[:], keep[0:3], 1.0, part[:, 0:1], ALU.subtract, ALU.mult).then_inc(p["mk"], 1)
                    dve.wait_ge(p["ks"], 1)
                    nc.vector.tensor_tensor(kT[:], kT[:], keep[:], ALU.mult).then_inc(p["kb"], 1)
                    dve.wait_ge(p["v"], 1)
                    nc.vector.tensor_tensor(vx[:, :, :, 0:DK], bank[0:NC, 2].rearrange("p (b h v) -> p b h v", b=GB, h=H),
                                            rows[0:NC, 2].rearrange("p (h v) -> p h v", h=H).unsqueeze(1).to_broadcast([NC, GB, H, DK]),
                                            ALU.add).then_inc(p["vb"], 1)
                    nc.vector.tensor_tensor(z_tok[:], x_tok[:], rows[:, 3].unsqueeze(1).to_broadcast([P, GB, D]), ALU.add)
                    dve.drain()

                    def add(b, psum):
                        nc.vector.tensor_tensor(r_tok[:, b], z_tok[:, b], psum, ALU.add)
                    at.dve(dve, add)
                    dve.drain()
                    norm.dve(dve, r_tok, y_tok).then_inc(p["out"], 1)
            s.clear()


def bf16_parts(v, n=3):
    out, rest = [], np.float32(v)
    for _ in range(n):
        bits = np.array([rest], np.float32).view(np.uint32) & np.uint32(0xFFFF0000)
        hi = bits.view(np.float32)[0]
        out.append(hi)
        rest = np.float32(rest - hi)
    return np.array(out, np.float32)


def xattn_host(i):
    A = lambda k: np.asarray(i["L0_xattn_" + k])
    return {"wq": A("wq").T, "wk": A("wk").T, "wv": A("wv").T, "wo": A("wo").T,
            "vecs": np.stack([A("bq"), A("bk")], 1),
            "rows": np.stack([np.asarray(i["L0_attn_normf_w"]), np.asarray(i["L0_attn_normf_b"]), A("bv"), A("bo")]),
            "part": -bf16_parts(BIG)[:, None]}

PH, NK, KD, EXPERTS = 8, 128, 64, 2048
FI = 2 * D
ROW = 2 * D + 2 * FI
IA, IB, OA, OB = 0, D, D + FI, D + 2 * FI


PER_GROUP = 16 * PH * GB // 2


def experts_stage(nc, w, consts, x_in, x_out):
    ident, half_neg = consts["ident"], consts["half_neg"]
    with ExitStack() as st:
        def sb(name, shape, dt=F32):
            return st.enter_context(nc.sbuf_tensor("ex_" + name, shape, dt))

        bank = st.enter_context(nc.psum_tensor("ex_bank", [P, 8, 512], F32))
        s = Sems(nc, st, ["ex_" + n for n in [
            "n_var", "n_rstd", "in", "xt", "xts", "sim", "top", "idx", "lin", "dgi", "hid", "gelu", "ht",
            "hts", "lout", "dgo", "y", "sum", "out", "store"]])
        p = Prefixed(s, "ex_")
        got = [st.enter_context(nc.semaphore(f"ex_got{i}")) for i in range(2)]
        w_sim = sb("w_sim", [P, 2 * PH, NK])
        w_in = sb("w_in", [P, FI])
        w_out = sb("w_out", [P, 2, D])
        x_tok, y_tok = sb("x_tok", [P, GB, D]), sb("y_tok", [P, GB, D])
        xT = sb("xT", [P, GB, SEQ])
        m8 = sb("m8", [P, 2 * PH, 8])
        i8 = sb("i8", [P, 2 * PH, 8], U32)
        iy = sb("iy", [P, PH])
        idx = [sb(f"idx{i}", [P, PH], U32) for i in range(2)]
        gate = [sb(f"gate{i}", [P, PH]) for i in range(2)]
        rowsb = [sb(f"rows{i}", [P, PH, ROW]) for i in range(2)]
        junk = sb("junk", [P, PH, FI])
        lin, lout = sb("lin", [P, PH]), sb("lout", [P, PH])
        dg_in = sb("dg_in", [P, PH, P])
        dg_out = sb("dg_out", [P, PH, P])
        hid = sb("hid", [P, FI])
        hidT = sb("hidT", [P, 2, P])
        norm = Norm(sb, p, "n", half_neg)

        s0 = Sems(nc, st, ["ex0_w", "ex0_m", "ex0_c"])
        wq = sb("wq", [KD, 2 * PH, D])
        keys = sb("keys", [KD, 2 * PH, NK])
        with nc.Block() as block:
            @block.sync
            def _(sp):
                for t, d in ((wq, w["wq"]), (keys, w["keys"]), (w_in, w["w_in"]), (w_out, w["w_out"])):
                    sp.dma_start(t[:], d).then_inc(s0["ex0_w"], 16)

            @block.tensor
            def _(pe):
                pe.wait_ge(s0["ex0_w"], 64)
                for j in range(2 * PH):
                    m = nc.tensor.matmul(bank[:, j // 4, (j % 4) * P:(j % 4 + 1) * P], wq[:, j], keys[:, j], start=True, stop=True)
                m.then_inc(s0["ex0_m"], 1)

            @block.scalar
            def _(act):
                act.wait_ge(s0["ex0_m"], 1)
                nc.scalar.activation(w_sim[:].rearrange("p (a h) k -> p a (h k)", a=4), bank[:, 0:4], ACT.Copy)
        s0.clear()

        with nc.Fori(0, GROUPS) as g:
            norm.on_dve = norm.on_pool = 0
            with nc.Block() as block:
                @block.sync
                def _(sp):
                    sp.dma_start(x_tok[:], tile_rows(x_in, g)).then_inc(p["in"], 16)
                    sp.wait_ge(p["out"], 1)
                    sp.dma_start(tile_rows(x_out, g), y_tok[:]).then_inc(p["store"], 16)
                    sp.wait_ge(p["store"], 16)

                @block.gpsimd
                def _(pool):
                    for b in range(GB):
                        pool.wait_ge(p["idx"], b + 1)
                        if b >= 2:
                            pool.wait_ge(p["y"], b - 1)
                        for h in range(PH):
                            nc.gpsimd.indirect_dma_start(rowsb[b % 2][:, h], None, w["table"],
                                                         bass.IndirectOffsetOnAxis(idx[b % 2][:, h:h + 1], 0)).then_inc(got[b % 2], 16)
                    norm.pool(pool)

                @block.tensor
                def _(pe):
                    pe.wait_ge(p["in"], 16)
                    for b in range(GB):
                        m = nc.tensor.transpose(bank[:, 7, b * P:(b + 1) * P], x_tok[:, b], ident[:])
                    m.then_inc(p["xt"], 1)
                    pe.wait_ge(p["xts"], 1)

                    def sims(b):
                        for j in range(4):
                            if b:
                                pe.wait_ge(p["top"], 4 * (b - 1) + j + 1)
                            nc.tensor.matmul(bank[:, j], xT[:, b], w_sim[:, 4 * j:4 * j + 4], start=True, stop=True).then_inc(p["sim"], 1)

                    sims(0)
                    for b in range(GB):
                        if b + 1 < GB:
                            sims(b + 1)
                        if b:
                            pe.wait_ge(p["gelu"], b)
                        pe.wait_ge(p["dgi"], b + 1)
                        nc.tensor.matmul(bank[:, 4, 0:FI], xT[:, b], w_in[:], start=True, stop=False)
                        for h in range(PH):
                            m = nc.tensor.matmul(bank[:, 4, 0:FI], dg_in[:, h], rowsb[b % 2][:, h, IB:IB + FI], start=False, stop=(h == PH - 1))
                        m.then_inc(p["hid"], 1)
                        pe.wait_ge(p["gelu"], b + 1)
                        for c in range(2):
                            m = nc.tensor.transpose(bank[:, 5, c * P:(c + 1) * P], hid[:, c * P:(c + 1) * P], ident[:])
                        m.then_inc(p["ht"], 1)
                        pe.wait_ge(p["hts"], b + 1)
                        pe.wait_ge(p["dgo"], b + 1)
                        if b:
                            pe.wait_ge(p["sum"], b)
                        for c in range(2):
                            nc.tensor.matmul(bank[:, 6, 0:D], hidT[:, c], w_out[:, c], start=(c == 0), stop=False)
                        for h in range(PH):
                            m = nc.tensor.matmul(bank[:, 6, 0:D], dg_out[:, h], rowsb[b % 2][:, h, OB:OB + D], start=False, stop=(h == PH - 1))
                        m.then_inc(p["y"], 1)

                @block.scalar
                def _(act):
                    act.wait_ge(p["xt"], 1)
                    nc.scalar.activation(xT[:].rearrange("p b t -> p (b t)"), bank[:, 7], ACT.Copy).then_inc(p["xts"], 1)
                    for b in range(GB):
                        act.wait_ge(p["lin"], b + 1)
                        if b:
                            act.wait_ge(p["hid"], b)
                        for h in range(PH):
                            m = nc.scalar.activation(dg_in[:, h], ident[:], ACT.Copy, scale=lin[:, h:h + 1])
                        m.then_inc(p["dgi"], 1)
                        act.wait_ge(p["hid"], b + 1)
                        if b:
                            act.wait_ge(p["ht"], b)
                            act.wait_ge(p["lout"], b)
                        nc.scalar.activation(hid[:], bank[:, 4, 0:FI], ACT.Gelu).then_inc(p["gelu"], 1)
                        act.wait_ge(p["ht"], b + 1)
                        if b:
                            act.wait_ge(p["y"], b)
                        nc.scalar.activation(hidT[:].rearrange("p c t -> p (c t)"), bank[:, 5, 0:2 * P], ACT.Copy).then_inc(p["hts"], 1)
                        act.wait_ge(p["lout"], b + 1)
                        for h in range(PH):
                            m = nc.scalar.activation(dg_out[:, h], ident[:], ACT.Copy, scale=lout[:, h:h + 1])
                        m.then_inc(p["dgo"], 1)

                @block.vector
                def _(dve):
                    def top(b):
                        i = b % 2
                        for j in range(4):
                            dve.wait_ge(p["sim"], 4 * b + j + 1)
                            for k in range(4):
                                nc.vector.max(m8[:, 4 * j + k], bank[:, j, k * NK:(k + 1) * NK])
                            dve.drain()
                            for k in range(4):
                                m = nc.vector.max_index(i8[:, 4 * j + k], m8[:, 4 * j + k], bank[:, j, k * NK:(k + 1) * NK])
                            m.then_inc(p["top"], 1)
                        dve.drain()
                        nc.vector.tensor_tensor(gate[i][:], m8[:, 0:PH, 0], m8[:, PH:, 0], ALU.add)
                        nc.vector.tensor_copy(iy[:], i8[:, PH:, 0])
                        dve.drain()
                        nc.vector.tensor_scalar(gate[i][:], gate[i][:], 0.0, None, ALU.max)
                        nc.vector.scalar_tensor_tensor(out=iy[:], in0=i8[:, 0:PH, 0], scalar=float(NK), in1=iy[:],
                                                       op0=ALU.mult, op1=ALU.add)
                        dve.drain()
                        if b >= 2:
                            dve.wait_ge(got[i], g * PER_GROUP + 16 * PH * (b // 2))
                        nc.vector.tensor_scalar(idx[i][:], iy[:], float(EXPERTS - 1), None, ALU.min).then_inc(p["idx"], 1)

                    top(0)
                    for b in range(GB):
                        i = b % 2
                        if b + 1 < GB:
                            top(b + 1)
                        dve.wait_ge(got[i], g * PER_GROUP + 16 * PH * (b // 2 + 1))
                        if b:
                            dve.wait_ge(p["dgi"], b)
                        nc.vector.tensor_tensor(junk[:, :, 0:D], rowsb[i][:, :, IA:IA + D], x_tok[:, b].unsqueeze(1).to_broadcast([P, PH, D]), ALU.mult)
                        dve.drain()
                        nc.vector.tensor_reduce(lin[:], junk[:, :, 0:D], AX.X, ALU.add)
                        dve.drain()
                        nc.vector.tensor_tensor(lin[:], lin[:], gate[i][:], ALU.mult).then_inc(p["lin"], 1)
                        dve.wait_ge(p["gelu"], b + 1)
                        if b:
                            dve.wait_ge(p["dgo"], b)
                        nc.vector.tensor_tensor(junk[:], rowsb[i][:, :, OA:OA + FI], hid[:].unsqueeze(1).to_broadcast([P, PH, FI]), ALU.mult)
                        dve.drain()
                        nc.vector.tensor_reduce(lout[:], junk[:], AX.X, ALU.add)
                        dve.drain()
                        nc.vector.tensor_tensor(lout[:], lout[:], gate[i][:], ALU.mult).then_inc(p["lout"], 1)
                        dve.wait_ge(p["y"], b + 1)
                        nc.vector.tensor_tensor(y_tok[:, b], x_tok[:, b], bank[:, 6, 0:D], ALU.add).then_inc(p["sum"], 1)
                    dve.drain()
                    norm.dve(dve, y_tok, y_tok).then_inc(p["out"], 1)
            s.clear()


def experts_host(i):
    A = lambda k: np.asarray(i["L0_ffn_" + k])
    return {"wq": A("Wq").reshape(2 * PH, KD, D).transpose(1, 0, 2),
            "keys": A("keys").transpose(3, 2, 0, 1).reshape(KD, 2 * PH, NK),
            "w_in": A("W_in").T, "w_out": A("W_out").T.reshape(2, P, D).transpose(1, 0, 2),
            "table": np.concatenate([A("in_a"), A("in_b"), A("out_a"), A("out_b")], axis=1)}

GN, WIN = 64, 8
GUIDE = 0.4
EPS_MAG, EPS_COS, EPS_WSUM = 1e-6, 1e-8, 1e-8


def trajectory_stage(nc, w, consts, x_in, x_out):
    ident, half_neg = consts["ident"], consts["half_neg"]
    with ExitStack() as st:
        def sb(name, shape, dt=F32):
            return st.enter_context(nc.sbuf_tensor("tj_" + name, shape, dt))

        bank = st.enter_context(nc.psum_tensor("tj_bank", [P, 8, 512], F32))
        s = Sems(nc, st, ["tj_" + n for n in [
            "n_var", "n_rstd", "in", "diff", "ds", "sq", "mag", "nrm", "sq2", "mag2", "mw", "nt", "nts", "sim", "sh",
            "ex", "gw", "gt", "gts", "inf", "cb", "tr", "out", "store"]])
        p = Prefixed(s, "tj_")
        shiftm, band = sb("shiftm", [P, P]), sb("band", [P, P])
        guide = sb("guide", [GN, D])
        gsq = sb("gsq", [GN, D])
        gr = sb("gr", [GN, 1])
        gr2 = sb("gr2", [GN, 1])
        half = sb("half", [P, GB])
        gnT = sb("gnT", [P, GN])
        x_tok, y_tok = sb("x_tok", [P, GB, D]), sb("y_tok", [P, GB, D])
        diff, nrm, sq = sb("diff", [P, GB, D]), sb("nrm", [P, GB, D]), sb("sq", [P, GB, D])
        m2, mag, ok, t4, inv, a2, an, mx, mw, sm = (sb(n, [P, GB]) for n in
                                                    ("m2", "mag", "ok", "t4", "inv", "a2", "an", "mx", "mw", "sm"))
        nT = sb("nT", [P, GB, P])
        sim = sb("sim", [P, GB, GN])
        gwT = sb("gwT", [GN, GB, P])
        cb = sb("cb", [P, GB, D])
        ws = sb("ws", [P, GB])
        norm = Norm(sb, p, "n", half_neg)

        s0 = Sems(nc, st, ["tj0_w", "tj0_a", "tj0_b", "tj0_c", "tj0_d"])
        with nc.Block() as block:
            @block.sync
            def _(sp):
                for t, d in ((shiftm, w["shiftm"]), (band, w["band"]), (guide, w["guide"])):
                    sp.dma_start(t[:], d).then_inc(s0["tj0_w"], 16)

            @block.vector
            def _(dve):
                nc.vector.memset(half[:], 0.5)
                dve.wait_ge(s0["tj0_w"], 48)
                nc.vector.tensor_tensor(gsq[:], guide[:], guide[:], ALU.mult)
                dve.drain()
                nc.vector.tensor_reduce(gr[:], gsq[:], AX.X, ALU.add).then_inc(s0["tj0_a"], 1)
                dve.wait_ge(s0["tj0_b"], 1)
                nc.vector.tensor_scalar(gr2[:], gr2[:], EPS_COS, None, ALU.max)
                dve.drain()
                nc.vector.reciprocal(gr[:], gr2[:])
                dve.drain()
                nc.vector.tensor_scalar(gsq[:], guide[:], gr[:, 0:1], None, ALU.mult).then_inc(s0["tj0_c"], 1)

            @block.gpsimd
            def _(pool):
                pool.wait_ge(s0["tj0_a"], 1)
                nc.gpsimd.tensor_tensor(gr2[:], gr[:], half[0:GN, 0:1], ALU.pow).then_inc(s0["tj0_b"], 1)

            @block.tensor
            def _(pe):
                pe.wait_ge(s0["tj0_c"], 1)
                nc.tensor.transpose(bank[:, 0, 0:GN], gsq[:], ident[0:GN, 0:GN]).then_inc(s0["tj0_d"], 1)

            @block.scalar
            def _(act):
                act.wait_ge(s0["tj0_d"], 1)
                nc.scalar.activation(gnT[:], bank[:, 0, 0:GN], ACT.Copy)
        s0.clear()

        def flat(t):
            return t[:].rearrange("p b d -> p (b d)")

        def wide(t, n=D):
            return t[:].unsqueeze(2).to_broadcast([P, GB, n])

        with nc.Fori(0, GROUPS) as g:
            norm.on_dve = norm.on_pool = 0
            with nc.Block() as block:
                @block.sync
                def _(sp):
                    sp.dma_start(x_tok[:], tile_rows(x_in, g)).then_inc(p["in"], 16)
                    sp.wait_ge(p["out"], 1)
                    sp.dma_start(tile_rows(x_out, g), y_tok[:]).then_inc(p["store"], 16)
                    sp.wait_ge(p["store"], 16)

                @block.gpsimd
                def _(pool):
                    pool.wait_ge(p["sq"], 1)
                    nc.gpsimd.tensor_tensor(mag[:], m2[:], half[:], ALU.pow).then_inc(p["mag"], 1)
                    pool.wait_ge(p["sq2"], 1)
                    nc.gpsimd.tensor_tensor(an[:], a2[:], half[:], ALU.pow).then_inc(p["mag2"], 1)
                    norm.pool(pool)

                @block.tensor
                def _(pe):
                    pe.wait_ge(p["in"], 16)
                    nc.tensor.matmul(bank[:, 0], shiftm[:], flat(x_tok), start=True, stop=True).then_inc(p["diff"], 1)
                    pe.wait_ge(p["nrm"], 1)
                    for b in range(GB):
                        m = nc.tensor.transpose(bank[:, 1, b * P:(b + 1) * P], nrm[:, b], ident[:])
                    m.then_inc(p["nt"], 1)
                    pe.wait_ge(p["nts"], 1)
                    for b in range(GB):
                        m = nc.tensor.matmul(bank[:, 2, b * GN:(b + 1) * GN], nT[:, b], gnT[:], start=True, stop=True)
                    m.then_inc(p["sim"], 1)
                    pe.wait_ge(p["gw"], 1)
                    for b in range(GB):
                        m = nc.tensor.transpose(bank[0:GN, 3, b * P:(b + 1) * P], sim[:, b], ident[:])
                    m.then_inc(p["gt"], 1)
                    pe.wait_ge(p["gts"], 1)
                    for b in range(GB):
                        m = nc.tensor.matmul(bank[:, 4, b * D:(b + 1) * D], gwT[:, b], guide[:], start=True, stop=True)
                    m.then_inc(p["inf"], 1)
                    pe.wait_ge(p["cb"], 1)
                    nc.tensor.matmul(bank[:, 5], band[:], flat(cb), start=True, stop=True)
                    nc.tensor.matmul(bank[:, 6, 0:GB], band[:], mw[:], start=True, stop=True).then_inc(p["tr"], 1)

                @block.scalar
                def _(act):
                    act.wait_ge(p["diff"], 1)
                    nc.scalar.activation(flat(diff), bank[:, 0], ACT.Copy).then_inc(p["ds"], 1)
                    act.wait_ge(p["mag"], 1)
                    nc.scalar.activation(mw[:], mag[:], ACT.Tanh, scale=2.0).then_inc(p["mw"], 1)
                    act.wait_ge(p["nt"], 1)
                    nc.scalar.activation(flat(nT), bank[:, 1], ACT.Copy).then_inc(p["nts"], 1)
                    act.wait_ge(p["sh"], 1)
                    nc.scalar.activation(flat(sim), flat(sim), ACT.Exp, scale=2.0).then_inc(p["ex"], 1)
                    act.wait_ge(p["gt"], 1)
                    nc.scalar.activation(flat(gwT), bank[0:GN, 3], ACT.Copy).then_inc(p["gts"], 1)

                @block.vector
                def _(dve):
                    dve.wait_ge(p["ds"], 1)
                    nc.vector.tensor_tensor(sq[:], diff[:], diff[:], ALU.mult)
                    dve.drain()
                    nc.vector.tensor_reduce(m2[:], sq[:], AX.X, ALU.add).then_inc(p["sq"], 1)
                    dve.wait_ge(p["mag"], 1)
                    nc.vector.tensor_scalar(ok[:], mag[:], EPS_MAG, None, ALU.is_gt)
                    dve.drain()
                    nc.vector.tensor_tensor(t4[:], mag[:], ok[:], ALU.mult)
                    nc.vector.tensor_scalar(inv[:], ok[:], -1.0, 1.0, ALU.mult, ALU.add)
                    dve.drain()
                    nc.vector.tensor_tensor(t4[:], t4[:], inv[:], ALU.add)
                    dve.drain()
                    nc.vector.reciprocal(inv[:], t4[:])
                    dve.drain()
                    nc.vector.tensor_tensor(inv[:], inv[:], ok[:], ALU.mult)
                    dve.drain()
                    nc.vector.tensor_tensor(nrm[:], diff[:], wide(inv), ALU.mult).then_inc(p["nrm"], 1)
                    dve.drain()
                    nc.vector.tensor_tensor(sq[:], nrm[:], nrm[:], ALU.mult)
                    dve.drain()
                    nc.vector.tensor_reduce(a2[:], sq[:], AX.X, ALU.add).then_inc(p["sq2"], 1)
                    dve.wait_ge(p["mag2"], 1)
                    nc.vector.tensor_scalar(an[:], an[:], EPS_COS, None, ALU.max)
                    dve.drain()
                    nc.vector.reciprocal(a2[:], an[:])
                    dve.drain()
                    dve.wait_ge(p["sim"], 1)
                    nc.vector.tensor_tensor(sim[:], bank[:, 2, 0:GB * GN].rearrange("p (b k) -> p b k", b=GB), wide(a2, GN), ALU.mult)
                    dve.drain()
                    nc.vector.tensor_reduce(mx[:], sim[:], AX.X, ALU.max)
                    dve.drain()
                    nc.vector.tensor_tensor(sim[:], sim[:], wide(mx, GN), ALU.subtract).then_inc(p["sh"], 1)
                    dve.wait_ge(p["ex"], 1)
                    nc.vector.tensor_reduce(sm[:], sim[:], AX.X, ALU.add)
                    dve.drain()
                    nc.vector.reciprocal(mx[:], sm[:])
                    dve.drain()
                    nc.vector.tensor_tensor(sim[:], sim[:], wide(mx, GN), ALU.mult).then_inc(p["gw"], 1)
                    nc.vector.tensor_scalar(sq[:], nrm[:], 1.0 - GUIDE, None, ALU.mult)
                    dve.drain()
                    dve.wait_ge(p["inf"], 1)
                    nc.vector.scalar_tensor_tensor(out=flat(sq), in0=bank[:, 4], scalar=GUIDE, in1=flat(sq), op0=ALU.mult, op1=ALU.add)
                    dve.drain()
                    dve.wait_ge(p["mw"], 1)
                    nc.vector.tensor_tensor(cb[:], sq[:], wide(mw), ALU.mult).then_inc(p["cb"], 1)
                    dve.wait_ge(p["tr"], 1)
                    nc.vector.tensor_scalar(ws[:], bank[:, 6, 0:GB], EPS_WSUM, None, ALU.max)
                    dve.drain()
                    nc.vector.reciprocal(sm[:], ws[:])
                    dve.drain()
                    nc.vector.tensor_tensor(cb[:], bank[:, 5].rearrange("p (b d) -> p b d", b=GB), wide(sm), ALU.mult)
                    dve.drain()
                    nc.vector.tensor_tensor(sq[:], cb[:], x_tok[:], ALU.add)
                    dve.drain()
                    norm.dve(dve, sq, y_tok).then_inc(p["out"], 1)
            s.clear()


def trajectory_host(i):
    shift = np.zeros((SEQ, SEQ), np.float32)
    band = np.zeros((SEQ, SEQ), np.float32)
    for j in range(SEQ - 1):
        shift[j + 1, j], shift[j, j] = 1.0, -1.0
    for pos in range(1, SEQ):
        width = min(pos, WIN)
        for k in range(WIN):
            j, at = k - (WIN - width), pos - WIN + k
            if at >= 0:
                band[at, pos] = 0.1 + 0.9 * j / max(width - 1, 1) if width > 1 else 0.1
    return {"shiftm": shift, "band": band, "guide": np.asarray(i["L1_attn_guidance_trajectories"])}

FF, FC = 512, 512 // P


def decoder_stage(nc, w, consts, x_in, ctx_in, x_out):
    ident, hmask, half_neg = consts["ident"], consts["hmask"], consts["half_neg"]
    with ExitStack() as st:
        def sb(name, shape, dt=F32):
            return st.enter_context(nc.sbuf_tensor("de_" + name, shape, dt))

        bank = st.enter_context(nc.psum_tensor("de_bank", [P, 8, 512], F32))
        s = Sems(nc, st, ["de_" + n for n in [
            "n_var", "n_rstd", "in", "ctx", "ct", "cts", "k", "ks", "v", "vb", "xt", "xts", "vx", "x1", "x1t", "x1s",
            "q", "qs", "x2", "x2t", "x2s", "f1", "f1s", "f2", "out", "store"]
            + ["s_" + n for n in ATTN_SEMS] + ["c_" + n for n in ATTN_SEMS]])
        p = Prefixed(s, "de_")
        wq, wk, wv, wo, ws = (sb(n, [P, D]) for n in ("wq", "wk", "wv", "wo", "ws"))
        w1, w2 = sb("w1", [P, FF]), sb("w2", [P, FC, D])
        vecs = sb("vecs", [P, 2 + FC])
        rows = sb("rows", [P, 10, D])
        SO, BV, CO, B2, G1 = 0, 1, 2, 3, 4
        x_tok, a_tok, b_tok, y_tok = (sb(n, [P, GB, D]) for n in ("x_tok", "a_tok", "b_tok", "y_tok"))
        c_tok = sb("c_tok", [NC, GB, D])
        xT, qT = sb("xT", [P, GB, SEQ]), sb("qT", [P, GB, SEQ])
        cT, kT = sb("cT", [P, GB, NC]), sb("kT", [P, GB, NC])
        vself = sb("vself", [P, GB, H, VW])
        vx = sb("vx", [NC, GB, H, VW])
        hT = sb("hT", [P, FC, TOK])
        norm = Norm(sb, p, "n", half_neg)
        own = Attention(nc, sb, p, "s", bank, ident, hmask, SEQ, D ** -0.5, topk=True)
        cross = Attention(nc, sb, p, "c", bank, ident, hmask, NC, DK ** -0.5)

        s0 = Sems(nc, st, ["de0_w"])
        with nc.Block() as block:
            @block.sync
            def _(sp):
                loads = [(wq, "wq"), (wk, "wk"), (wv, "wv"), (wo, "wo"), (ws, "ws"), (w1, "w1"), (w2, "w2"), (vecs, "vecs")]
                for t, k in loads:
                    sp.dma_start(t[:], w[k]).then_inc(s0["de0_w"], 16)
                sp.dma_start(rows[:].rearrange("p r d -> p (r d)"), w["rows"].rearrange("r d -> (r d)").unsqueeze(0)
                             .to_broadcast([P, 10 * D])).then_inc(s0["de0_w"], 16)
                sp.wait_ge(s0["de0_w"], 16 * (len(loads) + 1))

            @block.vector
            def _(dve):
                nc.vector.memset(vx[:], 1.0)
                nc.vector.memset(vself[:], 1.0)
                for i in range(2):
                    nc.vector.memset(own.sp[i][:], LOW)
        s0.clear()

        def flat(t):
            return t[:].rearrange("p b d -> p (b d)")

        def wide_row(r):
            return rows[:, r].unsqueeze(1).to_broadcast([P, GB, D])

        with nc.Fori(0, GROUPS) as g:
            norm.on_dve = norm.on_pool = 0
            with nc.Block() as block:
                @block.sync
                def _(sp):
                    sp.dma_start(x_tok[:], tile_rows(x_in, g)).then_inc(p["in"], 16)
                    sp.dma_start(c_tok[:], ctx_rows(ctx_in, g)).then_inc(p["ctx"], 16)
                    sp.wait_ge(p["out"], 1)
                    sp.dma_start(tile_rows(x_out, g), y_tok[:]).then_inc(p["store"], 16)
                    sp.wait_ge(p["store"], 16)

                @block.gpsimd
                def _(pool):
                    pool.wait_ge(p["xts"], 1)
                    own.pool(pool, lambda b: xT[:, b])
                    norm.pool(pool)
                    pool.wait_ge(p["ks"], 1)
                    cross.pool(pool, lambda b: kT[:, b])
                    for _ in range(3):
                        norm.pool(pool)

                @block.tensor
                def _(pe):
                    pe.wait_ge(p["in"], 16)
                    for b in range(GB):
                        m = nc.tensor.transpose(bank[:, 0, b * P:(b + 1) * P], x_tok[:, b], ident[:])
                    m.then_inc(p["xt"], 1)
                    pe.wait_ge(p["ctx"], 16)
                    for b in range(GB):
                        m = nc.tensor.transpose(bank[:, 1, b * NC:(b + 1) * NC], c_tok[:, b], ident[0:NC, 0:NC])
                    m.then_inc(p["ct"], 1)
                    pe.wait_ge(p["cts"], 1)
                    nc.tensor.matmul(bank[:, 2, 0:GB * NC], wk[:], flat(cT), start=True, stop=True).then_inc(p["k"], 1)
                    for b in range(GB):
                        m = nc.tensor.matmul(bank[0:NC, 3, b * D:(b + 1) * D], cT[:, b], wv[:], start=True, stop=True)
                    m.then_inc(p["v"], 1)
                    pe.wait_ge(p["xts"], 1)
                    pe.wait_ge(p["ks"], 1)
                    pe.wait_ge(p["vb"], 1)
                    pe.wait_ge(p["vx"], 1)
                    own.pe(pe, lambda b: xT[:, b], lambda b, h: vself[:, b, h], ws)
                    pe.wait_ge(p["x1"], 1)
                    for b in range(GB):
                        m = nc.tensor.transpose(bank[:, 0, b * P:(b + 1) * P], a_tok[:, b], ident[:])
                    m.then_inc(p["x1t"], 1)
                    pe.wait_ge(p["x1s"], 1)
                    nc.tensor.matmul(bank[:, 1], wq[:], flat(xT), start=True, stop=True).then_inc(p["q"], 1)
                    pe.wait_ge(p["qs"], 1)
                    cross.pe(pe, lambda b: qT[:, b], lambda b, h: vx[:, b, h], wo)
                    pe.wait_ge(p["x2"], 1)
                    for b in range(GB):
                        m = nc.tensor.transpose(bank[:, 0, b * P:(b + 1) * P], a_tok[:, b], ident[:])
                    m.then_inc(p["x2t"], 1)
                    pe.wait_ge(p["x2s"], 1)
                    for c in range(FC):
                        nc.tensor.matmul(bank[:, 1 + c], w1[:, c * P:(c + 1) * P], flat(xT), start=True, stop=True).then_inc(p["f1"], 1)
                    pe.wait_ge(p["f1s"], FC)
                    for b in range(GB):
                        for c in range(FC):
                            m = nc.tensor.matmul(bank[:, 5, b * D:(b + 1) * D], hT[:, c, b * SEQ:(b + 1) * SEQ], w2[:, c],
                                                 start=(c == 0), stop=(c == FC - 1))
                    m.then_inc(p["f2"], 1)

                @block.scalar
                def _(act):
                    act.wait_ge(p["xt"], 1)
                    nc.scalar.activation(flat(xT), bank[:, 0], ACT.Copy).then_inc(p["xts"], 1)
                    act.wait_ge(p["ct"], 1)
                    nc.scalar.activation(flat(cT), bank[:, 1, 0:GB * NC], ACT.Copy).then_inc(p["cts"], 1)
                    act.wait_ge(p["k"], 1)
                    nc.scalar.activation(flat(kT), bank[:, 2, 0:GB * NC], ACT.Identity, bias=vecs[:, 1:2]).then_inc(p["ks"], 1)
                    own.act(act)
                    act.wait_ge(p["x1t"], 1)
                    nc.scalar.activation(flat(xT), bank[:, 0], ACT.Copy).then_inc(p["x1s"], 1)
                    act.wait_ge(p["q"], 1)
                    nc.scalar.activation(flat(qT), bank[:, 1], ACT.Identity, bias=vecs[:, 0:1]).then_inc(p["qs"], 1)
                    cross.act(act)
                    act.wait_ge(p["x2t"], 1)
                    nc.scalar.activation(flat(xT), bank[:, 0], ACT.Copy).then_inc(p["x2s"], 1)
                    for c in range(FC):
                        act.wait_ge(p["f1"], c + 1)
                        nc.scalar.activation(hT[:, c], bank[:, 1 + c], ACT.Gelu, bias=vecs[:, 2 + c:3 + c]).then_inc(p["f1s"], 1)

                @block.vector
                def _(dve):
                    dve.wait_ge(p["in"], 16)
                    nc.vector.tensor_copy(vself[:, :, :, 0:DK], x_tok[:].rearrange("p b (h v) -> p b h v", v=DK)).then_inc(p["vx"], 1)
                    nc.vector.tensor_tensor(b_tok[:], x_tok[:], wide_row(SO), ALU.add)
                    dve.wait_ge(p["v"], 1)
                    nc.vector.tensor_tensor(vx[:, :, :, 0:DK], bank[0:NC, 3].rearrange("p (b h v) -> p b h v", b=GB, h=H),
                                            rows[0:NC, BV].rearrange("p (h v) -> p h v", h=H).unsqueeze(1).to_broadcast([NC, GB, H, DK]),
                                            ALU.add).then_inc(p["vb"], 1)
                    dve.drain()

                    def add(b, psum):
                        nc.vector.tensor_tensor(a_tok[:, b], b_tok[:, b], psum, ALU.add)

                    def affine_norm(k, src, dst):
                        norm.dve(dve, src, y_tok)
                        dve.drain()
                        nc.vector.tensor_tensor(y_tok[:], y_tok[:], wide_row(G1 + 2 * k), ALU.mult)
                        dve.drain()
                        return nc.vector.tensor_tensor(dst[:], y_tok[:], wide_row(G1 + 2 * k + 1), ALU.add)

                    own.dve(dve, add)
                    dve.drain()
                    affine_norm(0, a_tok, a_tok).then_inc(p["x1"], 1)
                    dve.wait_ge(p["x1"], 1)
                    nc.vector.tensor_tensor(b_tok[:], a_tok[:], wide_row(CO), ALU.add)
                    dve.wait_ge(p["x1t"], 1)
                    dve.drain()
                    cross.dve(dve, add)
                    dve.drain()
                    affine_norm(1, a_tok, a_tok).then_inc(p["x2"], 1)
                    dve.wait_ge(p["x2"], 1)
                    nc.vector.tensor_tensor(b_tok[:], a_tok[:], wide_row(B2), ALU.add)
                    dve.drain()
                    dve.wait_ge(p["f2"], 1)
                    nc.vector.tensor_tensor(a_tok[:], b_tok[:], bank[:, 5].rearrange("p (b d) -> p b d", b=GB), ALU.add)
                    dve.drain()
                    affine_norm(2, a_tok, b_tok)
                    dve.drain()
                    nc.vector.tensor_tensor(a_tok[:], b_tok[:], x_tok[:], ALU.add)
                    dve.drain()
                    norm.dve(dve, a_tok, y_tok).then_inc(p["out"], 1)
            s.clear()


def decoder_host(i):
    A = lambda k: np.asarray(i["L1_xattn_" + k])
    iw, ib = A("cross_in_w"), A("cross_in_b")
    return {"wq": iw[:D].T, "wk": iw[D:2 * D].T, "wv": iw[2 * D:].T, "wo": A("cross_out_w").T, "ws": A("self_out_w").T,
            "w1": A("ffn_w1").T, "w2": A("ffn_w2").T.reshape(FC, P, D).transpose(1, 0, 2),
            "vecs": np.concatenate([ib[:D, None], ib[D:2 * D, None], A("ffn_b1").reshape(FC, P).T], axis=1),
            "rows": np.stack([A("self_out_b"), ib[2 * D:], A("cross_out_b"), A("ffn_b2"), A("ln1_g"), A("ln1_b"),
                              A("ln2_g"), A("ln2_b"), A("ln3_g"), A("ln3_b")])}


ROUND = 1.5 * 2.0 ** 23
QMAX, QMIN, EPS_Q = 127.0, -128.0, 1e-5


def bitlinear_stage(nc, w, consts, x_in, x_out):
    ident, half_neg = consts["ident"], consts["half_neg"]
    with ExitStack() as st:
        def sb(name, shape, dt=F32):
            return st.enter_context(nc.sbuf_tensor("bl_" + name, shape, dt))

        bank = st.enter_context(nc.psum_tensor("bl_bank", [P, 6, 512], F32))
        bankb = st.enter_context(nc.psum_tensor("bl_bankb", [P, 2, 1024], BF16))
        s = Sems(nc, st, ["bl_" + n for n in [
            "n_var", "n_rstd", "in", "xq", "xt", "xts", "gu", "sg", "hq", "ht", "hts", "y", "sum", "out", "store"]])
        p = Prefixed(s, "bl_")
        wts = [sb(f"w{k}", [P, FF]) for k in range(3)]
        wa = sb("wa", [P, FF])
        wb = [sb(f"wb{k}", [P, FF], BF16) for k in range(3)]
        identb = sb("identb", [P, P], BF16)
        ones = sb("ones", [P, P])
        asum, mean, wsc = (sb(n, [P, 3]) for n in ("asum", "mean", "wsc"))
        x_tok, y_tok = sb("x_tok", [P, GB, D]), sb("y_tok", [P, GB, D])
        t_tok = sb("t_tok", [P, GB, D])
        xq = sb("xq", [P, GB, D], BF16)
        xqT = sb("xqT", [P, GB, P], BF16)
        mx, sc, rg, ru = (sb(n, [P, GB]) for n in ("mx", "sc", "rg", "ru"))
        sg = [sb(f"sg{i}", [P, FF]) for i in range(2)]
        hh = [sb(f"hh{i}", [P, FF]) for i in range(2)]
        hm, hs, hr = (sb(n, [P, GB]) for n in ("hm", "hs", "hr"))
        hq = [sb(f"hq{i}", [P, FF], BF16) for i in range(2)]
        hqT = [sb(f"hqT{i}", [P, FF], BF16) for i in range(2)]
        norm = Norm(sb, p, "n", half_neg)

        s0 = Sems(nc, st, ["bl0_w", "bl0_s", "bl0_m"])
        with nc.Block() as block:
            @block.sync
            def _(sp):
                for t, k in zip(wts, ("gate", "up", "down")):
                    sp.dma_start(t[:], w[k]).then_inc(s0["bl0_w"], 16)

            @block.tensor
            def _(pe):
                pe.wait_ge(s0["bl0_s"], 1)
                nc.tensor.matmul(bank[:, 0, 0:3], ones[:], asum[:], start=True, stop=True).then_inc(s0["bl0_m"], 1)

            @block.vector
            def _(dve):
                nc.vector.memset(ones[:], 1.0)
                nc.vector.tensor_copy(identb[:], ident[:])
                dve.wait_ge(s0["bl0_w"], 48)
                for k in range(3):
                    nc.vector.tensor_reduce(asum[:, k:k + 1], wts[k][:], AX.X, ALU.add, apply_absolute_value=True)
                    dve.drain()
                nc.vector.tensor_copy(mean[:], asum[:]).then_inc(s0["bl0_s"], 1)
                dve.wait_ge(s0["bl0_m"], 1)
                nc.vector.tensor_scalar(mean[:], bank[:, 0, 0:3], 1.0 / (P * FF), EPS_Q, ALU.mult, ALU.max)
                dve.drain()
                nc.vector.reciprocal(wsc[:], mean[:])
                dve.drain()
                for k in range(3):
                    nc.vector.tensor_scalar(wa[:], wts[k][:], wsc[:, k:k + 1], ROUND, ALU.mult, ALU.add)
                    dve.drain()
                    nc.vector.tensor_scalar(wa[:], wa[:], -ROUND, 1.0, ALU.add, ALU.min)
                    dve.drain()
                    nc.vector.tensor_scalar(wb[k][:], wa[:], -1.0, None, ALU.max)
                    dve.drain()
        s0.clear()

        def flat(t):
            return t[:].rearrange("p b d -> p (b d)")

        with nc.Fori(0, GROUPS) as g:
            norm.on_dve = norm.on_pool = 0
            with nc.Block() as block:
                @block.sync
                def _(sp):
                    sp.dma_start(x_tok[:], tile_rows(x_in, g)).then_inc(p["in"], 16)
                    sp.wait_ge(p["out"], 1)
                    sp.dma_start(tile_rows(x_out, g), y_tok[:]).then_inc(p["store"], 16)
                    sp.wait_ge(p["store"], 16)

                @block.gpsimd
                def _(pool):
                    norm.pool(pool)

                @block.tensor
                def _(pe):
                    pe.wait_ge(p["xq"], 1)
                    for b in range(GB):
                        m = nc.tensor.transpose(bankb[:, 0, b * P:(b + 1) * P], xq[:, b], identb[:])
                    m.then_inc(p["xt"], 1)
                    pe.wait_ge(p["xts"], 1)

                    def gate_up(b):
                        if b >= 2:
                            pe.wait_ge(p["hq"], b - 1)
                        for k in range(2):
                            nc.tensor.matmul(bank[:, 2 * (b % 2) + k], xqT[:, b], wb[k][:], start=True, stop=True).then_inc(p["gu"], 1)

                    gate_up(0)
                    for b in range(GB):
                        if b + 1 < GB:
                            gate_up(b + 1)
                        pe.wait_ge(p["hq"], b + 1)
                        if b:
                            pe.wait_ge(p["hts"], b)
                        for c in range(FC):
                            m = nc.tensor.transpose(bankb[:, 1, c * P:(c + 1) * P], hq[b % 2][:, c * P:(c + 1) * P], identb[:])
                        m.then_inc(p["ht"], 1)
                        pe.wait_ge(p["hts"], b + 1)
                        if b:
                            pe.wait_ge(p["sum"], b)
                        for c in range(FC):
                            m = nc.tensor.matmul(bank[:, 4, 0:D], hqT[b % 2][:, c * P:(c + 1) * P], wb[2][:, c * D:(c + 1) * D],
                                                 start=(c == 0), stop=(c == FC - 1))
                        m.then_inc(p["y"], 1)

                @block.scalar
                def _(act):
                    act.wait_ge(p["xt"], 1)
                    nc.scalar.activation(flat(xqT), bankb[:, 0, 0:TOK], ACT.Copy).then_inc(p["xts"], 1)

                    def silu(b):
                        act.wait_ge(p["gu"], 2 * b + 1)
                        if b >= 2:
                            act.wait_ge(p["hq"], b - 1)
                        nc.scalar.activation(sg[b % 2][:], bank[:, 2 * (b % 2)], ACT.Silu, scale=rg[:, b:b + 1]).then_inc(p["sg"], 1)

                    silu(0)
                    for b in range(GB):
                        if b + 1 < GB:
                            silu(b + 1)
                        act.wait_ge(p["ht"], b + 1)
                        if b >= 2:
                            act.wait_ge(p["y"], b - 1)
                        nc.scalar.activation(hqT[b % 2][:], bankb[:, 1, 0:FF], ACT.Copy).then_inc(p["hts"], 1)

                @block.vector
                def _(dve):
                    def magnitude(dst, src):
                        nc.vector.tensor_reduce(dst, src, AX.X, ALU.max, apply_absolute_value=True)
                        dve.drain()
                        nc.vector.tensor_scalar(dst, dst, EPS_Q, 1.0 / QMAX, ALU.max, ALU.mult)
                        dve.drain()

                    dve.wait_ge(p["in"], 16)
                    magnitude(mx[:], x_tok[:])
                    nc.vector.reciprocal(sc[:], mx[:])
                    nc.vector.tensor_scalar(rg[:], mx[:], mean[:, 0:1], None, ALU.mult)
                    nc.vector.tensor_scalar(ru[:], mx[:], mean[:, 1:2], None, ALU.mult)
                    dve.drain()
                    for b in range(GB):
                        nc.vector.tensor_scalar(t_tok[:, b], x_tok[:, b], sc[:, b:b + 1], ROUND, ALU.mult, ALU.add)
                    dve.drain()
                    nc.vector.tensor_scalar(t_tok[:], t_tok[:], -ROUND, QMAX, ALU.add, ALU.min)
                    dve.drain()
                    nc.vector.tensor_scalar(xq[:], t_tok[:], QMIN, None, ALU.max).then_inc(p["xq"], 1)
                    for b in range(GB):
                        i = b % 2
                        dve.wait_ge(p["sg"], b + 1)
                        dve.wait_ge(p["gu"], 2 * b + 2)
                        nc.vector.scalar_tensor_tensor(out=hh[i][:], in0=bank[:, 2 * i + 1], scalar=ru[:, b:b + 1], in1=sg[i][:],
                                                       op0=ALU.mult, op1=ALU.mult)
                        dve.drain()
                        magnitude(hm[:, b:b + 1], hh[i][:])
                        nc.vector.reciprocal(hs[:, b:b + 1], hm[:, b:b + 1])
                        nc.vector.tensor_scalar(hr[:, b:b + 1], hm[:, b:b + 1], mean[:, 2:3], None, ALU.mult)
                        dve.drain()
                        nc.vector.tensor_scalar(hh[i][:], hh[i][:], hs[:, b:b + 1], ROUND, ALU.mult, ALU.add)
                        dve.drain()
                        nc.vector.tensor_scalar(hh[i][:], hh[i][:], -ROUND, QMAX, ALU.add, ALU.min)
                        dve.drain()
                        if b >= 2:
                            dve.wait_ge(p["ht"], b - 1)
                        nc.vector.tensor_scalar(hq[i][:], hh[i][:], QMIN, None, ALU.max).then_inc(p["hq"], 1)
                        if b:
                            dve.wait_ge(p["y"], b)
                            nc.vector.scalar_tensor_tensor(out=t_tok[:, b - 1], in0=bank[:, 4, 0:D], scalar=hr[:, b - 1:b],
                                                           in1=x_tok[:, b - 1], op0=ALU.mult, op1=ALU.add).then_inc(p["sum"], 1)
                    dve.wait_ge(p["y"], GB)
                    nc.vector.scalar_tensor_tensor(out=t_tok[:, GB - 1], in0=bank[:, 4, 0:D], scalar=hr[:, GB - 1:GB],
                                                   in1=x_tok[:, GB - 1], op0=ALU.mult, op1=ALU.add)
                    dve.drain()
                    norm.dve(dve, t_tok, y_tok).then_inc(p["out"], 1)
            s.clear()


def bitlinear_host(i):
    A = lambda k: np.asarray(i["L1_ffn_w_" + k])
    return {"gate": A("gate").T, "up": A("up").T, "down": A("down").T.reshape(FC, P, D).transpose(1, 0, 2).reshape(P, FC * D)}


WEIGHTS = {"mb": mamba_host, "xa": xattn_host, "ex": experts_host, "tj": trajectory_host, "de": decoder_host, "bl": bitlinear_host}


def build(nc, a, out):
    of = lambda pre: {k[len(pre) + 1:]: v for k, v in a.items() if k.startswith(pre + "_")}
    with ExitStack() as st:
        consts = {"ident": st.enter_context(nc.sbuf_tensor("ident", [P, P], F32)),
                  "hmask": st.enter_context(nc.sbuf_tensor("hmask", [P, H], F32)),
                  "half_neg": st.enter_context(nc.sbuf_tensor("minus_half", [P, GB], F32))}
        padded = nc.dram_tensor("stream0", [(GROUPS + 2) * TOK, D], F32).ap()
        after_mamba = padded[TOK:TOK * (GROUPS + 1)]
        stream = [after_mamba] + [nc.dram_tensor(f"stream{k}", [BATCH * SEQ, D], F32).ap() for k in range(1, 5)]
        loaded = st.enter_context(nc.semaphore("consts_loaded"))
        with nc.Block() as block:
            @block.sync
            def _(sp):
                sp.dma_start(consts["ident"][:], a["ident"]).then_inc(loaded, 16)
                sp.dma_start(consts["hmask"][:], a["hmask"]).then_inc(loaded, 16)
                sp.dma_start(after_mamba, a["x"]).then_inc(loaded, 16)
                sp.dma_start(padded[0:TOK], a["x"][0:TOK]).then_inc(loaded, 16)
                sp.dma_start(padded[TOK * (GROUPS + 1):], a["x"][0:TOK]).then_inc(loaded, 16)
                sp.wait_ge(loaded, 5 * 16)

            @block.vector
            def _(dve):
                nc.vector.memset(consts["half_neg"][:], -0.5)
        mamba_stage(nc, of("mb"), consts, padded)
        xattn_stage(nc, of("xa"), consts, a["x"], stream[0], a["ctx"], a["mask"], stream[1])
        experts_stage(nc, of("ex"), consts, stream[1], stream[2])
        trajectory_stage(nc, of("tj"), consts, stream[2], stream[3])
        decoder_stage(nc, of("de"), consts, stream[3], a["ctx"], stream[4])
        bitlinear_stage(nc, of("bl"), consts, stream[4], out)


def kernel(**inputs):
    import concourse.bacc as bacc
    from concourse.bass_utils import run_bass_kernel_spmd

    host = {"x": np.asarray(inputs["x"]).reshape(BATCH * SEQ, D), "ctx": np.asarray(inputs["ctx_1024"]),
            "mask": np.asarray(inputs["mask_Bx1x1xS2_ik0"]).reshape(BATCH, NC),
            "ident": np.eye(P, dtype=np.float32), "hmask": np.repeat(np.eye(H, dtype=np.float32), DK, axis=0)}
    for pre, lay in WEIGHTS.items():
        host.update({f"{pre}_{k}": v for k, v in lay(inputs).items()})
    nc = bacc.Bacc("TRN2", target_bir_lowering=False, num_devices=1)
    arrays, a = {}, {}
    for k, v in host.items():
        arrays["in_" + k] = np.ascontiguousarray(v)
        a[k] = nc.dram_tensor("in_" + k, v.shape, mybir.dt.from_np(v.dtype), kind="ExternalInput").ap()
    out = nc.dram_tensor("out", [BATCH * SEQ, D], F32, kind="ExternalOutput").ap()
    build(nc, a, out)
    r = run_bass_kernel_spmd(nc, [arrays], core_ids=[0])
    return r.results[0]["out"].reshape(BATCH, SEQ, D)
```

```python
from contextlib import ExitStack

import numpy as np
import concourse.bass as bass
from concourse import mybir

F32 = mybir.dt.float32
BF16 = mybir.dt.bfloat16
I32 = mybir.dt.int32
U32 = mybir.dt.uint32
ALU = mybir.AluOpType
ACT = mybir.ActivationFunctionType
AX = mybir.AxisListType

P = 128
BATCH, SEQ, D = 64, 128, 128
GB = 4
TOK = GB * SEQ
GROUPS = BATCH // GB
LN_EPS = 1e-5

NL, DI, DS, DC = 4, 256, 16, 4
DR = D // 16
CH = DI // P
PADT = SEQ + 1
RING = 4
SMALL_Y = 2.0 ** -7
KW = SEQ + DC - 1


def tile_rows(ap, g):
    v = ap.rearrange("(g b t) d -> g t b d", b=GB, t=SEQ)
    return v[bass.ds(g, 1)].rearrange("g t b d -> (g t) b d")


class Sems:

    def __init__(self, nc, stack, names):
        self.nc = nc
        self.by = {n: stack.enter_context(nc.semaphore(n)) for n in names}
        self.runs = []
        for num in sorted(s.num for s in self.by.values()):
            if self.runs and self.runs[-1][1] == num:
                self.runs[-1][1] += 1
            else:
                self.runs.append([num, num + 1])

    def __getitem__(self, name):
        return self.by[name]

    def clear(self):
        for first, end in self.runs:
            self.nc.sync.sem_clear(range(first, end))
        self.nc.all_engine_barrier()


def mamba_stage(nc, w, consts, res):
    ident = consts["ident"]
    with ExitStack() as ctx:
        def sb(name, shape, dt=F32):
            return ctx.enter_context(nc.sbuf_tensor("mb_" + name, shape, dt))

        def pair(name, shape, dt=F32, n=2):
            return [sb(f"{name}{i}", shape, dt) for i in range(n)]

        bank = ctx.enter_context(nc.psum_tensor("mb_bank", [P, 8, 512], F32))
        w_in = sb("w_in", [P, 2 * DI])
        conv_row = sb("conv_row", [P, DC, DI])
        w_conv = sb("w_conv", [P, DC, DI])
        w_x = sb("w_x", [P, CH, 2 * DS + DR])
        w_dt = sb("w_dt", [2 * DS + DR, DI])
        w_out = sb("w_out", [P, CH, D])
        vec = sb("vec", [P, 2 + 3 * CH + CH * DS])
        a_neg = sb("a_neg", [P, CH * DS])
        conv_bh = sb("conv_bh", [P, CH])
        selcol = sb("selcol", [96, 2 * DS])
        sel = sb("sel", [96, 2 * DS, P], BF16)
        half_neg = sb("half_neg", [P, GB])
        small_at = sb("small_at", [P, 1])
        r_tok = sb("r_tok", [P, GB, D])
        stats = sb("stats", [P, GB, 6])
        mv = sb("mv", [P, GB, 2])
        rstd = sb("rstd", [P, GB])
        xh = sb("xh", [P, GB, D])
        h_ch = sb("h_ch", [P, GB, KW])
        th, zth = sb("th", [P, CH, TOK]), sb("zth", [P, CH, TOK])
        bc_f, bc_r = sb("bc_f", [2 * DS, TOK]), sb("bc_r", [2 * DS, TOK])
        bc_m = sb("bc_m", [2 * DS, TOK], BF16)
        dtr = sb("dtr", [2 * DS + DR, TOK])
        ab, ey, ey3, ln1, poly, small, relu = (sb(n, [P, CH, TOK]) for n in ("ab", "ey", "ey3", "ln1", "poly", "small", "relu"))
        bc_s = pair("bc_s", [96, TOK], BF16)
        dt, dtu, u2, zg = (pair(n, [P, CH, TOK]) for n in ("dt", "dtu", "u2", "zg"))
        dA, dBu = (pair(n, [P, CH * GB, PADT], n=RING) for n in ("dA", "dBu"))
        hs = pair("hs", [P, CH * GB, PADT])
        b_sb = pair("b_sb", [P, TOK], n=RING)
        hc = pair("hc", [P, CH, TOK])
        yv, yg, r_post = sb("yv", [P, CH, TOK]), sb("yg", [P, CH, TOK]), sb("r_post", [P, GB, D])

        NW, NB, CB, DB, DD, AL = 0, 1, 2, 2 + CH, 2 + 2 * CH, 2 + 3 * CH
        B_TR, B_X, B_Z, B_DT, B_OUT, B_B, B_C, B_Y = 0, 0, 2, 1, 3, 4, 5, 6

        s0 = Sems(nc, ctx, ["mbc_sel"])
        with nc.Block() as block:
            @block.sync
            def _(sp):
                sp.dma_start(selcol[:], w["selcol"]).then_inc(s0["mbc_sel"], 16)

            @block.vector
            def _(dve):
                nc.vector.memset(half_neg[:], -0.5)
                nc.vector.memset(small_at[:], SMALL_Y)
                nc.vector.memset(h_ch[:], 0.0)
                for i in range(RING):
                    nc.vector.memset(dA[i][:], 0.0)
                    nc.vector.memset(dBu[i][:], 0.0)
                nc.vector.memset(bank[:, B_Y:B_Y + 2], 0.0)
                nc.vector.memset(u2[1][:], 0.0)
                nc.vector.memset(zg[1][:], 0.0)
                dve.wait_ge(s0["mbc_sel"], 16)
                nc.vector.tensor_copy(sel[:], selcol[:].unsqueeze(2).to_broadcast([96, 2 * DS, P]))
        s0.clear()

        sw = Sems(nc, ctx, ["mbw_dma", "mbw_a"])
        s = Sems(nc, ctx, ["mb_" + n for n in [
            "res", "var", "rstd", "xh", "tr", "h", "conv", "z", "th", "th1", "zth", "u", "zg", "xp", "hi", "bcf", "r1",
            "mid", "lo", "split", "dtr", "poly", "dtp", "abs", "relu", "ey", "ln", "dt", "dtu",
            "bps", "cps", "bsb", "dbu", "da", "scan", "hc", "sum", "yv", "yg", "rp", "out", "new", "store"]])

        class Ahead:
            def __init__(self, q, behind=True):
                self.q = q
                self.behind = behind

            def load(self, sp, g):
                sp.dma_start(r_tok[:], tile_rows(res, g)).then_inc(s["mb_res"], 16)

            def dve(self, dve, n):
                q = self.q
                if n == -2:
                    for b in range(GB):
                        nc.vector.bn_stats(stats[:, b], r_tok[:, b])
                    dve.drain()
                    for b in range(GB):
                        nc.vector.bn_aggr(mv[:, b], stats[:, b])
                    dve.drain()
                    nc.vector.tensor_scalar(mv[:, :, 1], mv[:, :, 1], LN_EPS, None, ALU.add).then_inc(s["mb_var"], 1)
                if n == -1:
                    dve.wait_ge(s["mb_rstd"], 1)
                    for b in range(GB):
                        m = nc.vector.tensor_scalar(xh[:, b], r_tok[:, b], mv[:, b, 0:1], rstd[:, b:b + 1],
                                                    ALU.subtract, ALU.mult)
                    m.then_inc(s["mb_xh"], 1)
                if n in (4, 6):
                    c = (n - 4) // 2
                    dve.wait_ge(s["mb_th1"], c + 1)
                    nc.vector.scalar_tensor_tensor(out=u2[q][:, c], in0=bank[:, B_X + c], scalar=vec[:, CB + c:CB + c + 1],
                                                   in1=th[:, c], op0=ALU.add, op1=ALU.mult).then_inc(s["mb_u"], 1)
                if n == 7:
                    for c in range(CH):
                        dve.wait_ge(s["mb_zth"], c + 1)
                        nc.vector.scalar_tensor_tensor(out=zg[q][:, c], in0=zth[:, c], scalar=1.0, in1=bank[:, B_Z + c],
                                                       op0=ALU.add, op1=ALU.mult).then_inc(s["mb_zg"], 1)
                if n == 10:
                    dve.wait_ge(s["mb_ey"], 1)
                    nc.vector.scalar_tensor_tensor(out=poly[:], in0=ey[:], scalar=-1.5, in1=ey[:], op0=ALU.add,
                                                   op1=ALU.mult).then_inc(s["mb_poly"], 1)
                if n == 11:
                    dve.wait_ge(s["mb_poly"], 1)
                    dve.wait_ge(s["mb_ey"], 2)
                    nc.vector.scalar_tensor_tensor(out=poly[:], in0=poly[:], scalar=3.0, in1=ey3[:], op0=ALU.add, op1=ALU.mult)
                    dve.drain()
                    dve.wait_ge(s["mb_ln"], 2)
                    nc.vector.copy_predicated(ln1[:], small[:].bitcast(I32), poly[:])
                    dve.drain()
                    dve.wait_ge(s["mb_relu"], CH)
                    nc.vector.tensor_tensor(dt[q][:], ln1[:], relu[:], ALU.add).then_inc(s["mb_dt"], 1)

            def pool(self, pool, n):
                q = self.q
                if n == -1:
                    pool.wait_ge(s["mb_var"], 1)
                    nc.gpsimd.tensor_tensor(rstd[:], mv[:, :, 1], half_neg[:], ALU.pow).then_inc(s["mb_rstd"], 1)
                if n in (3, 5):
                    c = (n - 3) // 2
                    pool.wait_ge(s["mb_th"], c + 1)
                    nc.gpsimd.tensor_scalar(th[:, c], th[:, c], 1.0, 1.0, ALU.mult, ALU.add).then_inc(s["mb_th1"], 1)
                if n == 8:
                    pool.wait_ge(s["mb_bcf"], 1)
                    pool.wait_ge(s["mb_hi"], 1)
                    nc.gpsimd.tensor_tensor(bc_r[:], bc_f[:], bc_s[q][0:32, :], ALU.subtract).then_inc(s["mb_r1"], 1)
                if n == 10:
                    pool.wait_ge(s["mb_mid"], 2)
                    nc.gpsimd.tensor_tensor(bc_f[:], bc_r[:], bc_m[:], ALU.subtract).then_inc(s["mb_lo"], 1)
                if n == 12:
                    pool.wait_ge(s["mb_dt"], 1)
                    nc.gpsimd.tensor_tensor(dtu[q][:], dt[q][:], u2[q][:], ALU.mult).then_inc(s["mb_dtu"], 1)

            def act(self, act, n):
                q = self.q
                if n == -1:
                    act.wait_ge(s["mb_tr"], 1)
                    nc.scalar.activation(h_ch[:, :, DC - 1:], bank[:, B_TR].rearrange("p (b t) -> p b t", b=GB),
                                         ACT.Identity, bias=vec[:, NB:NB + 1], scale=vec[:, NW:NW + 1]).then_inc(s["mb_h"], 1)
                if n in (3, 5):
                    c = (n - 3) // 2
                    act.wait_ge(s["mb_conv"], c + 1)
                    nc.scalar.activation(th[:, c], bank[:, B_X + c], ACT.Tanh, bias=conv_bh[:, c:c + 1],
                                         scale=0.5).then_inc(s["mb_th"], 1)
                if n == 6:
                    for c in range(CH):
                        act.wait_ge(s["mb_z"], c + 1)
                        nc.scalar.activation(zth[:, c], bank[:, B_Z + c], ACT.Tanh, scale=0.5).then_inc(s["mb_zth"], 1)
                if n == 8:
                    act.wait_ge(s["mb_xp"], 1)
                    nc.scalar.activation(dtr[32:40, :], bank[32:40, B_TR], ACT.Copy).then_inc(s["mb_dtr"], 1)
                    nc.scalar.activation(bc_f[:], bank[0:32, B_TR], ACT.Copy).then_inc(s["mb_bcf"], 1)
                    nc.scalar.activation(bc_s[q][0:32, :], bank[0:32, B_TR], ACT.Copy).then_inc(s["mb_hi"], 1)
                if n == 9:
                    for c in range(CH):
                        act.wait_ge(s["mb_dtp"], c + 1)
                        bias = vec[:, DB + c:DB + c + 1]
                        nc.scalar.activation(ab[:, c], bank[:, B_DT + c], ACT.Abs, bias=bias).then_inc(s["mb_abs"], 1)
                        nc.scalar.activation(relu[:, c], bank[:, B_DT + c], ACT.Relu, bias=bias).then_inc(s["mb_relu"], 1)
                    act.wait_ge(s["mb_abs"], CH)
                    nc.scalar.activation(ey[:], ab[:], ACT.Exp, scale=-1.0).then_inc(s["mb_ey"], 1)
                    act.wait_ge(s["mb_r1"], 1)
                    nc.scalar.activation(bc_m[:], bc_r[:], ACT.Copy).then_inc(s["mb_mid"], 1)
                    nc.scalar.activation(bc_s[q][32:64, :], bc_r[:], ACT.Copy).then_inc(s["mb_mid"], 1)
                if n == 10:
                    act.wait_ge(s["mb_ey"], 1)
                    nc.scalar.activation(ey3[:], ey[:], ACT.Copy, scale=1.0 / 3).then_inc(s["mb_ey"], 1)
                    nc.scalar.activation(ln1[:], ey[:], ACT.Ln, bias=1.0).then_inc(s["mb_ln"], 1)
                    nc.scalar.activation(small[:], ey[:], ACT.Relu, scale=-1.0, bias=small_at[:, 0:1]).then_inc(s["mb_ln"], 1)
                if n == 11:
                    act.wait_ge(s["mb_lo"], 1)
                    nc.scalar.activation(bc_s[q][64:96, :], bc_f[:], ACT.Copy).then_inc(s["mb_split"], 1)

            def pe(self, pe, n):
                if n == -1:
                    pe.wait_ge(s["mb_xh"], 1)
                    for b in range(GB):
                        m = nc.tensor.transpose(bank[:, B_TR, b * SEQ:(b + 1) * SEQ], xh[:, b], ident[:])
                    m.then_inc(s["mb_tr"], 1)
                if n in (0, 1, 2, 3):
                    c, half = divmod(n, 2)
                    pe.wait_ge(s["mb_h"], 1)
                    for k in range(2 * half, 2 * half + 2):
                        m = nc.tensor.matmul(bank[:, B_X + c], w_conv[:, k, c * P:(c + 1) * P],
                                             h_ch[:, :, k:k + SEQ], start=(k == 0), stop=(k == DC - 1))
                    if half:
                        m.then_inc(s["mb_conv"], 1)
                if n == 4:
                    if self.behind:
                        pe.wait_ge(s["mb_new"], 1)
                    for c in range(CH):
                        nc.tensor.matmul(bank[:, B_Z + c], w_in[:, DI + c * P:DI + (c + 1) * P],
                                         h_ch[:, :, DC - 1:], start=True, stop=True).then_inc(s["mb_z"], 1)
                if n == 6:
                    pe.wait_ge(s["mb_u"], CH)
                    for c in range(CH):
                        m = nc.tensor.matmul(bank[0:2 * DS + DR, B_TR], w_x[:, c], u2[self.q][:, c], start=(c == 0), stop=(c == CH - 1))
                    m.then_inc(s["mb_xp"], 1)
                if n == 8:
                    pe.wait_ge(s["mb_dtr"], 1)
                    pe.wait_ge(s["mb_zg"], 1)
                    for c in range(CH):
                        nc.tensor.matmul(bank[:, B_DT + c], w_dt[32:40, c * P:(c + 1) * P], dtr[32:40, :],
                                         start=True, stop=True).then_inc(s["mb_dtp"], 1)

        class Behind:
            def __init__(self, q):
                self.q = q

            def dve(self, dve, n):
                if n == -1:
                    for c in range(CH):
                        nc.vector.scalar_tensor_tensor(out=yv[:, c], in0=u2[self.q][:, c], scalar=vec[:, DD + c:DD + c + 1],
                                                       in1=bank[:, B_Y + c], op0=ALU.mult, op1=ALU.add).then_inc(s["mb_yv"], 1)
                    dve.wait_ge(s["mb_yv"], CH)
                    nc.vector.tensor_tensor(yg[:], yv[:], zg[self.q][:], ALU.mult).then_inc(s["mb_yg"], 1)
                if n == 2:
                    dve.wait_ge(s["mb_out"], 1)
                    dve.wait_ge(s["mb_rp"], 16)
                    nc.vector.tensor_tensor(r_post[:], r_post[:], bank[:, B_OUT].rearrange("p (b d) -> p b d", b=GB),
                                            ALU.add).then_inc(s["mb_new"], 1)

            def pe(self, pe, n):
                if n == 0:
                    pe.wait_ge(s["mb_yg"], 1)
                    for b in range(GB):
                        for c in range(CH):
                            m = nc.tensor.matmul(bank[:, B_OUT, b * D:(b + 1) * D], yg[:, c, b * SEQ:(b + 1) * SEQ],
                                                 w_out[:, c], start=(c == 0), stop=(c == CH - 1))
                    m.then_inc(s["mb_out"], 1)

            def fetch(self, sp, g):
                sp.dma_start(r_post[:], tile_rows(res, g)).then_inc(s["mb_rp"], 16)

            def store(self, sp, g):
                sp.wait_ge(s["mb_new"], 1)
                sp.dma_start(tile_rows(res, g), r_post[:]).then_inc(s["mb_store"], 16)
                sp.wait_ge(s["mb_store"], 16)

        class Scan:
            def __init__(self, q, made=0, next_q=None):
                self.q = q
                self.made = made
                self.next_q = next_q

            def of(self, j):
                m = j + self.made
                return m % DS, (self.q if m < DS else self.next_q), m % DS == 0

            def spread_b(self, pe, j):
                m, q, new = self.of(j)
                if new:
                    pe.wait_ge(s["mb_split"], 1)
                if j:
                    pe.wait_ge(s["mb_bsb"], j)
                nc.tensor.matmul(bank[:, B_B], sel[:, m], bc_s[q][:], start=True, stop=True).then_inc(s["mb_bps"], 1)

            def act(self, act, j):
                m, q, new = self.of(j)
                i = m % RING
                act.wait_ge(s["mb_bps"], j + 1)
                if j >= RING:
                    act.wait_ge(s["mb_dbu"], j - RING + 1)
                nc.scalar.activation(b_sb[i][:], bank[:, B_B], ACT.Copy).then_inc(s["mb_bsb"], 1)
                if new:
                    act.wait_ge(s["mb_dt"], 1)
                if j and self.made:
                    act.wait_ge(s["mb_scan"], j)
                for c in range(CH):
                    k = c * DS + m
                    nc.scalar.activation(dA[i][:, c * GB:(c + 1) * GB, 1:],
                                         dt[q][:, c].rearrange("p (b t) -> p b t", b=GB), ACT.Exp,
                                         scale=a_neg[:, k:k + 1]).then_inc(s["mb_da"], 1)

            def pool(self, pool, j):
                m, q, new = self.of(j)
                i = m % RING
                pool.wait_ge(s["mb_bsb"], j + 1)
                if new:
                    pool.wait_ge(s["mb_dtu"], 1)
                if j and self.made:
                    pool.wait_ge(s["mb_scan"], j)
                nc.gpsimd.tensor_tensor(
                    dBu[i][:, :, 1:].rearrange("p (c b) t -> p c b t", c=CH),
                    dtu[q][:].rearrange("p c (b t) -> p c b t", b=GB),
                    b_sb[i][:].rearrange("p (b t) -> p b t", b=GB).unsqueeze(1).to_broadcast([P, CH, GB, SEQ]),
                    ALU.mult).then_inc(s["mb_dbu"], 1)

            def scan(self, dve, n):
                i = n % RING
                if n >= self.made:
                    dve.wait_ge(s["mb_da"], CH * (n - self.made + 1))
                    dve.wait_ge(s["mb_dbu"], n - self.made + 1)
                if n >= 2:
                    dve.wait_ge(s["mb_hc"], n - 1)
                nc.vector.tensor_tensor_scan(hs[n % 2][:].rearrange("p c t -> p (c t)"), dA[i][:].rearrange("p c t -> p (c t)"),
                                             dBu[i][:].rearrange("p c t -> p (c t)"), 0.0, ALU.mult, ALU.add).then_inc(s["mb_scan"], 1)

            def read_out(self, dve, n):
                i = n % 2
                dve.wait_ge(s["mb_scan"], n + 1)
                dve.wait_ge(s["mb_cps"], n + 1)
                if n >= 2:
                    dve.wait_ge(s["mb_sum"], n - 1)
                nc.vector.tensor_tensor(
                    hc[i][:].rearrange("p c (b t) -> p c b t", b=GB),
                    hs[i][:, :, 1:].rearrange("p (c b) t -> p c b t", c=CH),
                    bank[:, B_C].rearrange("p (b t) -> p b t", b=GB).unsqueeze(1).to_broadcast([P, CH, GB, SEQ]),
                    ALU.mult).then_inc(s["mb_hc"], 1)

            def spread_c(self, pe, n):
                if n:
                    pe.wait_ge(s["mb_hc"], n)
                nc.tensor.matmul(bank[:, B_C], sel[:, DS + n], bc_s[self.q][:], start=True, stop=True).then_inc(s["mb_cps"], 1)

            def sum(self, pe, n):
                pe.wait_ge(s["mb_hc"], n + 1)
                if n == 0:
                    pe.wait_ge(s["mb_yv"], CH)
                for c in range(CH):
                    m = nc.tensor.matmul(bank[:, B_Y + c], ident[:], hc[n % 2][:, c], start=(n == 0), stop=(n == DS - 1))
                m.then_inc(s["mb_sum"], 1)

        with nc.Fori(0, NL) as layer:
            with nc.Block() as block:
                @block.sync
                def _(sp):
                    def load(dst, src):
                        sp.dma_start(dst, src).then_inc(sw["mbw_dma"], 16)
                    load(w_in[:], w["w_in"][bass.ds(layer, 1)].rearrange("l p e -> (l p) e"))
                    load(conv_row[:].rearrange("p k e -> p (k e)"),
                         w["conv_row"][bass.ds(layer, 1)].rearrange("l k e -> l (k e)").to_broadcast([P, DC * DI]))
                    load(w_x[:], w["w_x"][bass.ds(layer, 1)].rearrange("l p c m -> (l p) c m"))
                    load(w_dt[2 * DS:2 * DS + DR, :], w["w_dt"][bass.ds(layer, 1)].rearrange("l r e -> (l r) e"))
                    load(w_out[:], w["w_out"][bass.ds(layer, 1)].rearrange("l p c e -> (l p) c e"))
                    load(vec[:], w["vec"][bass.ds(layer, 1)].rearrange("l p v -> (l p) v"))

                @block.scalar
                def _(act):
                    act.wait_ge(sw["mbw_dma"], 6 * 16)
                    nc.scalar.activation(a_neg[:], vec[:, AL:AL + CH * DS], ACT.Exp).then_inc(sw["mbw_a"], 1)

                @block.vector
                def _(dve):
                    dve.wait_ge(sw["mbw_dma"], 6 * 16)
                    for k in range(DC):
                        nc.vector.tensor_tensor(w_conv[:, k, :], w_in[:, 0:DI], conv_row[:, k, :], ALU.mult)
                    nc.vector.tensor_scalar(conv_bh[:], vec[:, CB:CB + CH], 0.5, None, ALU.mult)
                    nc.vector.tensor_scalar(w_x[:], w_x[:], 0.5, None, ALU.mult)
                    nc.vector.tensor_scalar(w_out[:], w_out[:], 0.25, None, ALU.mult)
                    dve.wait_ge(sw["mbw_a"], 1)
                    nc.vector.tensor_scalar(a_neg[:], a_neg[:], -1.0, None, ALU.mult)
            sw.clear()

            with nc.Block() as block:
                @block.sync
                def _(sp):
                    sp.dma_start(r_tok[:], tile_rows(res, 1)).then_inc(sw["mbw_dma"], 16)
                    sp.wait_ge(sw["mbw_dma"], 16)
            sw.clear()
            first, fill = Ahead(0, behind=False), Scan(0)
            with nc.Block() as block:
                @block.sync
                def _(sp):
                    sp.wait_ge(s["mb_xh"], 1)
                    first.load(sp, 2)
                    sp.wait_ge(s["mb_res"], 16)

                @block.gpsimd
                def _(pool):
                    for n in range(-1, DS):
                        first.pool(pool, n)
                    for j in range(RING - 1):
                        fill.pool(pool, j)

                @block.scalar
                def _(act):
                    for n in range(-1, DS):
                        first.act(act, n)
                    for j in range(RING - 1):
                        fill.act(act, j)

                @block.vector
                def _(dve):
                    for n in range(-2, DS):
                        first.dve(dve, n)

                @block.tensor
                def _(pe):
                    for n in range(-1, DS):
                        first.pe(pe, n)
                    for j in range(RING - 1):
                        fill.spread_b(pe, j)
            s.clear()

            with nc.Fori(0, GROUPS // 2) as pairs:
                for q in range(2):
                    ahead, scan, behind = Ahead(1 - q), Scan(q, RING - 1, 1 - q), Behind(1 - q)
                    with nc.Block() as block:
                        @block.sync
                        def _(sp):
                            behind.fetch(sp, 2 * pairs + q)
                            sp.wait_ge(s["mb_xh"], 1)
                            ahead.load(sp, 2 * pairs + q + 3)
                            behind.store(sp, 2 * pairs + q)
                            sp.wait_ge(s["mb_res"], 16)

                        @block.gpsimd
                        def _(pool):
                            ahead.pool(pool, -1)
                            for n in range(DS):
                                scan.pool(pool, n)
                                ahead.pool(pool, n)

                        @block.scalar
                        def _(act):
                            scan.act(act, 0)
                            ahead.act(act, -1)
                            for n in range(DS):
                                if n:
                                    scan.act(act, n)
                                ahead.act(act, n)

                        @block.vector
                        def _(dve):
                            scan.scan(dve, 0)
                            ahead.dve(dve, -2)
                            behind.dve(dve, -1)
                            ahead.dve(dve, -1)
                            for n in range(DS):
                                if n + 1 < DS:
                                    scan.scan(dve, n + 1)
                                scan.read_out(dve, n)
                                behind.dve(dve, n)
                                ahead.dve(dve, n)

                        @block.tensor
                        def _(pe):
                            scan.spread_b(pe, 0)
                            scan.spread_c(pe, 0)
                            scan.spread_b(pe, 1)
                            behind.pe(pe, 0)
                            ahead.pe(pe, -1)
                            for n in range(DS):
                                if 1 < n + 1 < DS:
                                    scan.spread_b(pe, n + 1)
                                if n + 1 < DS:
                                    scan.spread_c(pe, n + 1)
                                scan.sum(pe, n)
                                ahead.pe(pe, n)
                    s.clear()

            last = Behind(1)
            with nc.Block() as block:
                @block.sync
                def _(sp):
                    last.fetch(sp, GROUPS)
                    last.store(sp, GROUPS)

                @block.vector
                def _(dve):
                    last.dve(dve, -1)
                    last.dve(dve, 2)

                @block.tensor
                def _(pe):
                    last.pe(pe, 0)
            s.clear()


def mamba_host(i):
    A = lambda k: np.asarray(i["L0_attn_" + k])
    xp = A("x_proj_w")
    xp = np.concatenate([xp[:, DR:], xp[:, :DR]], axis=1)
    ch = lambda a: a.reshape(NL, CH, P).transpose(0, 2, 1)
    vec = np.concatenate([
        A("norm_w")[:, :, None], A("norm_b")[:, :, None], ch(A("conv_b")), ch(A("dt_proj_b")), ch(A("D")),
        A("A_log").reshape(NL, CH, P, DS).transpose(0, 2, 1, 3).reshape(NL, P, CH * DS)], axis=2)
    return {
        "w_in": A("in_proj_w").transpose(0, 2, 1),
        "conv_row": A("conv_w").transpose(0, 2, 1),
        "w_x": xp.reshape(NL, 2 * DS + DR, CH, P).transpose(0, 3, 2, 1),
        "w_dt": A("dt_proj_w").transpose(0, 2, 1),
        "w_out": A("out_proj_w").reshape(NL, D, CH, P).transpose(0, 3, 2, 1),
        "vec": vec,
        "selcol": np.tile(np.eye(2 * DS, dtype=np.float32), (3, 1)),
    }

H, DK = 16, 8
NC = 77
HH = H // 2
VW = DK + 1
TOPK = 5
PAD = 4
LOW, PICKED = -3.0e38, -2.0e38
BIG = -1.0e9


class Prefixed:

    def __init__(self, s, prefix):
        self.s, self.prefix, self.nc = s, prefix, s.nc

    def __getitem__(self, name):
        return self.s[self.prefix + name]


class Norm:

    def __init__(self, sb, s, pre, half_neg):
        self.s, self.var, self.rst, self.half_neg = s, pre + "_var", pre + "_rstd", half_neg
        self.stats = sb(pre + "_stats", [P, GB, 6])
        self.mv = sb(pre + "_mv", [P, GB, 2])
        self.rstd = sb(pre + "_rs", [P, GB])
        self.on_dve = self.on_pool = 0

    def dve(self, dve, src, dst):
        nc = self.s.nc
        for b in range(GB):
            nc.vector.bn_stats(self.stats[:, b], src[:, b])
        dve.drain()
        for b in range(GB):
            nc.vector.bn_aggr(self.mv[:, b], self.stats[:, b])
        dve.drain()
        nc.vector.tensor_scalar(self.mv[:, :, 1], self.mv[:, :, 1], LN_EPS, None, ALU.add).then_inc(self.s[self.var], 1)
        self.on_dve += 1
        dve.wait_ge(self.s[self.rst], self.on_dve)
        for b in range(GB):
            last = nc.vector.tensor_scalar(dst[:, b], src[:, b], self.mv[:, b, 0:1], self.rstd[:, b:b + 1],
                                           ALU.subtract, ALU.mult)
        return last

    def pool(self, pool):
        self.on_pool += 1
        pool.wait_ge(self.s[self.var], self.on_pool)
        self.s.nc.gpsimd.tensor_tensor(self.rstd[:], self.mv[:, :, 1], self.half_neg[:], ALU.pow).then_inc(self.s[self.rst], 1)


class Flow:

    def __init__(self, nc, st, pre, s, loads, x_out, y_toks):
        self.nc, self.s, self.loads, self.x_out, self.y_toks = nc, s, loads, x_out, y_toks
        self.into = s[pre + "_loaded"]
        self.stored = st.enter_context(nc.semaphore(pre + "_stored"))

    def fetch(self, sp, q, g):
        for dst, src in self.loads(q, g):
            sp.dma_start(dst, src).then_inc(self.into, 16)
        return 16 * len(self.loads(q, g))

    def first(self):
        with self.nc.Block() as block:
            @block.sync
            def _(sp):
                count = self.fetch(sp, 0, 0)
                sp.dma_start(self.y_toks[1][:], self.loads(0, 0)[-1][1]).then_inc(self.stored, 16)
                sp.wait_ge(self.into, count)
                sp.wait_ge(self.stored, 16)
        self.s.clear()

    def sync(self, sp, pairs, q, out):
        g = 2 * pairs + q
        count = self.fetch(sp, 1 - q, g + 1)
        sp.wait_ge(self.stored, pairs * 32 + 16 * (q + 1))
        sp.wait_ge(out, 1)
        sp.dma_start(tile_rows(self.x_out, g), self.y_toks[q][:]).then_inc(self.stored, 16)
        sp.wait_ge(self.into, count)

    def last(self):
        with self.nc.Block() as block:
            @block.sync
            def _(sp):
                sp.wait_ge(self.stored, 16 * (GROUPS + 1))


ATTN_SEMS = ["km", "vx", "score", "shift", "exp", "tr", "pta", "ptv", "pv", "o", "otp", "ot", "proj",
             "cp", "mx", "mr", "pick"]


class Attention:

    UNITS = 2 * GB

    def __init__(self, nc, sb, s, pre, bank, ident, hmask, nk, scale, topk=False, bias=None):
        self.nc, self.s, self.bank, self.ident, self.hmask = nc, s, bank, ident, hmask
        self.nk, self.scale, self.topk, self.bias, self.pre = nk, scale, topk, bias, pre
        self.km = [sb(f"{pre}_km{i}", [P, H, nk]) for i in range(2)]
        self.e = [sb(f"{pre}_e{i}", [P, HH, nk]) for i in range(2)]
        self.mx = sb(pre + "_mx", [P, 2, HH])
        self.pt = [sb(f"{pre}_pt{i}", [nk, HH, P]) for i in range(2)]
        self.rs = sb(pre + "_rs", [P, H])
        self.o = sb(pre + "_o", [P, 2, D])
        self.ot = sb(pre + "_ot", [P, 2, D])
        if topk:
            self.sp = [sb(f"{pre}_sp{i}", [P, HH, nk + PAD]) for i in range(2)]
            self.mr = [sb(f"{pre}_mr{i}", [P, HH, nk + PAD]) for i in range(2)]
            self.m8 = sb(pre + "_m8", [P, 2, HH, 8])
            self.nb = sb(pre + "_nb", [P, 2, HH])
            self.m5 = sb(pre + "_m5", [P, HH, 8])

    def sem(self, name):
        return self.s[self.pre + "_" + name]

    def scores_at(self, u, j):
        return self.bank[:, 2 * (u % 2) + j, 0:4 * self.nk].rearrange("p (h k) -> p h k", h=4)

    def scores_of(self, u):
        return self.bank[:, 2 * (u % 2):2 * (u % 2) + 2, 0:4 * self.nk].rearrange("p j (h k) -> p j h k", h=4)

    def pool(self, pool, kT):
        nk = self.nk
        for b in range(GB):
            if b >= 2:
                pool.wait_ge(self.sem("score"), 2 * (b - 1))
            self.nc.gpsimd.tensor_tensor(self.km[b % 2][:], kT(b).unsqueeze(1).to_broadcast([P, H, nk]),
                                         self.hmask[:].unsqueeze(2).to_broadcast([P, H, nk]), ALU.mult).then_inc(self.sem("km"), 1)

    def pe(self, pe, qT, vx, w_o):
        nc, nk = self.nc, self.nk

        def scores(u):
            b, hf = divmod(u, 2)
            pe.wait_ge(self.sem("km"), b + 1)
            if u >= 2:
                pe.wait_ge(self.sem("cp" if self.topk else "shift"), u - 1)
            for j in range(2):
                h0 = hf * HH + 4 * j
                m = nc.tensor.matmul(self.scores_at(u, j), qT(b), self.km[b % 2][:, h0:h0 + 4, :],
                                     start=True, stop=self.bias is None)
                if self.bias is not None:
                    ones3, parts = self.bias
                    m = nc.tensor.matmul(self.scores_at(u, j), ones3[:], parts(b).unsqueeze(1).to_broadcast([3, 4, nk]),
                                         start=False, stop=True)
            m.then_inc(self.sem("score"), 1)

        def project(b):
            pe.wait_ge(self.sem("o"), b + 1)
            nc.tensor.transpose(self.bank[:, 7, 0:P], self.o[:, b % 2], self.ident[:]).then_inc(self.sem("otp"), 1)
            pe.wait_ge(self.sem("ot"), b + 1)
            nc.tensor.matmul(self.bank[:, 7, P:2 * P], self.ot[:, b % 2], w_o[:], start=True, stop=True).then_inc(self.sem("proj"), 1)

        def values(u):
            b, hf = divmod(u, 2)
            pe.wait_ge(self.sem("pta"), u + 1)
            pe.wait_ge(self.sem("ptv"), u + 1)
            if hf == 0 and b >= 1:
                pe.wait_ge(self.sem("o"), b)
            for h in range(HH):
                at = (hf * HH + h) * VW
                m = nc.tensor.matmul(self.bank[:, 6, at:at + VW], self.pt[u % 2][:, h], vx(b, hf * HH + h), start=True, stop=True)
            m.then_inc(self.sem("pv"), 1)

        scores(0)
        scores(1)
        for u in range(self.UNITS):
            if self.topk and u + 2 < self.UNITS:
                scores(u + 2)
            pe.wait_ge(self.sem("pick" if self.topk else "exp"), u + 1)
            if u:
                pe.wait_ge(self.sem("pta"), u)
                pe.wait_ge(self.sem("ptv"), u)
            for h in range(HH):
                m = nc.tensor.transpose(self.bank[0:nk, 4 + h // 4, (h % 4) * P:(h % 4 + 1) * P], self.e[u % 2][:, h], self.ident[:])
            m.then_inc(self.sem("tr"), 1)
            if not self.topk and u + 2 < self.UNITS:
                scores(u + 2)
            if u:
                values(u - 1)
            if u % 2 == 1 and u > 1:
                project(u // 2 - 1)
        values(self.UNITS - 1)
        project(GB - 1)

    def act(self, act):
        nc, nk = self.nc, self.nk

        def evac(u):
            act.wait_ge(self.sem("tr"), u + 1)
            if u >= 2:
                act.wait_ge(self.sem("pv"), u - 1)
            nc.scalar.activation(self.pt[u % 2][:, 0:4].rearrange("p h q -> p (h q)"), self.bank[0:nk, 4],
                                 ACT.Copy).then_inc(self.sem("pta"), 1)

        def copy_scores(u):
            act.wait_ge(self.sem("score"), u + 1)
            if u >= 2:
                act.wait_ge(self.sem("exp"), HH * (u - 1))
                act.wait_ge(self.sem("mr"), u - 1)
            nc.scalar.activation(self.sp[u % 2][:, :, 0:nk].rearrange("p (j h) k -> p j h k", j=2), self.scores_of(u),
                                 ACT.Copy).then_inc(self.sem("cp"), 1)

        def turned(b):
            act.wait_ge(self.sem("otp"), b + 1)
            nc.scalar.activation(self.ot[:, b % 2], self.bank[:, 7, 0:P], ACT.Copy).then_inc(self.sem("ot"), 1)

        if self.topk:
            copy_scores(0)
        for u in range(self.UNITS):
            if self.topk:
                if u + 1 < self.UNITS:
                    copy_scores(u + 1)
                act.wait_ge(self.sem("mx"), u + 1)
                act.wait_ge(self.sem("cp"), u + 1)
                if u >= 2:
                    act.wait_ge(self.sem("tr"), u - 1)
                for h in range(HH):
                    nc.scalar.activation(self.e[u % 2][:, h], self.sp[u % 2][:, h, 0:nk], ACT.Exp, scale=self.scale,
                                         bias=self.nb[:, u % 2, h:h + 1]).then_inc(self.sem("exp"), 1)
            else:
                act.wait_ge(self.sem("shift"), u + 1)
                nc.scalar.activation(self.e[u % 2][:], self.e[u % 2][:], ACT.Exp, scale=self.scale).then_inc(self.sem("exp"), 1)
            if u:
                evac(u - 1)
            if u % 2 == 0 and u > 2:
                turned(u // 2 - 2)
        evac(self.UNITS - 1)
        turned(GB - 2)
        turned(GB - 1)

    def dve(self, dve, after):
        nc, nk = self.nc, self.nk

        def evac(u):
            dve.wait_ge(self.sem("tr"), u + 1)
            if u >= 2:
                dve.wait_ge(self.sem("pv"), u - 1)
            nc.vector.tensor_copy(self.pt[u % 2][:, 4:8].rearrange("p h q -> p (h q)"), self.bank[0:nk, 5]).then_inc(self.sem("ptv"), 1)

        def largest(u):
            i = u % 2
            dve.wait_ge(self.sem("cp"), u + 1)
            for h in range(HH):
                nc.vector.max(self.m8[:, i, h], self.sp[i][:, h, 0:nk])
            dve.drain()
            if u >= 2:
                dve.wait_ge(self.sem("exp"), HH * (u - 1))
            nc.vector.tensor_scalar(self.nb[:, i], self.m8[:, i, :, 0], -self.scale, None, ALU.mult).then_inc(self.sem("mx"), 1)
            nc.vector.memset(self.m8[:, i, :, TOPK:], LOW)
            dve.drain()
            if u >= 2:
                dve.wait_ge(self.sem("pick"), u - 1)
            for h in range(HH):
                m = nc.vector.match_replace(self.mr[i][:, h], self.m8[:, i, h], self.sp[i][:, h], PICKED)
            m.then_inc(self.sem("mr"), 1)

        def normalise(b):
            heads = self.bank[:, 6, 0:H * VW].rearrange("p (h v) -> p h v", v=VW)
            dve.wait_ge(self.sem("pv"), 2 * b + 2)
            nc.vector.reciprocal(self.rs[:], heads[:, :, DK])
            if b >= 2:
                dve.wait_ge(self.sem("otp"), b - 1)
            dve.drain()
            nc.vector.tensor_tensor(self.o[:, b % 2].rearrange("p (h v) -> p h v", v=DK), heads[:, :, 0:DK],
                                    self.rs[:].unsqueeze(2).to_broadcast([P, H, DK]), ALU.mult).then_inc(self.sem("o"), 1)

        def finish(b):
            dve.wait_ge(self.sem("proj"), b + 1)
            after(b, self.bank[:, 7, P:2 * P])

        if self.topk:
            largest(0)
        for u in range(self.UNITS):
            i = u % 2
            if self.topk:
                if u + 1 < self.UNITS:
                    largest(u + 1)
                dve.wait_ge(self.sem("mr"), u + 1)
                dve.wait_ge(self.sem("exp"), HH * (u + 1))
                nc.vector.scalar_tensor_tensor(out=self.e[i][:], in0=self.mr[i][:, :, 0:nk], scalar=PICKED, in1=self.e[i][:],
                                               op0=ALU.is_equal, op1=ALU.mult).then_inc(self.sem("pick"), 1)
            else:
                dve.wait_ge(self.sem("score"), u + 1)
                nc.vector.tensor_reduce(self.mx[:, i].rearrange("p (j h) -> p j h", j=2), self.scores_of(u), AX.X, ALU.max)
                if u >= 2:
                    dve.wait_ge(self.sem("tr"), u - 1)
                dve.drain()
                nc.vector.tensor_tensor(self.e[i][:].rearrange("p (j h) k -> p j h k", j=2), self.scores_of(u),
                                        self.mx[:, i].rearrange("p (j h) -> p j h", j=2).unsqueeze(3).to_broadcast([P, 2, 4, nk]),
                                        ALU.subtract).then_inc(self.sem("shift"), 1)
            if u:
                evac(u - 1)
            if u % 2 == 1 and u > 1:
                normalise(u // 2 - 1)
            if u % 2 == 0 and u > 2:
                finish(u // 2 - 2)
        evac(self.UNITS - 1)
        finish(GB - 2)
        normalise(GB - 1)
        finish(GB - 1)


def row(ap, parts):
    return ap.unsqueeze(0).to_broadcast([parts, ap.shape[0]])


def ctx_rows(ap, g):
    v = ap.rearrange("(g b) t d -> g t b d", b=GB)
    return v[bass.ds(g, 1)].rearrange("g t b d -> (g t) b d")


def xattn_stage(nc, w, consts, x_in, res, ctx_in, mask_in, x_out):
    ident, hmask, half_neg = consts["ident"], consts["hmask"], consts["half_neg"]
    with ExitStack() as st:
        def sb(name, shape, dt=F32):
            return st.enter_context(nc.sbuf_tensor("xa_" + name, shape, dt))

        bank = st.enter_context(nc.psum_tensor("xa_bank", [P, 8, 512], F32))
        s = Sems(nc, st, ["xa_" + n for n in ["n_var", "n_rstd", "xt", "xts", "ct", "cts", "q", "qs", "k", "ks", "kb",
                                          "mk", "v", "vb", "out", "loaded"] + ["a_" + n for n in ATTN_SEMS]])

        p = Prefixed(s, "xa_")
        wq, wk, wv, wo = (sb(n, [P, D]) for n in ("wq", "wk", "wv", "wo"))
        vecs = sb("vecs", [P, 2])
        rows = sb("rows", [P, 4, D])
        part = sb("part", [3, 1])
        ones3 = sb("ones3", [3, P], BF16)
        z_tok = sb("z_tok", [P, GB, D])
        r_toks, x_toks, y_toks = ([sb(f"{n}{i}", [P, GB, D]) for i in range(2)] for n in ("r_tok", "x_tok", "y_tok"))
        c_toks = [sb(f"c_tok{i}", [NC, GB, D]) for i in range(2)]
        m_ints = [sb(f"m_int{i}", [P, GB, NC], I32) for i in range(2)]
        xT, qT = sb("xT", [P, GB, SEQ]), sb("qT", [P, GB, SEQ])
        cT, kT = sb("cT", [P, GB, NC]), sb("kT", [P, GB, NC])
        keep = sb("keep", [P, GB, NC])
        mbias = sb("mbias", [3, GB, NC], BF16)
        vx = sb("vx", [NC, GB, H, VW])
        norm = Norm(sb, p, "n", half_neg)
        flow = Flow(nc, st, "xa", s, lambda q, g: [
            (c_toks[q][:], ctx_rows(ctx_in, g)),
            (m_ints[q][:].rearrange("p b k -> p (b k)"),
             mask_in.rearrange("(g b) k -> g (b k)", b=GB)[bass.ds(g, 1)].to_broadcast([P, GB * NC])),
            (r_toks[q][:], tile_rows(res, g)), (x_toks[q][:], tile_rows(x_in, g))], x_out, y_toks)
        at = Attention(nc, sb, p, "a", bank, ident, hmask, NC, DK ** -0.5, bias=(ones3, lambda b: mbias[:, b]))

        s0 = Sems(nc, st, ["xa0_w"])
        with nc.Block() as block:
            @block.sync
            def _(sp):
                loads = [(wq, w["wq"]), (wk, w["wk"]), (wv, w["wv"]), (wo, w["wo"]), (vecs, w["vecs"]), (part, w["part"])]
                for t, d in loads:
                    sp.dma_start(t[:], d).then_inc(s0["xa0_w"], 16)
                sp.dma_start(rows[:].rearrange("p r d -> p (r d)"), w["rows"].rearrange("r d -> (r d)").unsqueeze(0)
                             .to_broadcast([P, 4 * D])).then_inc(s0["xa0_w"], 16)
                sp.wait_ge(s0["xa0_w"], 16 * (len(loads) + 1))

            @block.vector
            def _(dve):
                nc.vector.memset(ones3[:], 1.0)
                nc.vector.memset(vx[:], 1.0)
        s0.clear()

        flow.first()
        with nc.Fori(0, GROUPS // 2) as pairs:
            for q in range(2):
                r_tok, x_tok, y_tok, c_tok, m_int = r_toks[q], x_toks[q], y_toks[q], c_toks[q], m_ints[q]
                norm.on_dve = norm.on_pool = 0
                with nc.Block() as block:
                    @block.sync
                    def _(sp):
                        flow.sync(sp, pairs, q, p["out"])

                    @block.gpsimd
                    def _(pool):
                        norm.pool(pool)
                        norm.pool(pool)
                        pool.wait_ge(p["kb"], 1)
                        at.pool(pool, lambda b: kT[:, b])
                        norm.pool(pool)

                    @block.tensor
                    def _(pe):
                        for b in range(GB):
                            m = nc.tensor.transpose(bank[:, 0, b * NC:(b + 1) * NC], c_tok[:, b], ident[0:NC, 0:NC])
                        m.then_inc(p["ct"], 1)
                        pe.wait_ge(p["cts"], 1)
                        nc.tensor.matmul(bank[:, 1, 0:GB * NC], wk[:], cT[:], start=True, stop=True).then_inc(p["k"], 1)
                        for b in range(GB):
                            m = nc.tensor.matmul(bank[0:NC, 2, b * D:(b + 1) * D], cT[:, b], wv[:], start=True, stop=True)
                        m.then_inc(p["v"], 1)
                        pe.wait_ge(p["xt"], 1)
                        for b in range(GB):
                            m = nc.tensor.transpose(bank[:, 3, b * P:(b + 1) * P], x_tok[:, b], ident[:])
                        m.then_inc(p["xts"], 1)
                        pe.wait_ge(p["q"], 1)
                        nc.tensor.matmul(bank[:, 4], wq[:], xT[:].rearrange("p b t -> p (b t)"), start=True, stop=True).then_inc(p["q"], 1)
                        pe.wait_ge(p["qs"], 1)
                        pe.wait_ge(p["ks"], 1)
                        pe.wait_ge(p["vb"], 1)
                        pe.wait_ge(p["mk"], 1)
                        at.pe(pe, lambda b: qT[:, b], lambda b, h: vx[:, b, h], wo)

                    @block.scalar
                    def _(act):
                        act.wait_ge(p["ct"], 1)
                        nc.scalar.activation(cT[:].rearrange("p b k -> p (b k)"), bank[:, 0, 0:GB * NC], ACT.Copy).then_inc(p["cts"], 1)
                        act.wait_ge(p["k"], 1)
                        nc.scalar.activation(kT[:].rearrange("p b k -> p (b k)"), bank[:, 1, 0:GB * NC], ACT.Identity,
                                             bias=vecs[:, 1:2]).then_inc(p["ks"], 1)
                        act.wait_ge(p["xts"], 1)
                        nc.scalar.activation(xT[:].rearrange("p b t -> p (b t)"), bank[:, 3], ACT.Copy).then_inc(p["q"], 1)
                        act.wait_ge(p["q"], 2)
                        nc.scalar.activation(qT[:].rearrange("p b t -> p (b t)"), bank[:, 4], ACT.Identity,
                                             bias=vecs[:, 0:1]).then_inc(p["qs"], 1)
                        at.act(act)

                    @block.vector
                    def _(dve):
                        norm.dve(dve, r_tok, z_tok)
                        dve.drain()
                        nc.vector.tensor_tensor(z_tok[:], z_tok[:], rows[:, 0].unsqueeze(1).to_broadcast([P, GB, D]), ALU.mult)
                        nc.vector.tensor_tensor(r_tok[:], x_tok[:], rows[:, 1].unsqueeze(1).to_broadcast([P, GB, D]), ALU.add)
                        dve.drain()
                        nc.vector.tensor_tensor(z_tok[:], z_tok[:], r_tok[:], ALU.add)
                        dve.drain()
                        norm.dve(dve, z_tok, x_tok).then_inc(p["xt"], 1)
                        nc.vector.tensor_scalar(keep[:], m_int[:], 0.0, None, ALU.not_equal)
                        dve.drain()
                        nc.vector.tensor_scalar(mbias[:], keep[0:3], 1.0, part[:, 0:1], ALU.subtract, ALU.mult).then_inc(p["mk"], 1)
                        dve.wait_ge(p["ks"], 1)
                        nc.vector.tensor_tensor(kT[:], kT[:], keep[:], ALU.mult).then_inc(p["kb"], 1)
                        dve.wait_ge(p["v"], 1)
                        nc.vector.tensor_tensor(vx[:, :, :, 0:DK], bank[0:NC, 2].rearrange("p (b h v) -> p b h v", b=GB, h=H),
                                                rows[0:NC, 2].rearrange("p (h v) -> p h v", h=H).unsqueeze(1).to_broadcast([NC, GB, H, DK]),
                                                ALU.add).then_inc(p["vb"], 1)
                        nc.vector.tensor_tensor(z_tok[:], x_tok[:], rows[:, 3].unsqueeze(1).to_broadcast([P, GB, D]), ALU.add)
                        dve.drain()

                        def add(b, psum):
                            nc.vector.tensor_tensor(r_tok[:, b], z_tok[:, b], psum, ALU.add)
                        at.dve(dve, add)
                        dve.drain()
                        norm.dve(dve, r_tok, y_tok).then_inc(p["out"], 1)
                s.clear()
        flow.last()


def bf16_parts(v, n=3):
    out, rest = [], np.float32(v)
    for _ in range(n):
        bits = np.array([rest], np.float32).view(np.uint32) & np.uint32(0xFFFF0000)
        hi = bits.view(np.float32)[0]
        out.append(hi)
        rest = np.float32(rest - hi)
    return np.array(out, np.float32)


def xattn_host(i):
    A = lambda k: np.asarray(i["L0_xattn_" + k])
    return {"wq": A("wq").T, "wk": A("wk").T, "wv": A("wv").T, "wo": A("wo").T,
            "vecs": np.stack([A("bq"), A("bk")], 1),
            "rows": np.stack([np.asarray(i["L0_attn_normf_w"]), np.asarray(i["L0_attn_normf_b"]), A("bv"), A("bo")]),
            "part": -bf16_parts(BIG)[:, None]}

PH, NK, KD, EXPERTS = 8, 128, 64, 2048
FI = 2 * D
ROW = 2 * D + 2 * FI
IA, IB, OA, OB = 0, D, D + FI, D + 2 * FI


PER_TILE = 16 * PH


def experts_stage(nc, w, consts, x_in, x_out):
    ident, half_neg = consts["ident"], consts["half_neg"]
    with ExitStack() as st:
        def sb(name, shape, dt=F32):
            return st.enter_context(nc.sbuf_tensor("ex_" + name, shape, dt))

        bank = st.enter_context(nc.psum_tensor("ex_bank", [P, 8, 512], F32))
        s = Sems(nc, st, ["ex_" + n for n in [
            "n_var", "n_rstd", "in", "xt", "xts", "sim", "top", "idx", "lin", "dgi", "hid", "gelu", "ht",
            "hts", "lout", "dgo", "y", "sum", "out"]])
        p = Prefixed(s, "ex_")
        got = [st.enter_context(nc.semaphore(f"ex_got{b}")) for b in range(GB)]
        w_sim = sb("w_sim", [P, 2 * PH, NK])
        w_in = sb("w_in", [P, FI])
        w_out = sb("w_out", [P, 2, D])
        x_tok = [sb(f"x_tok{i}", [P, GB, D]) for i in range(2)]
        y_toks = [sb(f"y_tok{i}", [P, GB, D]) for i in range(2)]
        xT = [sb(f"xT{i}", [P, GB, SEQ]) for i in range(2)]
        m8 = sb("m8", [P, 2 * PH, 8])
        i8 = sb("i8", [P, 2 * PH, 8], U32)
        iy = sb("iy", [P, PH])
        idx = [sb(f"idx{b}", [P, PH], U32) for b in range(GB)]
        gate = [sb(f"gate{i}", [P, GB, PH]) for i in range(2)]
        rowsb = [sb(f"rows{b}", [P, PH, ROW]) for b in range(GB)]
        junk = sb("junk", [P, PH, FI])
        lin, lout = sb("lin", [P, PH]), sb("lout", [P, PH])
        dg_in = sb("dg_in", [P, PH, P])
        dg_out = sb("dg_out", [P, PH, P])
        hid = sb("hid", [P, FI])
        hidT = sb("hidT", [P, 2, P])
        norm = Norm(sb, p, "n", half_neg)
        stored = st.enter_context(nc.semaphore("ex_stored"))

        s0 = Sems(nc, st, ["ex0_w", "ex0_m", "ex0_c"])
        wq = rowsb[0][0:KD, 0:4, 0:4 * D].rearrange("p a (b d) -> p a b d", b=4)
        keys = rowsb[1][0:KD, 0:4, 0:4 * NK].rearrange("p a (b d) -> p a b d", b=4)
        with nc.Block() as block:
            @block.sync
            def _(sp):
                for t, d in ((wq, w["wq"].rearrange("p (a b) d -> p a b d", b=4)), (keys, w["keys"].rearrange("p (a b) d -> p a b d", b=4)),
                             (w_in[:], w["w_in"]), (w_out[:], w["w_out"])):
                    sp.dma_start(t, d).then_inc(s0["ex0_w"], 16)

            @block.tensor
            def _(pe):
                pe.wait_ge(s0["ex0_w"], 64)
                for j in range(2 * PH):
                    m = nc.tensor.matmul(bank[:, j // 4, (j % 4) * P:(j % 4 + 1) * P], wq[:, j // 4, j % 4], keys[:, j // 4, j % 4], start=True, stop=True)
                m.then_inc(s0["ex0_m"], 1)

            @block.scalar
            def _(act):
                act.wait_ge(s0["ex0_m"], 1)
                nc.scalar.activation(w_sim[:].rearrange("p (a h) k -> p a (h k)", a=4), bank[:, 0:4], ACT.Copy)
        s0.clear()

        class Search:
            def __init__(self, q):
                self.q = q

            def load(self, sp, g):
                sp.dma_start(x_tok[self.q][:], tile_rows(x_in, g)).then_inc(p["in"], 16)

            def turn(self, pe):
                pe.wait_ge(p["in"], 16)
                for b in range(GB):
                    m = nc.tensor.transpose(bank[:, 7, b * P:(b + 1) * P], x_tok[self.q][:, b], ident[:])
                m.then_inc(p["xt"], 1)

            def turned(self, act):
                act.wait_ge(p["xt"], 1)
                nc.scalar.activation(xT[self.q][:].rearrange("p b t -> p (b t)"), bank[:, 7], ACT.Copy).then_inc(p["xts"], 1)

            def sims(self, pe, b):
                if b == 0:
                    pe.wait_ge(p["xts"], 1)
                for j in range(4):
                    if b:
                        pe.wait_ge(p["top"], 4 * (b - 1) + j + 1)
                    nc.tensor.matmul(bank[:, j], xT[self.q][:, b], w_sim[:, 4 * j:4 * j + 4], start=True, stop=True).then_inc(p["sim"], 1)

            def top(self, dve, b):
                gates = gate[self.q][:, b]
                for j in range(4):
                    dve.wait_ge(p["sim"], 4 * b + j + 1)
                    for k in range(4):
                        nc.vector.max(m8[:, 4 * j + k], bank[:, j, k * NK:(k + 1) * NK])
                    dve.drain()
                    for k in range(4):
                        m = nc.vector.max_index(i8[:, 4 * j + k], m8[:, 4 * j + k], bank[:, j, k * NK:(k + 1) * NK])
                    m.then_inc(p["top"], 1)
                dve.drain()
                nc.vector.tensor_tensor(gates, m8[:, 0:PH, 0], m8[:, PH:, 0], ALU.add)
                nc.vector.tensor_copy(iy[:], i8[:, PH:, 0])
                dve.drain()
                nc.vector.tensor_scalar(gates, gates, 0.0, None, ALU.max)
                nc.vector.scalar_tensor_tensor(out=iy[:], in0=i8[:, 0:PH, 0], scalar=float(NK), in1=iy[:],
                                               op0=ALU.mult, op1=ALU.add)
                dve.drain()
                nc.vector.tensor_scalar(idx[b][:], iy[:], float(EXPERTS - 1), None, ALU.min).then_inc(p["idx"], 1)

        def gather(b):
            for h in range(PH):
                nc.gpsimd.indirect_dma_start(rowsb[b][:, h], None, w["table"],
                                             bass.IndirectOffsetOnAxis(idx[b][:, h:h + 1], 0)).then_inc(got[b], 16)

        first = Search(0)
        with nc.Block() as block:
            @block.sync
            def _(sp):
                first.load(sp, 0)
                sp.dma_start(y_toks[1][:], tile_rows(x_in, 0)).then_inc(stored, 16)
                sp.wait_ge(stored, 16)

            @block.gpsimd
            def _(pool):
                for b in range(GB - 1):
                    pool.wait_ge(p["idx"], b + 1)
                    gather(b)

            @block.tensor
            def _(pe):
                first.turn(pe)
                for b in range(GB):
                    first.sims(pe, b)

            @block.scalar
            def _(act):
                first.turned(act)

            @block.vector
            def _(dve):
                for b in range(GB):
                    first.top(dve, b)
        s.clear()

        with nc.Fori(0, GROUPS // 2) as pairs:
            for q in range(2):
                norm.on_dve = norm.on_pool = 0
                search = Search(1 - q)
                x, xt, gates, y_tok = x_tok[q], xT[q], gate[q], y_toks[q]
                with nc.Block() as block:
                    @block.sync
                    def _(sp):
                        search.load(sp, 2 * pairs + q + 1)
                        sp.wait_ge(stored, pairs * 32 + 16 * (q + 1))
                        sp.wait_ge(p["out"], 1)
                        sp.dma_start(tile_rows(x_out, 2 * pairs + q), y_tok[:]).then_inc(stored, 16)

                    @block.gpsimd
                    def _(pool):
                        gather(GB - 1)
                        for b in range(GB - 1):
                            pool.wait_ge(p["idx"], b + 1)
                            pool.wait_ge(p["y"], b + 1)
                            gather(b)
                        norm.pool(pool)

                    @block.tensor
                    def _(pe):
                        def hidden(b):
                            if b:
                                pe.wait_ge(p["gelu"], b)
                            pe.wait_ge(p["dgi"], b + 1)
                            nc.tensor.matmul(bank[:, 4, 0:FI], xt[:, b], w_in[:], start=True, stop=False)
                            for h in range(PH):
                                m = nc.tensor.matmul(bank[:, 4, 0:FI], dg_in[:, h], rowsb[b][:, h, IB:IB + FI], start=False, stop=(h == PH - 1))
                            m.then_inc(p["hid"], 1)

                        def hidden_turned(b):
                            pe.wait_ge(p["gelu"], b + 1)
                            if b:
                                pe.wait_ge(p["hts"], b)
                            for c in range(2):
                                m = nc.tensor.transpose(bank[:, 5, c * P:(c + 1) * P], hid[:, c * P:(c + 1) * P], ident[:])
                            m.then_inc(p["ht"], 1)

                        def outer(b):
                            pe.wait_ge(p["hts"], b + 1)
                            pe.wait_ge(p["dgo"], b + 1)
                            if b:
                                pe.wait_ge(p["sum"], b)
                            for c in range(2):
                                nc.tensor.matmul(bank[:, 6, 0:D], hidT[:, c], w_out[:, c], start=(c == 0), stop=False)
                            for h in range(PH):
                                m = nc.tensor.matmul(bank[:, 6, 0:D], dg_out[:, h], rowsb[b][:, h, OB:OB + D], start=False, stop=(h == PH - 1))
                            m.then_inc(p["y"], 1)

                        search.turn(pe)
                        search.sims(pe, 0)
                        for b in range(GB):
                            hidden(b)
                            if b + 1 < GB:
                                search.sims(pe, b + 1)
                            hidden_turned(b)
                            outer(b)

                    @block.scalar
                    def _(act):
                        search.turned(act)
                        for b in range(GB):
                            act.wait_ge(p["lin"], b + 1)
                            if b:
                                act.wait_ge(p["hid"], b)
                            for h in range(PH):
                                m = nc.scalar.activation(dg_in[:, h], ident[:], ACT.Copy, scale=lin[:, h:h + 1])
                            m.then_inc(p["dgi"], 1)
                            act.wait_ge(p["hid"], b + 1)
                            if b:
                                act.wait_ge(p["ht"], b)
                                act.wait_ge(p["lout"], b)
                            nc.scalar.activation(hid[:], bank[:, 4, 0:FI], ACT.Gelu).then_inc(p["gelu"], 1)
                            act.wait_ge(p["ht"], b + 1)
                            if b:
                                act.wait_ge(p["y"], b)
                            nc.scalar.activation(hidT[:].rearrange("p c t -> p (c t)"), bank[:, 5, 0:2 * P], ACT.Copy).then_inc(p["hts"], 1)
                            act.wait_ge(p["lout"], b + 1)
                            for h in range(PH):
                                m = nc.scalar.activation(dg_out[:, h], ident[:], ACT.Copy, scale=lout[:, h:h + 1])
                            m.then_inc(p["dgo"], 1)

                    @block.vector
                    def _(dve):
                        def weights_in(b):
                            dve.wait_ge(got[b], pairs * (2 * PER_TILE) + PER_TILE * (q + 1))
                            if b:
                                dve.wait_ge(p["dgi"], b)
                            nc.vector.tensor_tensor(junk[:, :, 0:D], rowsb[b][:, :, IA:IA + D], x[:, b].unsqueeze(1).to_broadcast([P, PH, D]), ALU.mult)
                            dve.drain()
                            nc.vector.tensor_reduce(lin[:], junk[:, :, 0:D], AX.X, ALU.add)
                            dve.drain()
                            nc.vector.tensor_tensor(lin[:], lin[:], gates[:, b], ALU.mult).then_inc(p["lin"], 1)

                        def weights_out(b):
                            dve.wait_ge(p["gelu"], b + 1)
                            if b:
                                dve.wait_ge(p["dgo"], b)
                            dve.drain()
                            nc.vector.tensor_tensor(junk[:], rowsb[b][:, :, OA:OA + FI], hid[:].unsqueeze(1).to_broadcast([P, PH, FI]), ALU.mult)
                            dve.drain()
                            nc.vector.tensor_reduce(lout[:], junk[:], AX.X, ALU.add)
                            dve.drain()
                            nc.vector.tensor_tensor(lout[:], lout[:], gates[:, b], ALU.mult).then_inc(p["lout"], 1)

                        def residual(b):
                            dve.wait_ge(p["y"], b + 1)
                            nc.vector.tensor_tensor(y_tok[:, b], x[:, b], bank[:, 6, 0:D], ALU.add).then_inc(p["sum"], 1)

                        weights_in(0)
                        for b in range(GB):
                            search.top(dve, b)
                            weights_out(b)
                            if b + 1 < GB:
                                weights_in(b + 1)
                            residual(b)
                        dve.drain()
                        norm.dve(dve, y_tok, y_tok).then_inc(p["out"], 1)
                s.clear()

        with nc.Block() as block:
            @block.sync
            def _(sp):
                sp.wait_ge(stored, 16 * (GROUPS + 1))

            @block.gpsimd
            def _(pool):
                for b in range(GB - 1):
                    pool.wait_ge(got[b], PER_TILE * (GROUPS + 1))


def experts_host(i):
    A = lambda k: np.asarray(i["L0_ffn_" + k])
    return {"wq": A("Wq").reshape(2 * PH, KD, D).transpose(1, 0, 2),
            "keys": A("keys").transpose(3, 2, 0, 1).reshape(KD, 2 * PH, NK),
            "w_in": A("W_in").T, "w_out": A("W_out").T.reshape(2, P, D).transpose(1, 0, 2),
            "table": np.concatenate([A("in_a"), A("in_b"), A("out_a"), A("out_b")], axis=1)}

GN, WIN = 64, 8
GUIDE = 0.4
EPS_MAG, EPS_COS, EPS_WSUM = 1e-6, 1e-8, 1e-8


def trajectory_stage(nc, w, consts, x_in, x_out):
    ident, half_neg = consts["ident"], consts["half_neg"]
    with ExitStack() as st:
        def sb(name, shape, dt=F32):
            return st.enter_context(nc.sbuf_tensor("tj_" + name, shape, dt))

        bank = st.enter_context(nc.psum_tensor("tj_bank", [P, 8, 512], F32))
        s = Sems(nc, st, ["tj_" + n for n in [
            "n_var", "n_rstd", "diff", "ds", "sq", "mag", "nrm", "sq2", "mag2", "mw", "nt", "nts", "sim", "sh",
            "ex", "gw", "gt", "gts", "inf", "cb", "tr", "out", "loaded"]])
        p = Prefixed(s, "tj_")
        shiftm, band = sb("shiftm", [P, P]), sb("band", [P, P])
        guide = sb("guide", [GN, D])
        gsq = sb("gsq", [GN, D])
        gr = sb("gr", [GN, 1])
        gr2 = sb("gr2", [GN, 1])
        half = sb("half", [P, GB])
        gnT = sb("gnT", [P, GN])
        x_toks, y_toks = ([sb(f"{n}{i}", [P, GB, D]) for i in range(2)] for n in ("x_tok", "y_tok"))
        flow = Flow(nc, st, "tj", s, lambda q, g: [(x_toks[q][:], tile_rows(x_in, g))], x_out, y_toks)
        diff, nrm, sq = sb("diff", [P, GB, D]), sb("nrm", [P, GB, D]), sb("sq", [P, GB, D])
        m2, mag, ok, t4, inv, a2, an, mx, mw, sm = (sb(n, [P, GB]) for n in
                                                    ("m2", "mag", "ok", "t4", "inv", "a2", "an", "mx", "mw", "sm"))
        nT = sb("nT", [P, GB, P])
        sim = sb("sim", [P, GB, GN])
        gwT = sb("gwT", [GN, GB, P])
        cb = sb("cb", [P, GB, D])
        ws = sb("ws", [P, GB])
        norm = Norm(sb, p, "n", half_neg)

        s0 = Sems(nc, st, ["tj0_w", "tj0_a", "tj0_b", "tj0_c", "tj0_d"])
        with nc.Block() as block:
            @block.sync
            def _(sp):
                for t, d in ((shiftm, w["shiftm"]), (band, w["band"]), (guide, w["guide"])):
                    sp.dma_start(t[:], d).then_inc(s0["tj0_w"], 16)

            @block.vector
            def _(dve):
                nc.vector.memset(half[:], 0.5)
                dve.wait_ge(s0["tj0_w"], 48)
                nc.vector.tensor_tensor(gsq[:], guide[:], guide[:], ALU.mult)
                dve.drain()
                nc.vector.tensor_reduce(gr[:], gsq[:], AX.X, ALU.add).then_inc(s0["tj0_a"], 1)
                dve.wait_ge(s0["tj0_b"], 1)
                nc.vector.tensor_scalar(gr2[:], gr2[:], EPS_COS, None, ALU.max)
                dve.drain()
                nc.vector.reciprocal(gr[:], gr2[:])
                dve.drain()
                nc.vector.tensor_scalar(gsq[:], guide[:], gr[:, 0:1], None, ALU.mult).then_inc(s0["tj0_c"], 1)

            @block.gpsimd
            def _(pool):
                pool.wait_ge(s0["tj0_a"], 1)
                nc.gpsimd.tensor_tensor(gr2[:], gr[:], half[0:GN, 0:1], ALU.pow).then_inc(s0["tj0_b"], 1)

            @block.tensor
            def _(pe):
                pe.wait_ge(s0["tj0_c"], 1)
                nc.tensor.transpose(bank[:, 0, 0:GN], gsq[:], ident[0:GN, 0:GN]).then_inc(s0["tj0_d"], 1)

            @block.scalar
            def _(act):
                act.wait_ge(s0["tj0_d"], 1)
                nc.scalar.activation(gnT[:], bank[:, 0, 0:GN], ACT.Copy)
        s0.clear()

        def flat(t):
            return t[:].rearrange("p b d -> p (b d)")

        def wide(t, n=D):
            return t[:].unsqueeze(2).to_broadcast([P, GB, n])

        flow.first()
        with nc.Fori(0, GROUPS // 2) as pairs:
            for q in range(2):
                x_tok, y_tok = x_toks[q], y_toks[q]
                norm.on_dve = norm.on_pool = 0
                with nc.Block() as block:
                    @block.sync
                    def _(sp):
                        flow.sync(sp, pairs, q, p["out"])

                    @block.gpsimd
                    def _(pool):
                        pool.wait_ge(p["sq"], 1)
                        nc.gpsimd.tensor_tensor(mag[:], m2[:], half[:], ALU.pow).then_inc(p["mag"], 1)
                        pool.wait_ge(p["sq2"], 1)
                        nc.gpsimd.tensor_tensor(an[:], a2[:], half[:], ALU.pow).then_inc(p["mag2"], 1)
                        norm.pool(pool)

                    @block.tensor
                    def _(pe):
                        nc.tensor.matmul(bank[:, 0], shiftm[:], flat(x_tok), start=True, stop=True).then_inc(p["diff"], 1)
                        pe.wait_ge(p["nrm"], 1)
                        for b in range(GB):
                            m = nc.tensor.transpose(bank[:, 1, b * P:(b + 1) * P], nrm[:, b], ident[:])
                        m.then_inc(p["nt"], 1)
                        pe.wait_ge(p["nts"], 1)
                        for b in range(GB):
                            m = nc.tensor.matmul(bank[:, 2, b * GN:(b + 1) * GN], nT[:, b], gnT[:], start=True, stop=True)
                        m.then_inc(p["sim"], 1)
                        pe.wait_ge(p["gw"], 1)
                        for b in range(GB):
                            m = nc.tensor.transpose(bank[0:GN, 3, b * P:(b + 1) * P], sim[:, b], ident[:])
                        m.then_inc(p["gt"], 1)
                        pe.wait_ge(p["gts"], 1)
                        for b in range(GB):
                            m = nc.tensor.matmul(bank[:, 4, b * D:(b + 1) * D], gwT[:, b], guide[:], start=True, stop=True)
                        m.then_inc(p["inf"], 1)
                        pe.wait_ge(p["cb"], 1)
                        nc.tensor.matmul(bank[:, 5], band[:], flat(cb), start=True, stop=True)
                        nc.tensor.matmul(bank[:, 6, 0:GB], band[:], mw[:], start=True, stop=True).then_inc(p["tr"], 1)

                    @block.scalar
                    def _(act):
                        act.wait_ge(p["diff"], 1)
                        nc.scalar.activation(flat(diff), bank[:, 0], ACT.Copy).then_inc(p["ds"], 1)
                        act.wait_ge(p["mag"], 1)
                        nc.scalar.activation(mw[:], mag[:], ACT.Tanh, scale=2.0).then_inc(p["mw"], 1)
                        act.wait_ge(p["nt"], 1)
                        nc.scalar.activation(flat(nT), bank[:, 1], ACT.Copy).then_inc(p["nts"], 1)
                        act.wait_ge(p["sh"], 1)
                        nc.scalar.activation(flat(sim), flat(sim), ACT.Exp, scale=2.0).then_inc(p["ex"], 1)
                        act.wait_ge(p["gt"], 1)
                        nc.scalar.activation(flat(gwT), bank[0:GN, 3], ACT.Copy).then_inc(p["gts"], 1)

                    @block.vector
                    def _(dve):
                        dve.wait_ge(p["ds"], 1)
                        nc.vector.tensor_tensor(sq[:], diff[:], diff[:], ALU.mult)
                        dve.drain()
                        nc.vector.tensor_reduce(m2[:], sq[:], AX.X, ALU.add).then_inc(p["sq"], 1)
                        dve.wait_ge(p["mag"], 1)
                        nc.vector.tensor_scalar(ok[:], mag[:], EPS_MAG, None, ALU.is_gt)
                        dve.drain()
                        nc.vector.tensor_tensor(t4[:], mag[:], ok[:], ALU.mult)
                        nc.vector.tensor_scalar(inv[:], ok[:], -1.0, 1.0, ALU.mult, ALU.add)
                        dve.drain()
                        nc.vector.tensor_tensor(t4[:], t4[:], inv[:], ALU.add)
                        dve.drain()
                        nc.vector.reciprocal(inv[:], t4[:])
                        dve.drain()
                        nc.vector.tensor_tensor(inv[:], inv[:], ok[:], ALU.mult)
                        dve.drain()
                        nc.vector.tensor_tensor(nrm[:], diff[:], wide(inv), ALU.mult).then_inc(p["nrm"], 1)
                        dve.drain()
                        nc.vector.tensor_tensor(sq[:], nrm[:], nrm[:], ALU.mult)
                        dve.drain()
                        nc.vector.tensor_reduce(a2[:], sq[:], AX.X, ALU.add).then_inc(p["sq2"], 1)
                        dve.wait_ge(p["mag2"], 1)
                        nc.vector.tensor_scalar(an[:], an[:], EPS_COS, None, ALU.max)
                        dve.drain()
                        nc.vector.reciprocal(a2[:], an[:])
                        dve.drain()
                        dve.wait_ge(p["sim"], 1)
                        nc.vector.tensor_tensor(sim[:], bank[:, 2, 0:GB * GN].rearrange("p (b k) -> p b k", b=GB), wide(a2, GN), ALU.mult)
                        dve.drain()
                        nc.vector.tensor_reduce(mx[:], sim[:], AX.X, ALU.max)
                        dve.drain()
                        nc.vector.tensor_tensor(sim[:], sim[:], wide(mx, GN), ALU.subtract).then_inc(p["sh"], 1)
                        dve.wait_ge(p["ex"], 1)
                        nc.vector.tensor_reduce(sm[:], sim[:], AX.X, ALU.add)
                        dve.drain()
                        nc.vector.reciprocal(mx[:], sm[:])
                        dve.drain()
                        nc.vector.tensor_tensor(sim[:], sim[:], wide(mx, GN), ALU.mult).then_inc(p["gw"], 1)
                        nc.vector.tensor_scalar(sq[:], nrm[:], 1.0 - GUIDE, None, ALU.mult)
                        dve.drain()
                        dve.wait_ge(p["inf"], 1)
                        nc.vector.scalar_tensor_tensor(out=flat(sq), in0=bank[:, 4], scalar=GUIDE, in1=flat(sq), op0=ALU.mult, op1=ALU.add)
                        dve.drain()
                        dve.wait_ge(p["mw"], 1)
                        nc.vector.tensor_tensor(cb[:], sq[:], wide(mw), ALU.mult).then_inc(p["cb"], 1)
                        dve.wait_ge(p["tr"], 1)
                        nc.vector.tensor_scalar(ws[:], bank[:, 6, 0:GB], EPS_WSUM, None, ALU.max)
                        dve.drain()
                        nc.vector.reciprocal(sm[:], ws[:])
                        dve.drain()
                        nc.vector.tensor_tensor(cb[:], bank[:, 5].rearrange("p (b d) -> p b d", b=GB), wide(sm), ALU.mult)
                        dve.drain()
                        nc.vector.tensor_tensor(sq[:], cb[:], x_tok[:], ALU.add)
                        dve.drain()
                        norm.dve(dve, sq, y_tok).then_inc(p["out"], 1)
                s.clear()
        flow.last()


def trajectory_host(i):
    shift = np.zeros((SEQ, SEQ), np.float32)
    band = np.zeros((SEQ, SEQ), np.float32)
    for j in range(SEQ - 1):
        shift[j + 1, j], shift[j, j] = 1.0, -1.0
    for pos in range(1, SEQ):
        width = min(pos, WIN)
        for k in range(WIN):
            j, at = k - (WIN - width), pos - WIN + k
            if at >= 0:
                band[at, pos] = 0.1 + 0.9 * j / max(width - 1, 1) if width > 1 else 0.1
    return {"shiftm": shift, "band": band, "guide": np.asarray(i["L1_attn_guidance_trajectories"])}

FF, FC = 512, 512 // P


def decoder_stage(nc, w, consts, x_in, ctx_in, x_out):
    ident, hmask, half_neg = consts["ident"], consts["hmask"], consts["half_neg"]
    with ExitStack() as st:
        def sb(name, shape, dt=F32):
            return st.enter_context(nc.sbuf_tensor("de_" + name, shape, dt))

        bank = st.enter_context(nc.psum_tensor("de_bank", [P, 8, 512], F32))
        s = Sems(nc, st, ["de_" + n for n in [
            "n_var", "n_rstd", "ct", "cts", "k", "ks", "v", "vb", "xt", "xts", "vx", "x1", "x1t", "x1s",
            "q", "qs", "x2", "x2t", "x2s", "f1", "f1s", "f2", "out", "loaded"]
            + ["s_" + n for n in ATTN_SEMS] + ["c_" + n for n in ATTN_SEMS]])
        p = Prefixed(s, "de_")
        wq, wk, wv, wo, ws = (sb(n, [P, D]) for n in ("wq", "wk", "wv", "wo", "ws"))
        w1, w2 = sb("w1", [P, FF]), sb("w2", [P, FC, D])
        vecs = sb("vecs", [P, 2 + FC])
        rows = sb("rows", [P, 10, D])
        SO, BV, CO, B2, G1 = 0, 1, 2, 3, 4
        a_tok, b_tok = (sb(n, [P, GB, D]) for n in ("a_tok", "b_tok"))
        x_toks, y_toks = ([sb(f"{n}{i}", [P, GB, D]) for i in range(2)] for n in ("x_tok", "y_tok"))
        c_toks = [sb(f"c_tok{i}", [NC, GB, D]) for i in range(2)]
        xT, qT = sb("xT", [P, GB, SEQ]), sb("qT", [P, GB, SEQ])
        cT, kT = sb("cT", [P, GB, NC]), sb("kT", [P, GB, NC])
        vself = sb("vself", [P, GB, H, VW])
        vx = sb("vx", [NC, GB, H, VW])
        hT = sb("hT", [P, FC, TOK])
        norm = Norm(sb, p, "n", half_neg)
        flow = Flow(nc, st, "de", s, lambda q, g: [(c_toks[q][:], ctx_rows(ctx_in, g)), (x_toks[q][:], tile_rows(x_in, g))],
                    x_out, y_toks)
        own = Attention(nc, sb, p, "s", bank, ident, hmask, SEQ, D ** -0.5, topk=True)
        cross = Attention(nc, sb, p, "c", bank, ident, hmask, NC, DK ** -0.5)

        s0 = Sems(nc, st, ["de0_w"])
        with nc.Block() as block:
            @block.sync
            def _(sp):
                loads = [(wq, "wq"), (wk, "wk"), (wv, "wv"), (wo, "wo"), (ws, "ws"), (w1, "w1"), (w2, "w2"), (vecs, "vecs")]
                for t, k in loads:
                    sp.dma_start(t[:], w[k]).then_inc(s0["de0_w"], 16)
                sp.dma_start(rows[:].rearrange("p r d -> p (r d)"), w["rows"].rearrange("r d -> (r d)").unsqueeze(0)
                             .to_broadcast([P, 10 * D])).then_inc(s0["de0_w"], 16)
                sp.wait_ge(s0["de0_w"], 16 * (len(loads) + 1))

            @block.vector
            def _(dve):
                nc.vector.memset(vx[:], 1.0)
                nc.vector.memset(vself[:], 1.0)
                for i in range(2):
                    nc.vector.memset(own.sp[i][:], LOW)
        s0.clear()

        def flat(t):
            return t[:].rearrange("p b d -> p (b d)")

        def wide_row(r):
            return rows[:, r].unsqueeze(1).to_broadcast([P, GB, D])

        flow.first()
        with nc.Fori(0, GROUPS // 2) as pairs:
            for q in range(2):
                x_tok, y_tok, c_tok = x_toks[q], y_toks[q], c_toks[q]
                norm.on_dve = norm.on_pool = 0
                with nc.Block() as block:
                    @block.sync
                    def _(sp):
                        flow.sync(sp, pairs, q, p["out"])

                    @block.gpsimd
                    def _(pool):
                        pool.wait_ge(p["xts"], 1)
                        own.pool(pool, lambda b: xT[:, b])
                        norm.pool(pool)
                        pool.wait_ge(p["ks"], 1)
                        cross.pool(pool, lambda b: kT[:, b])
                        for _ in range(3):
                            norm.pool(pool)

                    @block.tensor
                    def _(pe):
                        for b in range(GB):
                            m = nc.tensor.transpose(bank[:, 0, b * P:(b + 1) * P], x_tok[:, b], ident[:])
                        m.then_inc(p["xt"], 1)
                        for b in range(GB):
                            m = nc.tensor.transpose(bank[:, 1, b * NC:(b + 1) * NC], c_tok[:, b], ident[0:NC, 0:NC])
                        m.then_inc(p["ct"], 1)
                        pe.wait_ge(p["cts"], 1)
                        nc.tensor.matmul(bank[:, 2, 0:GB * NC], wk[:], flat(cT), start=True, stop=True).then_inc(p["k"], 1)
                        for b in range(GB):
                            m = nc.tensor.matmul(bank[0:NC, 3, b * D:(b + 1) * D], cT[:, b], wv[:], start=True, stop=True)
                        m.then_inc(p["v"], 1)
                        pe.wait_ge(p["xts"], 1)
                        pe.wait_ge(p["ks"], 1)
                        pe.wait_ge(p["vb"], 1)
                        pe.wait_ge(p["vx"], 1)
                        own.pe(pe, lambda b: xT[:, b], lambda b, h: vself[:, b, h], ws)
                        pe.wait_ge(p["x1"], 1)
                        for b in range(GB):
                            m = nc.tensor.transpose(bank[:, 0, b * P:(b + 1) * P], a_tok[:, b], ident[:])
                        m.then_inc(p["x1t"], 1)
                        pe.wait_ge(p["x1s"], 1)
                        nc.tensor.matmul(bank[:, 1], wq[:], flat(xT), start=True, stop=True).then_inc(p["q"], 1)
                        pe.wait_ge(p["qs"], 1)
                        cross.pe(pe, lambda b: qT[:, b], lambda b, h: vx[:, b, h], wo)
                        pe.wait_ge(p["x2"], 1)
                        for b in range(GB):
                            m = nc.tensor.transpose(bank[:, 0, b * P:(b + 1) * P], a_tok[:, b], ident[:])
                        m.then_inc(p["x2t"], 1)
                        pe.wait_ge(p["x2s"], 1)
                        for c in range(FC):
                            nc.tensor.matmul(bank[:, 1 + c], w1[:, c * P:(c + 1) * P], flat(xT), start=True, stop=True).then_inc(p["f1"], 1)
                        pe.wait_ge(p["f1s"], FC)
                        for b in range(GB):
                            for c in range(FC):
                                m = nc.tensor.matmul(bank[:, 5, b * D:(b + 1) * D], hT[:, c, b * SEQ:(b + 1) * SEQ], w2[:, c],
                                                     start=(c == 0), stop=(c == FC - 1))
                        m.then_inc(p["f2"], 1)

                    @block.scalar
                    def _(act):
                        act.wait_ge(p["xt"], 1)
                        nc.scalar.activation(flat(xT), bank[:, 0], ACT.Copy).then_inc(p["xts"], 1)
                        act.wait_ge(p["ct"], 1)
                        nc.scalar.activation(flat(cT), bank[:, 1, 0:GB * NC], ACT.Copy).then_inc(p["cts"], 1)
                        act.wait_ge(p["k"], 1)
                        nc.scalar.activation(flat(kT), bank[:, 2, 0:GB * NC], ACT.Identity, bias=vecs[:, 1:2]).then_inc(p["ks"], 1)
                        own.act(act)
                        act.wait_ge(p["x1t"], 1)
                        nc.scalar.activation(flat(xT), bank[:, 0], ACT.Copy).then_inc(p["x1s"], 1)
                        act.wait_ge(p["q"], 1)
                        nc.scalar.activation(flat(qT), bank[:, 1], ACT.Identity, bias=vecs[:, 0:1]).then_inc(p["qs"], 1)
                        cross.act(act)
                        act.wait_ge(p["x2t"], 1)
                        nc.scalar.activation(flat(xT), bank[:, 0], ACT.Copy).then_inc(p["x2s"], 1)
                        for c in range(FC):
                            act.wait_ge(p["f1"], c + 1)
                            nc.scalar.activation(hT[:, c], bank[:, 1 + c], ACT.Gelu, bias=vecs[:, 2 + c:3 + c]).then_inc(p["f1s"], 1)

                    @block.vector
                    def _(dve):
                        nc.vector.tensor_copy(vself[:, :, :, 0:DK], x_tok[:].rearrange("p b (h v) -> p b h v", v=DK)).then_inc(p["vx"], 1)
                        nc.vector.tensor_tensor(b_tok[:], x_tok[:], wide_row(SO), ALU.add)
                        dve.wait_ge(p["v"], 1)
                        nc.vector.tensor_tensor(vx[:, :, :, 0:DK], bank[0:NC, 3].rearrange("p (b h v) -> p b h v", b=GB, h=H),
                                                rows[0:NC, BV].rearrange("p (h v) -> p h v", h=H).unsqueeze(1).to_broadcast([NC, GB, H, DK]),
                                                ALU.add).then_inc(p["vb"], 1)
                        dve.drain()

                        def add(b, psum):
                            nc.vector.tensor_tensor(a_tok[:, b], b_tok[:, b], psum, ALU.add)

                        def affine_norm(k, src, dst):
                            norm.dve(dve, src, y_tok)
                            dve.drain()
                            nc.vector.tensor_tensor(y_tok[:], y_tok[:], wide_row(G1 + 2 * k), ALU.mult)
                            dve.drain()
                            return nc.vector.tensor_tensor(dst[:], y_tok[:], wide_row(G1 + 2 * k + 1), ALU.add)

                        own.dve(dve, add)
                        dve.drain()
                        affine_norm(0, a_tok, a_tok).then_inc(p["x1"], 1)
                        dve.wait_ge(p["x1"], 1)
                        nc.vector.tensor_tensor(b_tok[:], a_tok[:], wide_row(CO), ALU.add)
                        dve.wait_ge(p["x1t"], 1)
                        dve.drain()
                        cross.dve(dve, add)
                        dve.drain()
                        affine_norm(1, a_tok, a_tok).then_inc(p["x2"], 1)
                        dve.wait_ge(p["x2"], 1)
                        nc.vector.tensor_tensor(b_tok[:], a_tok[:], wide_row(B2), ALU.add)
                        dve.drain()
                        dve.wait_ge(p["f2"], 1)
                        nc.vector.tensor_tensor(a_tok[:], b_tok[:], bank[:, 5].rearrange("p (b d) -> p b d", b=GB), ALU.add)
                        dve.drain()
                        affine_norm(2, a_tok, b_tok)
                        dve.drain()
                        nc.vector.tensor_tensor(a_tok[:], b_tok[:], x_tok[:], ALU.add)
                        dve.drain()
                        norm.dve(dve, a_tok, y_tok).then_inc(p["out"], 1)
                s.clear()
        flow.last()


def decoder_host(i):
    A = lambda k: np.asarray(i["L1_xattn_" + k])
    iw, ib = A("cross_in_w"), A("cross_in_b")
    return {"wq": iw[:D].T, "wk": iw[D:2 * D].T, "wv": iw[2 * D:].T, "wo": A("cross_out_w").T, "ws": A("self_out_w").T,
            "w1": A("ffn_w1").T, "w2": A("ffn_w2").T.reshape(FC, P, D).transpose(1, 0, 2),
            "vecs": np.concatenate([ib[:D, None], ib[D:2 * D, None], A("ffn_b1").reshape(FC, P).T], axis=1),
            "rows": np.stack([A("self_out_b"), ib[2 * D:], A("cross_out_b"), A("ffn_b2"), A("ln1_g"), A("ln1_b"),
                              A("ln2_g"), A("ln2_b"), A("ln3_g"), A("ln3_b")])}


ROUND = 1.5 * 2.0 ** 23
QMAX, QMIN, EPS_Q = 127.0, -128.0, 1e-5


def bitlinear_stage(nc, w, consts, x_in, x_out):
    ident, half_neg = consts["ident"], consts["half_neg"]
    with ExitStack() as st:
        def sb(name, shape, dt=F32):
            return st.enter_context(nc.sbuf_tensor("bl_" + name, shape, dt))

        bank = st.enter_context(nc.psum_tensor("bl_bank", [P, 6, 512], F32))
        bankb = st.enter_context(nc.psum_tensor("bl_bankb", [P, 2, 1024], BF16))
        s = Sems(nc, st, ["bl_" + n for n in [
            "n_var", "n_rstd", "xq", "xt", "xts", "gu", "sg", "hq", "ht", "hts", "y", "sum", "out", "loaded"]])
        p = Prefixed(s, "bl_")
        wts = [sb(f"w{k}", [P, FF]) for k in range(3)]
        wa = sb("wa", [P, FF])
        wb = [sb(f"wb{k}", [P, FF], BF16) for k in range(3)]
        identb = sb("identb", [P, P], BF16)
        ones = sb("ones", [P, P])
        asum, mean, wsc = (sb(n, [P, 3]) for n in ("asum", "mean", "wsc"))
        x_toks, y_toks = ([sb(f"{n}{i}", [P, GB, D]) for i in range(2)] for n in ("x_tok", "y_tok"))
        flow = Flow(nc, st, "bl", s, lambda q, g: [(x_toks[q][:], tile_rows(x_in, g))], x_out, y_toks)
        t_tok = sb("t_tok", [P, GB, D])
        xq = sb("xq", [P, GB, D], BF16)
        xqT = sb("xqT", [P, GB, P], BF16)
        mx, sc, rg, ru = (sb(n, [P, GB]) for n in ("mx", "sc", "rg", "ru"))
        sg = [sb(f"sg{i}", [P, FF]) for i in range(2)]
        hh = [sb(f"hh{i}", [P, FF]) for i in range(2)]
        hm, hs, hr = (sb(n, [P, GB]) for n in ("hm", "hs", "hr"))
        hq = [sb(f"hq{i}", [P, FF], BF16) for i in range(2)]
        hqT = [sb(f"hqT{i}", [P, FF], BF16) for i in range(2)]
        norm = Norm(sb, p, "n", half_neg)

        s0 = Sems(nc, st, ["bl0_w", "bl0_s", "bl0_m"])
        with nc.Block() as block:
            @block.sync
            def _(sp):
                for t, k in zip(wts, ("gate", "up", "down")):
                    sp.dma_start(t[:], w[k]).then_inc(s0["bl0_w"], 16)

            @block.tensor
            def _(pe):
                pe.wait_ge(s0["bl0_s"], 1)
                nc.tensor.matmul(bank[:, 0, 0:3], ones[:], asum[:], start=True, stop=True).then_inc(s0["bl0_m"], 1)

            @block.vector
            def _(dve):
                nc.vector.memset(ones[:], 1.0)
                nc.vector.tensor_copy(identb[:], ident[:])
                dve.wait_ge(s0["bl0_w"], 48)
                for k in range(3):
                    nc.vector.tensor_reduce(asum[:, k:k + 1], wts[k][:], AX.X, ALU.add, apply_absolute_value=True)
                    dve.drain()
                nc.vector.tensor_copy(mean[:], asum[:]).then_inc(s0["bl0_s"], 1)
                dve.wait_ge(s0["bl0_m"], 1)
                nc.vector.tensor_scalar(mean[:], bank[:, 0, 0:3], 1.0 / (P * FF), EPS_Q, ALU.mult, ALU.max)
                dve.drain()
                nc.vector.reciprocal(wsc[:], mean[:])
                dve.drain()
                for k in range(3):
                    nc.vector.tensor_scalar(wa[:], wts[k][:], wsc[:, k:k + 1], ROUND, ALU.mult, ALU.add)
                    dve.drain()
                    nc.vector.tensor_scalar(wa[:], wa[:], -ROUND, 1.0, ALU.add, ALU.min)
                    dve.drain()
                    nc.vector.tensor_scalar(wb[k][:], wa[:], -1.0, None, ALU.max)
                    dve.drain()
        s0.clear()

        def flat(t):
            return t[:].rearrange("p b d -> p (b d)")

        flow.first()
        with nc.Fori(0, GROUPS // 2) as pairs:
            for q in range(2):
                x_tok, y_tok = x_toks[q], y_toks[q]
                norm.on_dve = norm.on_pool = 0
                with nc.Block() as block:
                    @block.sync
                    def _(sp):
                        flow.sync(sp, pairs, q, p["out"])

                    @block.gpsimd
                    def _(pool):
                        norm.pool(pool)

                    @block.tensor
                    def _(pe):
                        pe.wait_ge(p["xq"], 1)
                        for b in range(GB):
                            m = nc.tensor.transpose(bankb[:, 0, b * P:(b + 1) * P], xq[:, b], identb[:])
                        m.then_inc(p["xt"], 1)
                        pe.wait_ge(p["xts"], 1)

                        def gate_up(b):
                            if b >= 2:
                                pe.wait_ge(p["hq"], b - 1)
                            for k in range(2):
                                nc.tensor.matmul(bank[:, 2 * (b % 2) + k], xqT[:, b], wb[k][:], start=True, stop=True).then_inc(p["gu"], 1)

                        gate_up(0)
                        for b in range(GB):
                            if b + 1 < GB:
                                gate_up(b + 1)
                            pe.wait_ge(p["hq"], b + 1)
                            if b:
                                pe.wait_ge(p["hts"], b)
                            for c in range(FC):
                                m = nc.tensor.transpose(bankb[:, 1, c * P:(c + 1) * P], hq[b % 2][:, c * P:(c + 1) * P], identb[:])
                            m.then_inc(p["ht"], 1)
                            pe.wait_ge(p["hts"], b + 1)
                            if b:
                                pe.wait_ge(p["sum"], b)
                            for c in range(FC):
                                m = nc.tensor.matmul(bank[:, 4, 0:D], hqT[b % 2][:, c * P:(c + 1) * P], wb[2][:, c * D:(c + 1) * D],
                                                     start=(c == 0), stop=(c == FC - 1))
                            m.then_inc(p["y"], 1)

                    @block.scalar
                    def _(act):
                        act.wait_ge(p["xt"], 1)
                        nc.scalar.activation(flat(xqT), bankb[:, 0, 0:TOK], ACT.Copy).then_inc(p["xts"], 1)

                        def silu(b):
                            act.wait_ge(p["gu"], 2 * b + 1)
                            if b >= 2:
                                act.wait_ge(p["hq"], b - 1)
                            nc.scalar.activation(sg[b % 2][:], bank[:, 2 * (b % 2)], ACT.Silu, scale=rg[:, b:b + 1]).then_inc(p["sg"], 1)

                        silu(0)
                        for b in range(GB):
                            if b + 1 < GB:
                                silu(b + 1)
                            act.wait_ge(p["ht"], b + 1)
                            if b >= 2:
                                act.wait_ge(p["y"], b - 1)
                            nc.scalar.activation(hqT[b % 2][:], bankb[:, 1, 0:FF], ACT.Copy).then_inc(p["hts"], 1)

                    @block.vector
                    def _(dve):
                        def magnitude(dst, src):
                            nc.vector.tensor_reduce(dst, src, AX.X, ALU.max, apply_absolute_value=True)
                            dve.drain()
                            nc.vector.tensor_scalar(dst, dst, EPS_Q, 1.0 / QMAX, ALU.max, ALU.mult)
                            dve.drain()

                        magnitude(mx[:], x_tok[:])
                        nc.vector.reciprocal(sc[:], mx[:])
                        nc.vector.tensor_scalar(rg[:], mx[:], mean[:, 0:1], None, ALU.mult)
                        nc.vector.tensor_scalar(ru[:], mx[:], mean[:, 1:2], None, ALU.mult)
                        dve.drain()
                        for b in range(GB):
                            nc.vector.tensor_scalar(t_tok[:, b], x_tok[:, b], sc[:, b:b + 1], ROUND, ALU.mult, ALU.add)
                        dve.drain()
                        nc.vector.tensor_scalar(t_tok[:], t_tok[:], -ROUND, QMAX, ALU.add, ALU.min)
                        dve.drain()
                        nc.vector.tensor_scalar(xq[:], t_tok[:], QMIN, None, ALU.max).then_inc(p["xq"], 1)
                        for b in range(GB):
                            i = b % 2
                            dve.wait_ge(p["sg"], b + 1)
                            dve.wait_ge(p["gu"], 2 * b + 2)
                            nc.vector.scalar_tensor_tensor(out=hh[i][:], in0=bank[:, 2 * i + 1], scalar=ru[:, b:b + 1], in1=sg[i][:],
                                                           op0=ALU.mult, op1=ALU.mult)
                            dve.drain()
                            magnitude(hm[:, b:b + 1], hh[i][:])
                            nc.vector.reciprocal(hs[:, b:b + 1], hm[:, b:b + 1])
                            nc.vector.tensor_scalar(hr[:, b:b + 1], hm[:, b:b + 1], mean[:, 2:3], None, ALU.mult)
                            dve.drain()
                            nc.vector.tensor_scalar(hh[i][:], hh[i][:], hs[:, b:b + 1], ROUND, ALU.mult, ALU.add)
                            dve.drain()
                            nc.vector.tensor_scalar(hh[i][:], hh[i][:], -ROUND, QMAX, ALU.add, ALU.min)
                            dve.drain()
                            if b >= 2:
                                dve.wait_ge(p["ht"], b - 1)
                            nc.vector.tensor_scalar(hq[i][:], hh[i][:], QMIN, None, ALU.max).then_inc(p["hq"], 1)
                            if b:
                                dve.wait_ge(p["y"], b)
                                nc.vector.scalar_tensor_tensor(out=t_tok[:, b - 1], in0=bank[:, 4, 0:D], scalar=hr[:, b - 1:b],
                                                               in1=x_tok[:, b - 1], op0=ALU.mult, op1=ALU.add).then_inc(p["sum"], 1)
                        dve.wait_ge(p["y"], GB)
                        nc.vector.scalar_tensor_tensor(out=t_tok[:, GB - 1], in0=bank[:, 4, 0:D], scalar=hr[:, GB - 1:GB],
                                                       in1=x_tok[:, GB - 1], op0=ALU.mult, op1=ALU.add)
                        dve.drain()
                        norm.dve(dve, t_tok, y_tok).then_inc(p["out"], 1)
                s.clear()
        flow.last()


def bitlinear_host(i):
    A = lambda k: np.asarray(i["L1_ffn_w_" + k])
    return {"gate": A("gate").T, "up": A("up").T, "down": A("down").T.reshape(FC, P, D).transpose(1, 0, 2).reshape(P, FC * D)}


WEIGHTS = {"mb": mamba_host, "xa": xattn_host, "ex": experts_host, "tj": trajectory_host, "de": decoder_host, "bl": bitlinear_host}


def build(nc, a, out):
    of = lambda pre: {k[len(pre) + 1:]: v for k, v in a.items() if k.startswith(pre + "_")}
    with ExitStack() as st:
        consts = {"ident": st.enter_context(nc.sbuf_tensor("ident", [P, P], F32)),
                  "hmask": st.enter_context(nc.sbuf_tensor("hmask", [P, H], F32)),
                  "half_neg": st.enter_context(nc.sbuf_tensor("minus_half", [P, GB], F32))}
        padded = nc.dram_tensor("stream0", [(GROUPS + 3) * TOK, D], F32).ap()
        after_mamba = padded[TOK:TOK * (GROUPS + 1)]
        stream = [None] + [nc.dram_tensor(f"stream{k}", [(GROUPS + 1) * TOK, D], F32).ap() for k in range(1, 5)]
        x_ahead = nc.dram_tensor("x_ahead", [(GROUPS + 1) * TOK, D], F32).ap()
        ctx_ahead = nc.dram_tensor("ctx_ahead", [BATCH + GB, NC, D], F32).ap()
        mask_ahead = nc.dram_tensor("mask_ahead", [BATCH + GB, NC], I32).ap()
        loaded = st.enter_context(nc.semaphore("consts_loaded"))
        with nc.Block() as block:
            @block.sync
            def _(sp):
                sp.dma_start(consts["ident"][:], a["ident"]).then_inc(loaded, 16)
                sp.dma_start(consts["hmask"][:], a["hmask"]).then_inc(loaded, 16)
                sp.dma_start(after_mamba, a["x"]).then_inc(loaded, 16)
                sp.dma_start(padded[0:TOK], a["x"][0:TOK]).then_inc(loaded, 16)
                sp.dma_start(padded[TOK * (GROUPS + 1):], a["x"][0:2 * TOK]).then_inc(loaded, 16)
                for k in range(1, 5):
                    sp.dma_start(stream[k][TOK * GROUPS:], a["x"][0:TOK]).then_inc(loaded, 16)
                for whole, src, rows in ((x_ahead, a["x"], TOK), (ctx_ahead, a["ctx"], GB), (mask_ahead, a["mask"], GB)):
                    sp.dma_start(whole[0:src.shape[0]], src).then_inc(loaded, 16)
                    sp.dma_start(whole[src.shape[0]:], src[0:rows]).then_inc(loaded, 16)
                sp.wait_ge(loaded, 15 * 16)

            @block.vector
            def _(dve):
                nc.vector.memset(consts["half_neg"][:], -0.5)
        mamba_stage(nc, of("mb"), consts, padded)
        xattn_stage(nc, of("xa"), consts, x_ahead, padded[TOK:TOK * (GROUPS + 2)], ctx_ahead, mask_ahead, stream[1][0:TOK * GROUPS])
        experts_stage(nc, of("ex"), consts, stream[1], stream[2])
        trajectory_stage(nc, of("tj"), consts, stream[2], stream[3])
        decoder_stage(nc, of("de"), consts, stream[3], ctx_ahead, stream[4])
        bitlinear_stage(nc, of("bl"), consts, stream[4], out)


def kernel(**inputs):
    import concourse.bacc as bacc
    from concourse.bass_utils import run_bass_kernel_spmd

    host = {"x": np.asarray(inputs["x"]).reshape(BATCH * SEQ, D), "ctx": np.asarray(inputs["ctx_1024"]),
            "mask": np.asarray(inputs["mask_Bx1x1xS2_ik0"]).reshape(BATCH, NC),
            "ident": np.eye(P, dtype=np.float32), "hmask": np.repeat(np.eye(H, dtype=np.float32), DK, axis=0)}
    for pre, lay in WEIGHTS.items():
        host.update({f"{pre}_{k}": v for k, v in lay(inputs).items()})
    nc = bacc.Bacc("TRN2", target_bir_lowering=False, num_devices=1)
    arrays, a = {}, {}
    for k, v in host.items():
        arrays["in_" + k] = np.ascontiguousarray(v)
        a[k] = nc.dram_tensor("in_" + k, v.shape, mybir.dt.from_np(v.dtype), kind="ExternalInput").ap()
    out = nc.dram_tensor("out", [BATCH * SEQ, D], F32, kind="ExternalOutput").ap()
    build(nc, a, out)
    r = run_bass_kernel_spmd(nc, [arrays], core_ids=[0])
    return r.results[0]["out"].reshape(BATCH, SEQ, D)
```
